# Optimizing a Trainium2 kernel written in Bass

```python
import numpy as np
import jax
import jax.numpy as jnp

def _softmax(x, axis=-1):
    return jax.nn.softmax(x, axis=axis)

def _gelu(x):
    return jax.nn.gelu(x, approximate=True)

def _silu(x):
    return jax.nn.silu(x)

def _sigmoid(x):
    return jax.nn.sigmoid(x)

def _layernorm(x, axis=-1, eps=1e-05):
    m = jnp.mean(x, axis=axis, keepdims=True)
    v = jnp.var(x, axis=axis, keepdims=True)
    return (x - m) / jnp.sqrt(v + eps)

def _scatter_add(tgt, idx, src, axis=0):
    return tgt.at[idx].add(src)

def _segment_sum(src, seg, n):
    return jax.ops.segment_sum(src, seg, n)
kernel_name = 'mk_gnn_preln_d2_gnn_r64_5ad940'

def setup_inputs(seed: int=0):
    np.random.seed(seed)
    _w = jnp.asarray

    def _rec_inputs():
        import jax
        import jax.numpy as jnp
        _gk = jax.random.key(seed)
        x = -0.000202 + 1 * jax.random.normal(jax.random.fold_in(_gk, 1), (100000, 128), jnp.float32)
        src = jax.random.randint(jax.random.fold_in(_gk, 2), (25000,), 0, 100000, jnp.int32)
        dst = jax.random.randint(jax.random.fold_in(_gk, 3), (25000,), 0, 100000, jnp.int32)
        _o = jnp.argsort(dst, stable=True)
        src = src[_o]
        dst = dst[_o]
        edge_attr_64 = -9.77346e-05 + 0.999888 * jax.random.normal(jax.random.fold_in(_gk, 11), (25000, 64), jnp.float32)
        edge_weight1 = jax.random.uniform(jax.random.fold_in(_gk, 13), (25000, 1), jnp.float32, 0.0, 0.999998)
        node_vec1 = jax.random.uniform(jax.random.fold_in(_gk, 14), (100000, 1), jnp.float32, 0.0, 0.999884)
        return (x, src, dst, edge_attr_64, edge_weight1, node_vec1)
    x, src, dst, edge_attr_64, edge_weight1, node_vec1 = _rec_inputs()

    def _L0_gnn_setup():
        import jax, jax.numpy as jnp
        import numpy as np
        N_NODES = 50000
        N_EDGES = 500000
        D = 128
        D_OUT = 128
        L_TRANS = 2
        L_GNN = 3
        EPS_LN = 1e-05
        EPS_BN = 1e-05

        def _ln(x, g, b):
            mu = jnp.mean(x, axis=-1, keepdims=True)
            var = jnp.mean(jnp.square(x - mu), axis=-1, keepdims=True)
            return (x - mu) * jax.lax.rsqrt(var + EPS_LN) * g + b

        def _bn_eval(x, g, b):
            return x * (g / np.sqrt(1.0 + EPS_BN)) + b

        def _attn(x, wq, wk, wv):
            n = x.shape[0]
            q = x @ wq
            k = x @ wk
            v = x @ wv
            eps = 1e-06
            q = jnp.where(q == 0, eps, q)
            k = jnp.where(k == 0, eps, k)
            q = q / jnp.linalg.norm(q, axis=-1, keepdims=True)
            k = k / jnp.linalg.norm(k, axis=-1, keepdims=True)
            kv = jnp.einsum('lm,ld->md', k, v)
            num = q @ kv + n * v
            denom = q @ jnp.sum(k, axis=0) + n
            return num / denom[:, None]

        def _gcn(x, edge_index, w, b, n):
            sl = jnp.arange(n, dtype=edge_index.dtype)
            row = jnp.concatenate([edge_index[0], sl])
            col = jnp.concatenate([edge_index[1], sl])
            deg = jax.ops.segment_sum(jnp.ones_like(col, dtype=x.dtype), col, num_segments=n)
            dinv = jnp.where(deg > 0, jax.lax.rsqrt(deg), 0.0)
            norm = dinv[row] * dinv[col]
            xw = x @ w
            out = jax.ops.segment_sum(norm[:, None] * xw[row], col, num_segments=n)
            return out + b
        key = jax.random.key(seed)
        ks = jax.random.split(key, 8)
        s = 1.0 / np.sqrt(D)
        return {'x': jax.random.normal(ks[0], (N_NODES, D), jnp.float32), 'edge_index': jax.random.randint(ks[1], (2, N_EDGES), 0, N_NODES, dtype=jnp.int32), 't_fc_w': jax.random.normal(ks[2], (D, D), jnp.float32) * s, 't_fc_b': jnp.zeros((D,), jnp.float32), 't_ln_g': jnp.ones((L_TRANS + 1, D), jnp.float32), 't_ln_b': jnp.zeros((L_TRANS + 1, D), jnp.float32), 'qkv_w': jax.random.normal(ks[3], (L_TRANS, 3, D, D), jnp.float32) * s, 'g_fc_w': jax.random.normal(ks[4], (D, D), jnp.float32) * s, 'g_fc_b': jnp.zeros((D,), jnp.float32), 'bn_g': jnp.ones((L_GNN + 1, D), jnp.float32), 'bn_b': jnp.zeros((L_GNN + 1, D), jnp.float32), 'conv_w': jax.random.normal(ks[5], (L_GNN, D, D), jnp.float32) * s, 'conv_b': jnp.zeros((L_GNN, D), jnp.float32), 'fc_w': jax.random.normal(ks[6], (D, D_OUT), jnp.float32) * s, 'fc_b': jnp.zeros((D_OUT,), jnp.float32)}
    _L0_gnn_all = _L0_gnn_setup()
    _L0_gnn_in = {k: v for k, v in _L0_gnn_all.items() if k in ('t_fc_w', 't_fc_b', 't_ln_g', 't_ln_b', 'qkv_w', 'g_fc_w', 'g_fc_b', 'bn_g', 'bn_b', 'conv_w', 'conv_b', 'fc_w', 'fc_b')}
    del _L0_gnn_all

    def _L1_gnn_setup():
        import jax, jax.numpy as jnp
        import numpy as np
        N_NODES, N_EDGES = (50000, 12500)
        NODE_DIM, EDGE_DIM, HIDDEN, HEADS = (128, 64, 128, 8)
        HEAD_DIM = HIDDEN // HEADS
        key = jax.random.key(seed)
        ks = jax.random.split(key, 24)

        def lin(k, fan_in, fan_out):
            lim = 1.0 / np.sqrt(fan_in)
            kw, kb = jax.random.split(k)
            W = jax.random.uniform(kw, (fan_in, fan_out), jnp.float32, -lim, lim)
            b = jax.random.uniform(kb, (fan_out,), jnp.float32, -lim, lim)
            return (W, b)
        inp = {}
        inp['nodes'] = jax.random.normal(ks[0], (N_NODES, NODE_DIM), jnp.float32)
        inp['edges'] = jax.random.normal(ks[1], (N_EDGES, EDGE_DIM), jnp.float32)
        inp['edge_index'] = jax.random.randint(ks[2], (2, N_EDGES), 0, N_NODES, jnp.int32)
        inp['conservation_scores'] = jax.random.uniform(ks[3], (N_NODES, 1), jnp.float32)
        inp['distances'] = jax.random.uniform(ks[4], (N_EDGES, 1), jnp.float32)
        inp['Wq'], inp['bq'] = lin(ks[5], NODE_DIM, HIDDEN)
        inp['Wk'], inp['bk'] = lin(ks[6], NODE_DIM, HIDDEN)
        inp['Wv'], inp['bv'] = lin(ks[7], NODE_DIM, HIDDEN)
        inp['We'], inp['be'] = lin(ks[8], EDGE_DIM, HEADS)
        inp['Wc1'], inp['bc1'] = lin(ks[9], 1, 32)
        inp['Wc2'], inp['bc2'] = lin(ks[10], 32, HEADS)
        inp['Wd1'], inp['bd1'] = lin(ks[11], 1, 16)
        inp['Wd2'], inp['bd2'] = lin(ks[12], 16, HEADS)
        inp['Wo'], inp['bo'] = lin(ks[13], HIDDEN, NODE_DIM)
        inp['gamma'] = jnp.ones((NODE_DIM,), jnp.float32)
        inp['beta'] = jnp.zeros((NODE_DIM,), jnp.float32)
        return inp
    _L1_gnn_all = _L1_gnn_setup()
    _L1_gnn_in = {k: v for k, v in _L1_gnn_all.items() if k in ('Wq', 'bq', 'Wk', 'bk', 'Wv', 'bv', 'We', 'be', 'Wc1', 'bc1', 'Wc2', 'bc2', 'Wd1', 'bd1', 'Wd2', 'bd2', 'Wo', 'bo', 'gamma', 'beta')}
    del _L1_gnn_all
    return {'x': x, 'src': src, 'dst': dst, 'edge_attr_64': edge_attr_64, 'edge_weight1': edge_weight1, 'node_vec1': node_vec1, 'L0_gnn_t_fc_w': _L0_gnn_in['t_fc_w'], 'L0_gnn_t_fc_b': _L0_gnn_in['t_fc_b'], 'L0_gnn_t_ln_g': _L0_gnn_in['t_ln_g'], 'L0_gnn_t_ln_b': _L0_gnn_in['t_ln_b'], 'L0_gnn_qkv_w': _L0_gnn_in['qkv_w'], 'L0_gnn_g_fc_w': _L0_gnn_in['g_fc_w'], 'L0_gnn_g_fc_b': _L0_gnn_in['g_fc_b'], 'L0_gnn_bn_g': _L0_gnn_in['bn_g'], 'L0_gnn_bn_b': _L0_gnn_in['bn_b'], 'L0_gnn_conv_w': _L0_gnn_in['conv_w'], 'L0_gnn_conv_b': _L0_gnn_in['conv_b'], 'L0_gnn_fc_w': _L0_gnn_in['fc_w'], 'L0_gnn_fc_b': _L0_gnn_in['fc_b'], 'L1_gnn_Wq': _L1_gnn_in['Wq'], 'L1_gnn_bq': _L1_gnn_in['bq'], 'L1_gnn_Wk': _L1_gnn_in['Wk'], 'L1_gnn_bk': _L1_gnn_in['bk'], 'L1_gnn_Wv': _L1_gnn_in['Wv'], 'L1_gnn_bv': _L1_gnn_in['bv'], 'L1_gnn_We': _L1_gnn_in['We'], 'L1_gnn_be': _L1_gnn_in['be'], 'L1_gnn_Wc1': _L1_gnn_in['Wc1'], 'L1_gnn_bc1': _L1_gnn_in['bc1'], 'L1_gnn_Wc2': _L1_gnn_in['Wc2'], 'L1_gnn_bc2': _L1_gnn_in['bc2'], 'L1_gnn_Wd1': _L1_gnn_in['Wd1'], 'L1_gnn_bd1': _L1_gnn_in['bd1'], 'L1_gnn_Wd2': _L1_gnn_in['Wd2'], 'L1_gnn_bd2': _L1_gnn_in['bd2'], 'L1_gnn_Wo': _L1_gnn_in['Wo'], 'L1_gnn_bo': _L1_gnn_in['bo'], 'L1_gnn_gamma': _L1_gnn_in['gamma'], 'L1_gnn_beta': _L1_gnn_in['beta']}

def reference(x, src, dst, edge_attr_64, edge_weight1, node_vec1, L0_gnn_t_fc_w, L0_gnn_t_fc_b, L0_gnn_t_ln_g, L0_gnn_t_ln_b, L0_gnn_qkv_w, L0_gnn_g_fc_w, L0_gnn_g_fc_b, L0_gnn_bn_g, L0_gnn_bn_b, L0_gnn_conv_w, L0_gnn_conv_b, L0_gnn_fc_w, L0_gnn_fc_b, L1_gnn_Wq, L1_gnn_bq, L1_gnn_Wk, L1_gnn_bk, L1_gnn_Wv, L1_gnn_bv, L1_gnn_We, L1_gnn_be, L1_gnn_Wc1, L1_gnn_bc1, L1_gnn_Wc2, L1_gnn_bc2, L1_gnn_Wd1, L1_gnn_bd1, L1_gnn_Wd2, L1_gnn_bd2, L1_gnn_Wo, L1_gnn_bo, L1_gnn_gamma, L1_gnn_beta):
    import jax
    import jax.numpy as jnp

    def _L0_gnn_ref(x, edge_index, t_fc_w, t_fc_b, t_ln_g, t_ln_b, qkv_w, g_fc_w, g_fc_b, bn_g, bn_b, conv_w, conv_b, fc_w, fc_b):
        import jax, jax.numpy as jnp
        import numpy as np
        N_NODES = 50000
        N_EDGES = 500000
        D = 128
        D_OUT = 128
        L_TRANS = 2
        L_GNN = 3
        EPS_LN = 1e-05
        EPS_BN = 1e-05

        def _ln(x, g, b):
            mu = jnp.mean(x, axis=-1, keepdims=True)
            var = jnp.mean(jnp.square(x - mu), axis=-1, keepdims=True)
            return (x - mu) * jax.lax.rsqrt(var + EPS_LN) * g + b

        def _bn_eval(x, g, b):
            return x * (g / np.sqrt(1.0 + EPS_BN)) + b

        def _attn(x, wq, wk, wv):
            n = x.shape[0]
            q = x @ wq
            k = x @ wk
            v = x @ wv
            eps = 1e-06
            q = jnp.where(q == 0, eps, q)
            k = jnp.where(k == 0, eps, k)
            q = q / jnp.linalg.norm(q, axis=-1, keepdims=True)
            k = k / jnp.linalg.norm(k, axis=-1, keepdims=True)
            kv = jnp.einsum('lm,ld->md', k, v)
            num = q @ kv + n * v
            denom = q @ jnp.sum(k, axis=0) + n
            return num / denom[:, None]

        def _gcn(x, edge_index, w, b, n):
            sl = jnp.arange(n, dtype=edge_index.dtype)
            row = jnp.concatenate([edge_index[0], sl])
            col = jnp.concatenate([edge_index[1], sl])
            deg = jax.ops.segment_sum(jnp.ones_like(col, dtype=x.dtype), col, num_segments=n)
            dinv = jnp.where(deg > 0, jax.lax.rsqrt(deg), 0.0)
            norm = dinv[row] * dinv[col]
            xw = x @ w
            out = jax.ops.segment_sum(norm[:, None] * xw[row], col, num_segments=n)
            return out + b
        n = x.shape[0]
        h = jax.nn.relu(_ln(x @ t_fc_w + t_fc_b, t_ln_g[0], t_ln_b[0]))
        layers = [h]
        cur = h
        for i in range(L_TRANS):
            a = _attn(cur, qkv_w[i, 0], qkv_w[i, 1], qkv_w[i, 2])
            cur = jax.nn.relu(_ln((a + layers[i]) * 0.5, t_ln_g[i + 1], t_ln_b[i + 1]))
            layers.append(cur)
        x1 = cur
        g = jax.nn.relu(_bn_eval(x @ g_fc_w + g_fc_b, bn_g[0], bn_b[0]))
        last = g
        for i in range(L_GNN):
            g = _gcn(g, edge_index, conv_w[i], conv_b[i], n)
            g = jax.nn.relu(_bn_eval(g, bn_g[i + 1], bn_b[i + 1])) + last
        x2 = g
        return (0.5 * x2 + 0.5 * x1) @ fc_w + fc_b

    def _L1_gnn_ref(nodes, edges, edge_index, conservation_scores, distances, Wq, bq, Wk, bk, Wv, bv, We, be, Wc1, bc1, Wc2, bc2, Wd1, bd1, Wd2, bd2, Wo, bo, gamma, beta):
        import jax, jax.numpy as jnp
        import numpy as np
        N_NODES, N_EDGES = (50000, 12500)
        NODE_DIM, EDGE_DIM, HIDDEN, HEADS = (128, 64, 128, 8)
        HEAD_DIM = HIDDEN // HEADS
        N = nodes.shape[0]
        src, tgt = (edge_index[0], edge_index[1])
        q = (nodes @ Wq + bq).reshape(N, HEADS, HEAD_DIM)
        k = (nodes @ Wk + bk).reshape(N, HEADS, HEAD_DIM)
        v = (nodes @ Wv + bv).reshape(N, HEADS, HEAD_DIM)
        scores = jnp.einsum('ehd,ehd->eh', q[src], k[tgt]) / np.sqrt(HEAD_DIM)
        scores = scores + edges @ We + be
        cons = jax.nn.sigmoid(jax.nn.relu(conservation_scores @ Wc1 + bc1) @ Wc2 + bc2)
        scores = scores * cons[tgt]
        scores = scores + jax.nn.relu(distances @ Wd1 + bd1) @ Wd2 + bd2
        seg_max = jax.ops.segment_max(scores, tgt, num_segments=N)
        w = jnp.exp(scores - seg_max[tgt])
        seg_sum = jax.ops.segment_sum(w, tgt, num_segments=N)
        weights = w / seg_sum[tgt]
        attended = weights[..., None] * v[tgt]
        agg = jax.ops.segment_sum(attended, tgt, num_segments=N).reshape(N, HIDDEN)
        out = agg @ Wo + bo
        x = nodes + out
        mu = jnp.mean(x, axis=-1, keepdims=True)
        var = jnp.var(x, axis=-1, keepdims=True)
        return (x - mu) / jnp.sqrt(var + 1e-05) * gamma + beta
    edge_index = jnp.stack([src, dst])
    h = jnp.maximum(_layernorm(x, axis=-1), 0.0)
    x = x + _L0_gnn_ref(h, edge_index, L0_gnn_t_fc_w, L0_gnn_t_fc_b, L0_gnn_t_ln_g, L0_gnn_t_ln_b, L0_gnn_qkv_w, L0_gnn_g_fc_w, L0_gnn_g_fc_b, L0_gnn_bn_g, L0_gnn_bn_b, L0_gnn_conv_w, L0_gnn_conv_b, L0_gnn_fc_w, L0_gnn_fc_b)
    h = jnp.maximum(_layernorm(x, axis=-1), 0.0)
    x = x + _L1_gnn_ref(h, edge_attr_64, edge_index, node_vec1, edge_weight1, L1_gnn_Wq, L1_gnn_bq, L1_gnn_Wk, L1_gnn_bk, L1_gnn_Wv, L1_gnn_bv, L1_gnn_We, L1_gnn_be, L1_gnn_Wc1, L1_gnn_bc1, L1_gnn_Wc2, L1_gnn_bc2, L1_gnn_Wd1, L1_gnn_bd1, L1_gnn_Wd2, L1_gnn_bd2, L1_gnn_Wo, L1_gnn_bo, L1_gnn_gamma, L1_gnn_beta)
    return x

_drawn_inputs = setup_inputs


def setup_inputs(seed=0):
    import zlib

    import numpy as np

    out = dict(_drawn_inputs(seed))
    spreads = {'L0_gnn_t_fc_b': (0.0, 0.1),
     'L0_gnn_t_ln_g': (1.0, 0.2),
     'L0_gnn_t_ln_b': (0.0, 0.1),
     'L0_gnn_g_fc_b': (0.0, 0.1),
     'L0_gnn_bn_g': (1.0, 0.2),
     'L0_gnn_bn_b': (0.0, 0.1),
     'L0_gnn_conv_b': (0.0, 0.1),
     'L0_gnn_fc_b': (0.0, 0.1),
     'L1_gnn_gamma': (1.0, 0.2),
     'L1_gnn_beta': (0.0, 0.1)}
    factors = {'edge_attr_64': 64.0,
     'edge_weight1': 64.0,
     'node_vec1': 64.0,
     'L1_gnn_Wq': 64.0,
     'L1_gnn_bq': 64.0,
     'L1_gnn_Wk': 64.0,
     'L1_gnn_bk': 64.0,
     'L1_gnn_bv': 5.596,
     'L1_gnn_We': 64.0,
     'L1_gnn_be': 64.0,
     'L1_gnn_Wc1': 64.0,
     'L1_gnn_bc1': 64.0,
     'L1_gnn_Wc2': 64.0,
     'L1_gnn_bc2': 64.0,
     'L1_gnn_Wd1': 64.0,
     'L1_gnn_bd1': 64.0,
     'L1_gnn_Wd2': 64.0,
     'L1_gnn_bd2': 64.0}
    for name, (base, spread) in spreads.items():
        noise = np.random.default_rng([zlib.crc32(name.encode()), seed]).standard_normal(out[name].shape)
        drawn = base * np.exp(spread * noise) if base else spread * noise
        out[name] = jnp.asarray(drawn.astype(out[name].dtype))
    for name, factor in factors.items():
        out[name] = (out[name] * factor).astype(out[name].dtype)
    return out
```

```python
from contextlib import ExitStack

import concourse.bass as bass
from concourse import mybir

ALU = mybir.AluOpType
ACT = mybir.ActivationFunctionType
F32 = mybir.dt.float32
I32 = mybir.dt.int32
AX_X = mybir.AxisListType.X

P = 128
K = 4
ROWS = P * K
D = 128
HEADS = 8
HEAD_DIM = D // HEADS
LAYERS = 3
EPS_LN = 1e-5
EPS_BN = 1e-5
EPS_Q = 1e-6
EXP_MAX = 87.0
LOWEST = -1e30
REC = 16
SRC, DST, REP, ADD_AT, SOFT_AT, WRITE_AT = range(0, 6 * K, K)


class Turn:

    def __init__(self, reg, offset):
        self.reg, self.offset = reg, offset
        self.slot = offset % 2

    def __sub__(self, n):
        return Turn(self.reg, self.offset - n)

    @property
    def known(self):
        return self.reg is None

    def follows(self, n):
        return not self.known or self.number >= n

    @property
    def number(self):
        return self.offset if self.reg is None else 2 * self.reg + self.offset

    @property
    def half(self):
        return self.offset // 2 if self.reg is None else self.reg + self.offset // 2


class Steps:

    def __init__(self, sem, *names):
        self.sem, self.names = sem, names

    def step(self, name):
        assert name in self.names
        return self.sem

    def at(self, name, turn):
        return turn.number * len(self.names) + self.names.index(name) + 1


class Landed:

    def __init__(self, sems, each=1):
        self.sems, self.each = sems, each

    def full(self, turn):
        return 16 * self.each * turn.half + 16 * self.each


def run(engine, groups, lag, body):
    head = (2 + lag + 1) // 2 * 2
    for t in range(min(head, groups + lag)):
        body(Turn(None, t))
    if groups > head:
        with engine.Fori(head // 2, groups // 2) as i:
            for odd in range(2):
                body(Turn(i, odd))
    for t in range(max(groups, head), groups + lag):
        body(Turn(None, t))


def inside(turn, groups):
    return not turn.known or 0 <= turn.number < groups


def graph_kernel(nc, a, out):
    n_nodes = a["n_nodes"]
    NG = a["x"].shape[0] // ROWS
    EG = a["src"].shape[0] // ROWS
    NP, EP = NG * ROWS, EG * ROWS
    SPARE = ROWS
    last_nodes = n_nodes - (NG - 1) * ROWS
    assert NG % 2 == 0 and EG % 2 == 0 and 0 < last_nodes <= ROWS and last_nodes % K == 0
    last_parts = last_nodes // K

    def dram(name, shape, dtype=F32):
        return nc.dram_tensor(name, shape, dtype, kind="Internal").ap()

    node_rec = dram("node_rec", [NP + SPARE, REC])
    g_rows = [dram(f"g{i}_rows", [NP + SPARE, D]) for i in range(LAYERS + 1)]
    t0_T = dram("t0_T", [NG * P, ROWS])
    t1_T = dram("t1_T", [NG * P, ROWS])
    xl_rows = dram("xl_rows", [NP, D])
    first_e = dram("first_e", [EG * P, K])
    index_rec = dram("index_rec", [EG * P, 6 * K], I32)
    scale_rec = dram("scale_rec", [EG * P, 2 * K])
    nodevec_e = dram("nodevec_e", [EP, 1])
    g0_e = dram("g0_e", [EP, D])
    acc = [dram(f"acc{i}", [EP + SPARE // 2, 2 * D]) for i in range(LAYERS)]
    soft = dram("soft", [EP * K + SPARE, 2 * HEADS])
    v_e = dram("v_e", [EP, D])
    h_e = dram("h_e", [EP, D])
    xl_e = dram("xl_e", [EP, D])

    def group(table, turn):
        return table[bass.ds(turn.number * ROWS, ROWS), :].rearrange("(p k) d -> p (k d)", p=P)

    def block_of(table, turn, rows=P):
        return table[bass.ds(turn.number * rows, rows), :]

    def indirect(pool, go, **args):
        pool.sem_inc(go)
        return pool.indirect_dma_start(**args)

    def rows_at(column):
        return bass.IndirectOffsetOnAxis(ap=column, axis=0)

    with ExitStack() as whole:
        def keep(name, shape, dtype=F32):
            return whole.enter_context(nc.sbuf_tensor(name, shape, dtype))

        names = ("t_w", "wq0", "wk0", "wv0", "wq1", "wk1", "wv1", "g_w", "c0", "c1", "c2", "fc_w",
                 "l1_q", "l1_k", "l1_v", "l1_o")
        weights = keep("weights", [P, len(names), D])
        W = {n: weights[:, i, :] for i, n in enumerate(names)}
        rows_names = ("t_b", "fc_b", "bq", "bk", "bv", "bo", "gamma", "beta")
        wide = keep("wide", [P, len(rows_names), K, D])
        R = {n: wide[:, i, :, :] for i, n in enumerate(rows_names)}
        col_names = ("g_b", "cb0", "cb1", "cb2", "bg0", "bg1", "bg2", "bg3", "bb0", "bb1", "bb2", "bb3",
                     "lg0", "lg1", "lg2", "lb0", "lb1", "lb2")
        cols = keep("cols", [P, len(col_names)])
        C = {n: cols[:, i:i + 1] for i, n in enumerate(col_names)}
        bn_bias = keep("bn_bias", [P, LAYERS + 1])
        bn_scale = keep("bn_scale", [P, LAYERS + 1])
        ident = keep("ident", [P, P])
        before = keep("before", [P, K, P])
        spare_node = keep("spare_node", [P, K])
        lane = keep("lane", [P, 4 * K])
        ones = keep("ones", [P, P])
        c1w = keep("c1w", [2, 33])
        c2w = keep("c2w", [33, HEADS])
        d1w = keep("d1w", [2, 17])
        d2w = keep("d2w", [17, HEADS])
        ew = keep("ew", [65, HEADS])
        zeros = keep("zeros", [P, K, D])
        eps = keep("eps", [P, 2])
        kv = [keep(f"kv{i}", [P, D + 1]) for i in range(2)]
        passed = whole.enter_context(nc.semaphore("passed"))

        with ExitStack() as ctx:
            def sem(name):
                return ctx.enter_context(nc.semaphore(name))

            fill = ctx.enter_context(nc.sbuf_tensor("fill", [P, (NP + SPARE) // P, REC], F32))
            nodevec = ctx.enter_context(nc.sbuf_tensor("nodevec", [P, (NP + SPARE) // P], F32))
            nosoft = ctx.enter_context(nc.sbuf_tensor("nosoft", [P, (EP * K + SPARE) // P, 2, HEADS], F32))
            landed, filled, stored, scaled = sem("landed"), sem("filled"), sem("stored"), sem("scaled")
            cleared = sem("cleared")
            n_loads = len(names) + K * len(rows_names) + 10 + K
            with nc.Block() as block:
                @block.sync
                def _(sp):
                    n = 0
                    for name in names:
                        sp.dma_start(W[name], a[name]).then_inc(landed, 16)
                        n += 1
                    for name in rows_names:
                        for k in range(K):
                            sp.dma_start(R[name][:, k, :], a[name].partition_broadcast(P)).then_inc(landed, 16)
                            n += 1
                    sp.dma_start(cols[:, :], a["cols"]).then_inc(landed, 16)
                    for tile, name in ((ident, "ident"), (spare_node, "spare_node"), (lane, "lane"),
                                       (c1w, "c1w"), (c2w, "c2w"), (d1w, "d1w"), (d2w, "d2w"), (ew, "ew")):
                        sp.dma_start(tile[:, :], a[name]).then_inc(landed, 16)
                    for k in range(K):
                        sp.dma_start(before[:, k, :], a["before"]).then_inc(landed, 16)
                    sp.dma_start(nodevec[:, :], a["node_vec"].rearrange("(p n) o -> p (n o)", p=P)).then_inc(landed, 16)
                    n += 10 + K
                    assert n == n_loads
                    sp.wait_ge(filled, 1)
                    sp.dma_start(node_rec.rearrange("(p n) r -> p (n r)", p=P),
                                 fill[:, :, :].rearrange("p n r -> p (n r)")).then_inc(stored, 16)
                    sp.wait_ge(cleared, 7)
                    sp.dma_start(soft.rearrange("(p n) r -> p (n r)", p=P),
                                 nosoft[:, :, :, :].rearrange("p n t h -> p (n t h)")).then_inc(stored, 16)
                    for table in acc:
                        sp.dma_start(table[EP:EP + SPARE // 2, :].rearrange("(p n) d -> p (n d)", p=P),
                                     zeros[:, :, :].rearrange("p k d -> p (k d)")).then_inc(stored, 16)
                    sp.wait_ge(stored, 16 * (2 + LAYERS))


                @block.vector
                def _(dve):
                    dve.memset(fill[:, :, :], 0.0).then_inc(cleared, 1)
                    dve.memset(nosoft[:, :, 0, :], LOWEST).then_inc(cleared, 1)
                    dve.memset(nosoft[:, :, 1, :], 0.0).then_inc(cleared, 1)
                    dve.memset(zeros[:, :, :], 0.0).then_inc(cleared, 1)
                    dve.memset(ones[:, :], 1.0).then_inc(cleared, 1)
                    dve.memset(eps[:, 0:1], EPS_LN).then_inc(cleared, 1)
                    dve.memset(eps[:, 1:2], 4 * EPS_LN).then_inc(cleared, 1)
                    dve.wait_ge(cleared, 7)
                    dve.wait_ge(landed, 16 * n_loads)
                    dve.tensor_copy(fill[:, :, 8], nodevec[:, :]).then_inc(filled, 1)
                    for w in ("wq0", "wk0", "wq1", "wk1"):
                        dve.tensor_scalar(W[w], W[w], 1.0 / EPS_Q, None, ALU.mult)
                    dve.tensor_scalar(W["fc_w"], W["fc_w"], 0.5, None, ALU.mult)
                    at = col_names.index("bg0")
                    dve.tensor_scalar(bn_scale[:, :], cols[:, at:at + 4], (1.0 + EPS_BN) ** -0.5, None,
                                      ALU.mult).then_inc(scaled, 1)
                    dve.wait_ge(scaled, 1)
                    dve.tensor_tensor(bn_bias[:, :], cols[:, 0:4], bn_scale[:, :], ALU.mult).then_inc(scaled, 1)
                    dve.wait_ge(scaled, 2)
                    at = col_names.index("bb0")
                    dve.tensor_tensor(bn_bias[:, :], bn_bias[:, :], cols[:, at:at + 4], ALU.add)


        class Phase:

            def __init__(self, name):
                self.name, self.ctx, self.sems = name, ExitStack(), []
                self.ctx.callback(self.clear)

            def clear(self):
                nc.clear_and_free_semaphores(self.sems)
                nc.all_engine_barrier()

            def sb(self, name, shape, dtype=F32):
                return [self.ctx.enter_context(nc.sbuf_tensor(f"{self.name}_{name}{i}", shape, dtype))
                        for i in range(2)]

            def one(self, name, shape, dtype=F32):
                return self.ctx.enter_context(nc.sbuf_tensor(f"{self.name}_{name}", shape, dtype))

            def bank(self, name, banks=1):
                return self.ctx.enter_context(nc.psum_tensor(f"{self.name}_{name}", [P, 512 * banks], F32))

            def sem(self, name):
                self.sems.append(nc.alloc_semaphore(name=f"{self.name}_{name}"))
                return self.sems[-1]

            def steps(self, name, *steps):
                return Steps(self.sem(name), *steps)

            def dmas(self, name, each=1):
                return Landed([self.sem(f"{name}{i}") for i in range(2)], each)

        def by_k(tile):
            return tile.rearrange("p (k d) -> p k d", k=K)

        def flat(tile):
            return tile.rearrange("p k d -> p (k d)")

        def over(column, n):
            return column.unsqueeze(2).to_broadcast([P, column.shape[1], n])

        def moments_of(dve, steps, turn, src, norm, names):
            for k in range(K):
                ins = dve.bn_stats(norm["stats"][:, k, :], src[:, k, :])
            ins.then_inc(steps.step(names[0]), 1)
            dve.wait_ge(steps.sem, steps.at(names[0], turn))
            dve.sem_inc(passed)
            for k in range(K):
                ins = dve.bn_aggr(norm["moments"][:, k, :], norm["stats"][:, k, :])
            ins.then_inc(steps.step(names[1]), 1)

        def deviation(act, norm, column=0):
            return act.activation(norm["dev"][:, :], norm["moments"][:, :, 1], ACT.Sqrt,
                                  bias=eps[:, column:column + 1])

        def norm_tiles(ph, name):
            return {"stats": ph.one(f"{name}_stats", [P, K, 6]), "moments": ph.one(f"{name}_moments", [P, K, 2]),
                    "dev": ph.one(f"{name}_dev", [P, K]), "rstd": ph.one(f"{name}_rstd", [P, K])}

        def normalize(dve, dst, src, norm):
            for k in range(K):
                ins = dve.tensor_scalar(dst[:, k, :], src[:, k, :], norm["moments"][:, k, 0:1],
                                        norm["rstd"][:, k:k + 1], ALU.subtract, ALU.mult)
            return ins

        def inverted(dve, norm):
            return dve.reciprocal(norm["rstd"][:, :], norm["dev"][:, :])

        def transposed(pe, dst, src):
            for k in range(K):
                ins = pe.transpose(dst[:, k * P:(k + 1) * P], src[:, k, :], ident[:, :])
            return ins

        def index_edges():
            ph = Phase("count")
            with ph.ctx:
                dst_col, dst_row = ph.sb("dst_col", [P, K], I32), ph.sb("dst_row", [P, ROWS], I32)
                edge_no = ph.sb("edge_no", [P, K])
                same, earlier = ph.one("same", [P, K, P]), ph.one("earlier", [P, K, P])
                n_earlier, first = ph.one("n_earlier", [P, K]), ph.sb("first", [P, K])
                count = ph.sb("count", [P, K])
                dst_f, node, at = ph.one("dst_f", [P, K]), ph.one("node", [P, K]), ph.one("at", [P, K])
                count_at, edge_at = ph.sb("count_at", [P, K], I32), ph.sb("edge_at", [P, K], I32)
                cols_in, first_out = ph.dmas("cols_in", 3), ph.dmas("first_out")
                found = ph.steps("found", "same", "earlier", "n_earlier", "count", "first", "dst_f", "less",
                                 "picked", "node", "scaled", "count_at", "edge_at")
                counted = [ph.sem(f"counted{k}") for k in range(K)]
                named = [ph.sem(f"named{k}") for k in range(K)]
                go = ph.sem("go")
                rec = node_rec.rearrange("n (r o) -> (n r) o", o=1)

                def done_with(engine, turn):
                    if turn.known and turn.number < 0:
                        return
                    for k in range(K):
                        engine.wait_ge(counted[k], turn.number * 16 + 16)
                        engine.wait_ge(named[k], turn.number * 16 + 16)

                with nc.Block() as block:
                    @block.sync
                    def _(sp):
                        def body(t):
                            s = t.slot
                            if t.follows(2):
                                sp.wait_ge(found.sem, found.at("edge_at", t - 2))
                            done_with(sp, t - 2)
                            sp.dma_start(dst_col[s][:, :], group(a["dst"], t)).then_inc(cols_in.sems[t.slot], 16)
                            sp.dma_start(edge_no[s][:, :], group(a["edge_no"], t)).then_inc(cols_in.sems[t.slot], 16)
                            sp.dma_start(
                                dst_row[s][:, :],
                                a["dst"][bass.ds(t.number * ROWS, ROWS), :].rearrange("e o -> (e o)")
                                .partition_broadcast(P)).then_inc(cols_in.sems[t.slot], 16)

                        run(sp, EG, 0, body)

                    @block.scalar
                    def _(act):
                        def body(t):
                            s = t.slot
                            act.wait_ge(found.sem, found.at("first", t))
                            act.dma_start(block_of(first_e, t), first[s][:, :]).then_inc(first_out.sems[t.slot], 16)

                        run(act, EG, 0, body)
                        act.wait_ge(first_out.sems[(Turn(None, EG - 2)).slot], first_out.full(Turn(None, EG - 2)))
                        act.wait_ge(first_out.sems[(Turn(None, EG - 1)).slot], first_out.full(Turn(None, EG - 1)))

                    @block.vector
                    def _(dve):
                        def body(t):
                            s = t.slot
                            dve.wait_ge(cols_in.sems[t.slot], cols_in.full(t))
                            done_with(dve, t - 2)
                            if t.follows(2):
                                dve.wait_ge(first_out.sems[(t - 2).slot], first_out.full(t - 2))
                            dve.tensor_tensor(
                                same[:, :, :], dst_row[s].rearrange("p (q k) -> p k q", k=K),
                                over(dst_col[s][:, :], P), ALU.is_equal).then_inc(found.step("same"), 1)
                            dve.wait_ge(found.sem, found.at("same", t))
                            dve.tensor_tensor(earlier[:, :, :], same[:, :, :], before[:, :, :],
                                                         ALU.mult).then_inc(found.step("earlier"), 1)
                            dve.wait_ge(found.sem, found.at("earlier", t))
                            dve.tensor_reduce(n_earlier[:, :], earlier[:, :, :], AX_X, ALU.add).then_inc(found.step("n_earlier"), 1)
                            dve.tensor_reduce(count[s][:, :], same[:, :, :], AX_X, ALU.add).then_inc(found.step("count"), 1)
                            dve.wait_ge(found.sem, found.at("n_earlier", t))
                            dve.tensor_scalar(first[s][:, :], n_earlier[:, :], 0.0, None,
                                                         ALU.is_equal).then_inc(found.step("first"), 1)
                            dve.tensor_copy(dst_f[:, :], dst_col[s][:, :]).then_inc(found.step("dst_f"), 1)
                            dve.wait_ge(found.sem, found.at("dst_f", t))
                            dve.tensor_tensor(node[:, :], dst_f[:, :], spare_node[:, :],
                                                         ALU.subtract).then_inc(found.step("less"), 1)
                            dve.wait_ge(found.sem, found.at("less", t))
                            dve.tensor_tensor(node[:, :], node[:, :], first[s][:, :], ALU.mult).then_inc(found.step("picked"), 1)
                            dve.wait_ge(found.sem, found.at("picked", t))
                            dve.tensor_tensor(node[:, :], node[:, :], spare_node[:, :], ALU.add).then_inc(found.step("node"), 1)
                            dve.wait_ge(found.sem, found.at("node", t))
                            dve.scalar_tensor_tensor(at[:, :], node[:, :], float(REC), lane[:, 0:K],
                                                                ALU.mult, ALU.add).then_inc(found.step("scaled"), 1)
                            dve.wait_ge(found.sem, found.at("scaled", t))
                            dve.tensor_copy(count_at[s][:, :], at[:, :]).then_inc(found.step("count_at"), 1)
                            dve.tensor_scalar(edge_at[s][:, :], at[:, :], float(K), None, ALU.add).then_inc(found.step("edge_at"), 1)

                        run(dve, EG, 0, body)

                    @block.gpsimd
                    def _(pool):
                        def body(t):
                            s = t.slot
                            pool.wait_ge(found.sem, found.at("edge_at", t))
                            pool.wait_ge(cols_in.sems[t.slot], cols_in.full(t))
                            for k in range(K):
                                if not (t.known and t.number == 0):
                                    pool.wait_ge(counted[k], t.number * 16)
                                    pool.wait_ge(named[k], t.number * 16)
                                indirect(pool, go, out=rec, out_offset=rows_at(count_at[s][:, k:k + 1]),
                                         in_=count[s][:, k:k + 1], in_offset=None,
                                         compute_op=ALU.add).then_inc(counted[k], 16)
                                indirect(pool, go, out=rec, out_offset=rows_at(edge_at[s][:, k:k + 1]),
                                         in_=edge_no[s][:, k:k + 1], in_offset=None).then_inc(named[k], 16)

                        run(pool, EG, 0, body)
                        done_with(pool, Turn(None, EG - 1))

            ph = Phase("recs")
            with ph.ctx:
                src_col, dst_col = ph.sb("src_col", [P, K], I32), ph.sb("dst_col", [P, K], I32)
                edge_no, first = ph.sb("edge_no", [P, K]), ph.sb("first", [P, K])
                src_rec, dst_rec = ph.sb("src_rec", [P, K, REC]), ph.sb("dst_rec", [P, K, REC])
                degree, root = ph.one("degree", [P, 2 * K]), ph.one("root", [P, 2 * K])
                scale = ph.sb("scale", [P, 2 * K])
                rep, mine, dst_f = ph.one("rep", [P, K]), ph.one("mine", [P, K]), ph.one("dst_f", [P, K])
                to_add, to_soft, to_write = (ph.one(n, [P, K]) for n in ("to_add", "to_soft", "to_write"))
                index, nodevec = ph.sb("index", [P, 6 * K], I32), ph.sb("nodevec", [P, K])
                cols_in, out_dmas = ph.dmas("cols_in", 4), ph.dmas("out", 3)
                fetched = [[ph.sem(f"fetched{i}{k}") for k in range(2)] for i in range(2)]
                go = ph.sem("go")
                made = ph.steps("made", "sums", "scale", "rep1", "rep", "mine", "dst_f", "a0", "a1",
                                "a2", "b0", "b1", "b2", "all")
                rooted = ph.steps("rooted", "root")

                def fetched_wait(engine, t):
                    if t.known and t.number < 0:
                        return
                    for i in range(2):
                        engine.wait_ge(fetched[i][t.slot], 64 * t.half + 64)

                with nc.Block() as block:
                    @block.sync
                    def _(sp):
                        def body(t):
                            s = t.slot
                            if t.follows(2):
                                sp.wait_ge(made.sem, made.at("all", t - 2))
                            for tile, table in ((src_col, "src"), (dst_col, "dst"), (edge_no, "edge_no")):
                                sp.dma_start(tile[s][:, :], group(a[table], t)).then_inc(cols_in.sems[t.slot], 16)
                            sp.dma_start(first[s][:, :], block_of(first_e, t)).then_inc(cols_in.sems[t.slot], 16)

                        run(sp, EG, 0, body)

                    @block.gpsimd
                    def _(pool):
                        def body(t):
                            s = t.slot
                            pool.wait_ge(cols_in.sems[t.slot], cols_in.full(t))
                            if t.follows(2):
                                pool.wait_ge(made.sem, made.at("all", t - 2))
                            for i, (rec, col) in enumerate(((src_rec, src_col), (dst_rec, dst_col))):
                                for k in range(K):
                                    indirect(pool, go, out=rec[s][:, k, :], out_offset=None, in_=node_rec,
                                             in_offset=rows_at(col[s][:, k:k + 1])).then_inc(fetched[i][s], 16)

                        run(pool, EG, 0, body)

                    @block.vector
                    def _(dve):
                        def body(t):
                            s = t.slot
                            dve.wait_ge(cols_in.sems[t.slot], cols_in.full(t))
                            fetched_wait(dve, t)
                            if t.follows(2):
                                dve.wait_ge(out_dmas.sems[(t - 2).slot], out_dmas.full(t - 2))
                            dve.tensor_reduce(degree[:, 0:K], src_rec[s][:, :, 0:K], AX_X, ALU.add)
                            dve.tensor_reduce(degree[:, K:2 * K], dst_rec[s][:, :, 0:K], AX_X,
                                                        ALU.add).then_inc(made.step("sums"), 1)
                            dve.wait_ge(made.sem, made.at("sums", t))
                            dve.wait_ge(rooted.sem, rooted.at("root", t))
                            dve.reciprocal(scale[s][:, :], root[:, :]).then_inc(made.step("scale"), 1)
                            dve.tensor_reduce(rep[:, :], dst_rec[s][:, :, K:2 * K], AX_X, ALU.max).then_inc(made.step("rep1"), 1)
                            dve.wait_ge(made.sem, made.at("rep1", t))
                            dve.tensor_scalar(rep[:, :], rep[:, :], -1.0, None, ALU.add).then_inc(made.step("rep"), 1)
                            dve.wait_ge(made.sem, made.at("rep", t))
                            dve.scalar_tensor_tensor(mine[:, :], rep[:, :], 1.0, edge_no[s][:, :],
                                                               ALU.add, ALU.is_equal).then_inc(made.step("mine"), 1)
                            dve.tensor_copy(dst_f[:, :], dst_col[s][:, :]).then_inc(made.step("dst_f"), 1)
                            dve.wait_ge(made.sem, made.at("dst_f", t))
                            dve.scalar_tensor_tensor(to_add[:, :], rep[:, :], 2.0, lane[:, K:2 * K],
                                                     ALU.mult, ALU.add)
                            dve.scalar_tensor_tensor(to_soft[:, :], rep[:, :], float(K), lane[:, 2 * K:3 * K],
                                                     ALU.mult, ALU.add)
                            dve.tensor_tensor(to_write[:, :], dst_f[:, :], spare_node[:, :],
                                                        ALU.subtract).then_inc(made.step("a0"), 1)
                            dve.wait_ge(made.sem, made.at("a0", t))
                            dve.tensor_tensor(to_add[:, :], to_add[:, :], first[s][:, :], ALU.mult)
                            dve.tensor_tensor(to_soft[:, :], to_soft[:, :], first[s][:, :], ALU.mult)
                            dve.tensor_tensor(to_write[:, :], to_write[:, :], mine[:, :], ALU.mult).then_inc(made.step("a1"), 1)
                            dve.wait_ge(made.sem, made.at("a1", t))
                            dve.scalar_tensor_tensor(index[s][:, ADD_AT:ADD_AT + K], to_add[:, :],
                                                     float(2 * EP), lane[:, 3 * K:4 * K], ALU.add, ALU.add)
                            dve.scalar_tensor_tensor(index[s][:, SOFT_AT:SOFT_AT + K], to_soft[:, :],
                                                     float(K * EP), lane[:, 3 * K:4 * K], ALU.add, ALU.add)
                            dve.tensor_tensor(index[s][:, WRITE_AT:WRITE_AT + K], to_write[:, :],
                                                        spare_node[:, :], ALU.add).then_inc(made.step("a2"), 1)
                            dve.tensor_copy(index[s][:, REP:REP + K], rep[:, :]).then_inc(made.step("b0"), 1)
                            dve.tensor_copy(index[s][:, SRC:SRC + K], src_col[s][:, :]).then_inc(made.step("b1"), 1)
                            dve.tensor_copy(index[s][:, DST:DST + K], dst_col[s][:, :]).then_inc(made.step("b2"), 1)
                            dve.tensor_copy(nodevec[s][:, :], dst_rec[s][:, :, 8]).then_inc(made.step("all"), 1)

                        run(dve, EG, 0, body)

                    @block.scalar
                    def _(act):
                        def body(t):
                            s = t.slot
                            act.wait_ge(made.sem, made.at("sums", t))
                            act.activation(root[:, :], degree[:, :], ACT.Sqrt, bias=ones[:, 0:1]).then_inc(rooted.step("root"), 1)
                            act.wait_ge(made.sem, made.at("all", t))
                            act.dma_start(block_of(index_rec, t), index[s][:, :]).then_inc(out_dmas.sems[t.slot], 16)
                            act.dma_start(block_of(scale_rec, t), scale[s][:, :]).then_inc(out_dmas.sems[t.slot], 16)
                            act.dma_start(group(nodevec_e, t), nodevec[s][:, :]).then_inc(out_dmas.sems[t.slot], 16)

                        run(act, EG, 0, body)
                        act.wait_ge(out_dmas.sems[(Turn(None, EG - 2)).slot], out_dmas.full(Turn(None, EG - 2)))
                        act.wait_ge(out_dmas.sems[(Turn(None, EG - 1)).slot], out_dmas.full(Turn(None, EG - 1)))

        def kv_tiles(ph):
            return {
                "k_raw": ph.one("k_raw", [P, K, D]), "k": ph.one("k", [P, K, D]), "v": ph.one("v", [P, K, D + 1]), "k_sq": ph.one("k_sq", [P, K, D]),
                "k_norm": ph.one("k_norm", [P, K]), "k_dev": ph.one("k_dev", [P, K]), "pk": ph.bank("pk"), "pv": ph.bank("pv"),
                "sum": ph.bank("sum"),
            }

        def kv_project(pe, ph, cur, wk, wv):
            for w, bank in ((wk, "pk"), (wv, "pv")):
                for k in range(K):
                    ins = pe.matmul(ph[bank][:, k * D:(k + 1) * D], cur[:, k * P:(k + 1) * P], W[w],
                                    start=True, stop=True)
                yield ins

        def kv_sum(pe, ph, rows, first=False):
            for k in range(K):
                ins = pe.matmul(ph["sum"][:, 0:D + 1], ph["k"][0:rows, k, :], ph["v"][0:rows, k, :],
                                start=False, stop=False, skip_group_check=True)
            return ins

        def kv_clear(pe, ph):
            pe.matmul(ph["sum"][:, 0:D + 1], zeros[:, 0, :], flat(zeros[:, 0:2, :])[:, 0:D + 1], start=True,
                      stop=False, skip_group_check=True)

        KV_STEPS = ("k", "k_sq", "k_norm", "v")

        def kv_guard(dve, ph, steps, t):
            raw = ph["k_raw"][:, :, :]
            dve.scalar_tensor_tensor(ph["k"][:, :, :], raw, 0.0, raw, ALU.is_equal, ALU.add).then_inc(steps.step("k"), 1)
            dve.wait_ge(steps.sem, steps.at("k", t))
            for k in range(K):
                ins = dve.tensor_tensor_reduce(ph["k_sq"][:, k, :], ph["k"][:, k, :], ph["k"][:, k, :], 1.0, 0.0,
                                               ALU.mult, ALU.add, ph["k_norm"][:, k:k + 1])
            ins.then_inc(steps.step("k_sq"), 1)

        def kv_root(act, ph):
            return act.activation(ph["k_dev"][:, :], ph["k_norm"][:, :], ACT.Sqrt)

        def kv_scale(dve, ph, steps, t):
            dve.reciprocal(ph["v"][:, :, D], ph["k_dev"][:, :]).then_inc(steps.step("k_norm"), 1)
            dve.wait_ge(steps.sem, steps.at("k_norm", t))
            dve.tensor_tensor(ph["v"][:, :, 0:D], by_k(ph["pv"][:, :]), over(ph["v"][:, :, D], D),
                                         ALU.mult).then_inc(steps.step("v"), 1)

        def dense_first():
            ph = Phase("first")
            with ph.ctx:
                x, x_norm, y_norm = ph.sb("x", [P, K, D]), norm_tiles(ph, "x"), norm_tiles(ph, "y")
                xn, hT = ph.sb("xn", [P, K, D]), ph.sb("hT", [P, ROWS])
                gT = [ph.one(f"g{i}T", [P, K, P]) for i in range(LAYERS + 1)]
                u = ph.one("u", [P, K, P])
                rows_out = [ph.sb(f"rows{i}", [P, ROWS]) for i in range(LAYERS + 1)]
                y, yn, tT = ph.one("y", [P, K, D]), ph.one("yn", [P, K, D]), ph.sb("tT", [P, ROWS])
                pa, pg, pt, pr = ph.bank("pa"), ph.bank("pg"), ph.bank("pt"), ph.bank("pr")
                kvt = kv_tiles(ph)
                x_in, g_out, t_out = ph.dmas("x_in"), ph.dmas("g_out", LAYERS + 1), ph.dmas("t_out")
                normed = ph.steps("normed", "stats", "moments", "rstd", "xn")
                y_done = ph.steps("y_done", "y", "stats", "moments", "rstd", "yn", *KV_STEPS)
                pe_x, act_x = ph.steps("pe_x", "xT"), ph.steps("act_x", "dev")
                pe_g = ph.steps("pe_g", "g", "t", "g0r", "c0", "yT", "c1", "g1r", "k", "v", "c2", "g2r",
                                "g3r", "sum")
                act_h = ph.steps("act_h", "hT")
                act_g = ph.steps("act_g", "g0T", "g0r", "u0", "dev", "tT", "u1", "g1r", "k_raw", "u2", "g2r",
                                 "k_root", "g3r")
                added = ph.steps("added", "g1T", "g2T", "g3T")
                kept = ph.sem("kept")

                with nc.Block() as block:
                    @block.sync
                    def _(sp):
                        def body(t):
                            if inside(t, NG):
                                if t.follows(2):
                                    sp.wait_ge(normed.sem, normed.at("xn", t - 2))
                                sp.dma_start(flat(x[t.slot][:, :, :]), group(a["x"], t)).then_inc(x_in.sems[t.slot], 16)
                            b = t - 1
                            if inside(b, NG):
                                for i, step in enumerate(("g0r", "g1r", "g2r", "g3r")):
                                    sp.wait_ge(act_g.sem, act_g.at(step, b))
                                    sp.dma_start(group(g_rows[i], b), rows_out[i][b.slot][:, :]).then_inc(g_out.sems[b.slot], 16)
                                sp.wait_ge(act_g.sem, act_g.at("tT", b))
                                sp.dma_start(block_of(t0_T, b), tT[b.slot][:, :]).then_inc(t_out.sems[b.slot], 16)

                        run(sp, NG, 1, body)
                        for t in (NG - 2, NG - 1):
                            sp.wait_ge(g_out.sems[(Turn(None, t)).slot], g_out.full(Turn(None, t)))
                            sp.wait_ge(t_out.sems[(Turn(None, t)).slot], t_out.full(Turn(None, t)))

                    @block.vector
                    def _(dve):
                        def body(t):
                            s = t.slot
                            if inside(t, NG):
                                dve.wait_ge(x_in.sems[t.slot], x_in.full(t))
                                moments_of(dve, normed, t, x[s], x_norm, ("stats", "moments"))
                                dve.wait_ge(act_x.sem, act_x.at("dev", t))
                                inverted(dve, x_norm).then_inc(normed.step("rstd"), 1)
                                dve.wait_ge(normed.sem, normed.at("rstd", t))
                                if t.follows(2):
                                    dve.wait_ge(pe_x.sem, pe_x.at("xT", t - 2))
                                normalize(dve, xn[s], x[s], x_norm).then_inc(normed.step("xn"), 1)
                            b = t - 1
                            if inside(b, NG):
                                dve.wait_ge(pe_g.sem, pe_g.at("t", b))
                                dve.tensor_tensor(y[:, :, :], by_k(pt[:, :]), R["t_b"], ALU.add).then_inc(y_done.step("y"), 1)
                                dve.wait_ge(y_done.sem, y_done.at("y", b))
                                moments_of(dve, y_done, b, y, y_norm, ("stats", "moments"))
                                dve.wait_ge(act_g.sem, act_g.at("dev", b))
                                inverted(dve, y_norm).then_inc(y_done.step("rstd"), 1)
                                dve.wait_ge(y_done.sem, y_done.at("rstd", b))
                                if b.follows(1):
                                    dve.wait_ge(pe_g.sem, pe_g.at("yT", b - 1))
                                normalize(dve, yn, y, y_norm).then_inc(y_done.step("yn"), 1)
                                if b.follows(1):
                                    dve.wait_ge(pe_g.sem, pe_g.at("sum", b - 1))
                                dve.wait_ge(act_g.sem, act_g.at("k_raw", b))
                                dve.wait_ge(pe_g.sem, pe_g.at("v", b))
                                kv_guard(dve, kvt, y_done, b)
                                dve.wait_ge(act_g.sem, act_g.at("k_root", b))
                                kv_scale(dve, kvt, y_done, b)

                        run(dve, NG, 1, body)
                        dve.wait_ge(pe_g.sem, pe_g.at("sum", Turn(None, NG - 1)))
                        dve.tensor_copy(kv[0][:, :], kvt["sum"][:, 0:D + 1]).then_inc(kept, 1)
                        dve.wait_ge(kept, 1)

                    @block.gpsimd
                    def _(pool):
                        def body(t):
                            for i, step in enumerate(("u0", "u1", "u2")):
                                pool.wait_ge(act_g.sem, act_g.at(step, t))
                                if t.follows(1):
                                    pool.wait_ge(pe_g.sem, pe_g.at(("g1r", "g2r", "g3r")[i], t - 1))
                                pool.tensor_tensor(gT[i + 1][:, :, :], u[:, :, :], gT[0][:, :, :],
                                                              ALU.add).then_inc(added.step(("g1T", "g2T", "g3T")[i]), 1)

                        run(pool, NG, 0, body)

                    @block.scalar
                    def _(act):
                        def relu(dst, src, bias=None, scale=1.0):
                            if bias is None:
                                return act.activation(dst, src, ACT.Relu)
                            return act.activation(dst, src, ACT.Relu, bias=bias, scale=scale)

                        def to_rows(b, i):
                            step = f"g{i}r"
                            act.wait_ge(pe_g.sem, pe_g.at(step, b))
                            if i == 0:
                                if b.follows(2):
                                    act.wait_ge(g_out.sems[(b - 2).slot], g_out.full(b - 2))
                            act.copy(rows_out[i][b.slot][:, :], pr[:, :]).then_inc(act_g.step(step), 1)

                        def body(t):
                            if inside(t, NG):
                                act.wait_ge(normed.sem, normed.at("moments", t))
                                deviation(act, x_norm).then_inc(act_x.step("dev"), 1)
                            b = t - 1
                            if inside(b, NG):
                                act.wait_ge(pe_g.sem, pe_g.at("g", b))
                                if b.follows(1):
                                    act.wait_ge(added.sem, added.at("g3T", b - 1))
                                if b.follows(1):
                                    act.wait_ge(pe_g.sem, pe_g.at("g0r", b - 1))
                                relu(flat(gT[0][:, :, :]), pg[:, :], bn_bias[:, 0:1],
                                                bn_scale[:, 0:1]).then_inc(act_g.step("g0T"), 1)
                                to_rows(b, 0)
                                act.wait_ge(pe_g.sem, pe_g.at("c0", b))
                                relu(flat(u[:, :, :]), pg[:, :], bn_bias[:, 1:2], bn_scale[:, 1:2]).then_inc(act_g.step("u0"), 1)
                                act.wait_ge(y_done.sem, y_done.at("moments", b))
                                deviation(act, y_norm).then_inc(act_g.step("dev"), 1)
                                act.wait_ge(pe_g.sem, pe_g.at("yT", b))
                                if b.follows(2):
                                    act.wait_ge(t_out.sems[(b - 2).slot], t_out.full(b - 2))
                                if b.follows(2):
                                    act.wait_ge(pe_g.sem, pe_g.at("v", b - 2))
                                relu(tT[b.slot][:, :], pt[:, :], C["lb0"], C["lg0"]).then_inc(act_g.step("tT"), 1)
                                for i in (1, 2):
                                    act.wait_ge(pe_g.sem, pe_g.at(f"c{i}", b))
                                    act.wait_ge(added.sem, added.at(f"g{i}T", b))
                                    relu(flat(u[:, :, :]), pg[:, :], bn_bias[:, i + 1:i + 2],
                                                    bn_scale[:, i + 1:i + 2]).then_inc(act_g.step(f"u{i}"), 1)
                                    to_rows(b, i)
                                    if i == 1:
                                        act.wait_ge(pe_g.sem, pe_g.at("k", b))
                                        if b.follows(1):
                                            act.wait_ge(y_done.sem, y_done.at("k", b - 1))
                                        act.copy(flat(kvt["k_raw"][:, :, :]), kvt["pk"][:, :]).then_inc(act_g.step("k_raw"), 1)
                                act.wait_ge(y_done.sem, y_done.at("k_sq", b))
                                kv_root(act, kvt).then_inc(act_g.step("k_root"), 1)
                                to_rows(b, 3)
                            if inside(t, NG):
                                act.wait_ge(pe_x.sem, pe_x.at("xT", t))
                                if t.follows(2):
                                    act.wait_ge(pe_g.sem, pe_g.at("t", t - 2))
                                relu(hT[t.slot][:, :], pa[:, :]).then_inc(act_h.step("hT"), 1)

                        run(act, NG, 1, body)

                    @block.tensor
                    def _(pe):
                        def product(bank, w, right):
                            return pe.matmul(bank[:, :], W[w], right, start=True, stop=True)

                        def to_rows(b, i, step, turn):
                            if turn.follows(0):
                                    pe.wait_ge(act_g.sem, act_g.at(step, turn))
                            transposed(pe, pr, gT[i]).then_inc(pe_g.step(f"g{i}r"), 1)

                        kv_clear(pe, kvt)

                        def body(t):
                            b = t - 1
                            if inside(b, NG):
                                s = b.slot
                                pe.wait_ge(act_h.sem, act_h.at("hT", b))
                                if b.follows(1):
                                    pe.wait_ge(act_g.sem, act_g.at("u2", b - 1))
                                product(pg, "g_w", hT[s][:, :]).then_inc(pe_g.step("g"), 1)
                                if b.follows(1):
                                    pe.wait_ge(act_g.sem, act_g.at("tT", b - 1))
                                for k in range(K):
                                    ins = pe.matmul(pt[:, k * D:(k + 1) * D], hT[s][:, k * P:(k + 1) * P],
                                                    W["t_w"], start=True, stop=True)
                                ins.then_inc(pe_g.step("t"), 1)
                                pe.wait_ge(act_g.sem, act_g.at("g0T", b))
                                to_rows(b, 0, "g3r", b - 1)
                                product(pg, "c0", flat(gT[0][:, :, :])).then_inc(pe_g.step("c0"), 1)
                                pe.wait_ge(y_done.sem, y_done.at("yn", b))
                                transposed(pe, pt, yn).then_inc(pe_g.step("yT"), 1)
                                pe.wait_ge(added.sem, added.at("g1T", b))
                                product(pg, "c1", flat(gT[1][:, :, :])).then_inc(pe_g.step("c1"), 1)
                                to_rows(b, 1, "g0r", b)
                                pe.wait_ge(act_g.sem, act_g.at("tT", b))
                                if b.follows(1):
                                    pe.wait_ge(y_done.sem, y_done.at("v", b - 1))
                                for ins, step in zip(kv_project(pe, kvt, tT[s], "wk0", "wv0"), ("k", "v")):
                                    ins.then_inc(pe_g.step(step), 1)
                                pe.wait_ge(added.sem, added.at("g2T", b))
                                product(pg, "c2", flat(gT[2][:, :, :])).then_inc(pe_g.step("c2"), 1)
                                to_rows(b, 2, "g1r", b)
                                pe.wait_ge(added.sem, added.at("g3T", b))
                                to_rows(b, 3, "g2r", b)
                                pe.wait_ge(y_done.sem, y_done.at("v", b))
                                full = not (b.known and b.number == NG - 1)
                                kv_sum(pe, kvt, P if full else last_parts).then_inc(pe_g.step("sum"), 1)
                            if inside(t, NG):
                                pe.wait_ge(normed.sem, normed.at("xn", t))
                                if t.follows(1):
                                    pe.wait_ge(act_h.sem, act_h.at("hT", t - 1))
                                transposed(pe, pa, xn[t.slot]).then_inc(pe_x.step("xT"), 1)

                        run(pe, NG, 1, body)

        ATTEND_STEPS = ("q", "norm", "shares", "share", "den", "rden", "weights", "t", "y", "stats",
                        "moments", "rstd", "yn")

        def attend_tiles(ph):
            return {
                "cT": ph.sb("cT", [P, ROWS]), "q_raw": ph.one("q_raw", [P, K, P]), "qT": ph.one("qT", [P, K, P]), "rows": ph.one("rows", [P, K, D]), "qT_sq": ph.one("qT_sq", [P, K, P]),
                "rq": ph.one("rq", [P, K]), "den": ph.one("den", [P, K]), "rden": ph.one("rden", [P, K]),
                "wkv": ph.one("wkv", [P, K]), "wv": ph.one("wv", [P, K]), "t": ph.one("t", [P, K, D]),
                "y": ph.one("y", [P, K, D]), "yn": ph.one("yn", [P, K, D]),
                "norm": norm_tiles(ph, "a"), "q_dev": ph.one("q_dev", [P, K]),
                "pq": ph.bank("pq"), "pn": ph.bank("pn"), "pav": ph.bank("pav"), "pu": ph.bank("pu"),
            }

        def attend_guard(dve, at, steps, pe_a, act_a, t):
            dve.wait_ge(act_a.sem, act_a.at("q_raw", t))
            raw = at["q_raw"][:, :, :]
            if t.follows(1):
                dve.wait_ge(pe_a.sem, pe_a.at("apply", t - 1))
            if t.follows(1):
                dve.wait_ge(act_a.sem, act_a.at("q_sq", t - 1))
            dve.scalar_tensor_tensor(at["qT"][:, :, :], raw, 0.0, raw, ALU.is_equal, ALU.add).then_inc(steps.step("q"), 1)

        def attend_mix(dve, at, steps, pe_a, act_a, t):
            dve.wait_ge(pe_a.sem, pe_a.at("apply", t))
            dve.wait_ge(act_a.sem, act_a.at("q_dev", t))
            dve.reciprocal(at["rq"][:, :], at["q_dev"][:, :]).then_inc(steps.step("norm"), 1)
            dve.wait_ge(steps.sem, steps.at("norm", t))
            dve.tensor_tensor(at["den"][:, :], at["pn"][:, K:2 * K], at["rq"][:, :], ALU.mult).then_inc(steps.step("shares"), 1)
            dve.wait_ge(steps.sem, steps.at("shares", t))
            dve.tensor_scalar(at["den"][:, :], at["den"][:, :], float(n_nodes), None, ALU.add).then_inc(steps.step("share"), 1)
            dve.wait_ge(steps.sem, steps.at("share", t))
            dve.reciprocal(at["rden"][:, :], at["den"][:, :]).then_inc(steps.step("den"), 1)
            dve.wait_ge(steps.sem, steps.at("den", t))
            dve.tensor_tensor(at["wkv"][:, :], at["rq"][:, :], at["rden"][:, :], ALU.mult).then_inc(steps.step("rden"), 1)
            dve.tensor_scalar(at["wv"][:, :], at["rden"][:, :], float(n_nodes), None, ALU.mult).then_inc(steps.step("weights"), 1)
            dve.wait_ge(steps.sem, steps.at("weights", t))
            dve.wait_ge(act_a.sem, act_a.at("rows", t))
            for k in range(K):
                ins = dve.scalar_tensor_tensor(at["t"][:, k, :], at["pu"][:, k * D:(k + 1) * D],
                                               at["wkv"][:, k:k + 1], at["rows"][:, k, :], ALU.mult, ALU.add)
            ins.then_inc(steps.step("t"), 1)
            dve.wait_ge(steps.sem, steps.at("t", t))
            for k in range(K):
                ins = dve.scalar_tensor_tensor(at["y"][:, k, :], at["pav"][:, k * D:(k + 1) * D],
                                               at["wv"][:, k:k + 1], at["t"][:, k, :], ALU.mult, ALU.add)
            ins.then_inc(steps.step("y"), 1)
            dve.wait_ge(steps.sem, steps.at("y", t))
            moments_of(dve, steps, t, at["y"], at["norm"], ("stats", "moments"))

        def attend_normalize(dve, at, steps, pe_y, act_a, t):
            dve.wait_ge(act_a.sem, act_a.at("dev", t))
            inverted(dve, at["norm"]).then_inc(steps.step("rstd"), 1)
            dve.wait_ge(steps.sem, steps.at("rstd", t))
            if t.follows(1):
                dve.wait_ge(pe_y.sem, pe_y.at("yT", t - 1))
            normalize(dve, at["yn"], at["y"], at["norm"]).then_inc(steps.step("yn"), 1)

        def attend_project(pe, at, layer, c_in, steps, dve_a, act_a, t):
            cT = at["cT"][t.slot]
            pe.wait_ge(c_in.sems[t.slot], c_in.full(t))
            if t.follows(1):
                pe.wait_ge(dve_a.sem, dve_a.at("t", t - 1))
            if t.follows(1):
                pe.wait_ge(act_a.sem, act_a.at("rows", t - 1))
            pe.matmul(at["pq"][:, :], W[f"wq{layer}"], cT[:, :], start=True, stop=True).then_inc(steps.step("q"), 1)
            if t.follows(1):
                pe.wait_ge(dve_a.sem, dve_a.at("y", t - 1))
            for k in range(K):
                ins = pe.matmul(at["pav"][:, k * D:(k + 1) * D], cT[:, k * P:(k + 1) * P], W[f"wv{layer}"],
                                start=True, stop=True)
            ins.then_inc(steps.step("v"), 1)
            pe.wait_ge(act_a.sem, act_a.at("q_raw", t))
            for k in range(K):
                ins = pe.transpose(at["pq"][:, k * D:(k + 1) * D], cT[:, k * P:(k + 1) * P], ident[:, :])
            ins.then_inc(steps.step("rows"), 1)

        def attend_apply(pe, at, kvs, steps, dve_a, act_a, t):
            pe.wait_ge(dve_a.sem, dve_a.at("q", t))
            for k in range(K):
                pe.matmul(at["pu"][:, k * D:(k + 1) * D], at["qT"][:, k, :], kvs[:, 0:D], start=True, stop=True)
                pe.matmul(at["pn"][:, K + k:K + k + 1], at["qT"][:, k, :], kvs[:, D:D + 1], start=True, stop=True)
            pe.wait_ge(act_a.sem, act_a.at("q_sq", t))
            for k in range(K):
                ins = pe.matmul(at["pn"][:, k:k + 1], at["qT_sq"][:, k, :], ones[:, 0:1], start=True, stop=True)
            ins.then_inc(steps.step("apply"), 1)

        def attend_act(act, at, steps, pe_a, dve_a, t):
            act.wait_ge(pe_a.sem, pe_a.at("q", t))
            if t.follows(1):
                act.wait_ge(dve_a.sem, dve_a.at("q", t - 1))
            act.copy(flat(at["q_raw"][:, :, :]), at["pq"][:, :]).then_inc(steps.step("q_raw"), 1)
            act.wait_ge(pe_a.sem, pe_a.at("rows", t))
            if t.follows(1):
                act.wait_ge(dve_a.sem, dve_a.at("t", t - 1))
            act.copy(flat(at["rows"][:, :, :]), at["pq"][:, :]).then_inc(steps.step("rows"), 1)
            act.wait_ge(dve_a.sem, dve_a.at("q", t))
            if t.follows(1):
                act.wait_ge(pe_a.sem, pe_a.at("apply", t - 1))
            act.activation(at["qT_sq"][:, :, :], at["qT"][:, :, :], ACT.Square).then_inc(steps.step("q_sq"), 1)

        def attend_roots(act, at, steps, pe_a, dve_a, t):
            act.wait_ge(pe_a.sem, pe_a.at("apply", t))
            act.activation(at["q_dev"][:, :], at["pn"][:, 0:K], ACT.Sqrt).then_inc(steps.step("q_dev"), 1)
            act.wait_ge(dve_a.sem, dve_a.at("moments", t))
            deviation(act, at["norm"], 1).then_inc(steps.step("dev"), 1)

        ATTEND_PE_STEPS = ("q", "v", "rows", "apply")
        ATTEND_ACT_STEPS = ("q_raw", "rows", "q_sq", "q_dev", "dev")

        def dense_second():
            ph = Phase("second")
            with ph.ctx:
                at, kvt = attend_tiles(ph), kv_tiles(ph)
                tT = ph.sb("tT", [P, ROWS])
                pt = at["pn"]
                c_in, t_out = ph.dmas("c_in"), ph.dmas("t_out")
                dve_a = ph.steps("dve_a", *ATTEND_STEPS)
                pe_a, act_a = ph.steps("pe_a", *ATTEND_PE_STEPS), ph.steps("act_a", *ATTEND_ACT_STEPS)
                dve_k, pe_k = ph.steps("dve_k", *KV_STEPS), ph.steps("pe_k", "k", "v", "sum")
                pe_y, act_t = ph.steps("pe_y", "yT"), ph.steps("act_t", "tT")
                act_k = ph.steps("act_k", "k_raw", "k_root")
                kept = ph.sem("kept")

                with nc.Block() as block:
                    @block.sync
                    def _(sp):
                        def body(t):
                            if inside(t, NG):
                                if t.follows(2):
                                    sp.wait_ge(pe_a.sem, pe_a.at("rows", t - 2))
                                sp.dma_start(at["cT"][t.slot][:, :], block_of(t0_T, t)).then_inc(c_in.sems[t.slot], 16)
                            b = t - 1
                            if inside(b, NG):
                                sp.wait_ge(act_t.sem, act_t.at("tT", b))
                                sp.dma_start(block_of(t1_T, b), tT[b.slot][:, :]).then_inc(t_out.sems[b.slot], 16)

                        run(sp, NG, 1, body)
                        for t in (NG - 2, NG - 1):
                            sp.wait_ge(t_out.sems[(Turn(None, t)).slot], t_out.full(Turn(None, t)))

                    @block.tensor
                    def _(pe):
                        kv_clear(pe, kvt)

                        def body(t):
                            b = t - 1
                            if inside(b, NG):
                                pe.wait_ge(dve_a.sem, dve_a.at("yn", b))
                                pe.wait_ge(act_a.sem, act_a.at("rows", b))
                                transposed(pe, at["pq"], at["yn"]).then_inc(pe_y.step("yT"), 1)
                                pe.wait_ge(act_t.sem, act_t.at("tT", b))
                            if inside(t, NG):
                                attend_project(pe, at, 0, c_in, pe_a, dve_a, act_a, t)
                            if inside(b, NG):
                                if b.follows(1):
                                    pe.wait_ge(dve_k.sem, dve_k.at("v", b - 1))
                                for ins, step in zip(kv_project(pe, kvt, tT[b.slot], "wk1", "wv1"), ("k", "v")):
                                    ins.then_inc(pe_k.step(step), 1)
                            if inside(t, NG):
                                attend_apply(pe, at, kv[0], pe_a, dve_a, act_a, t)
                            if inside(b, NG):
                                pe.wait_ge(dve_k.sem, dve_k.at("v", b))
                                full = not (b.known and b.number == NG - 1)
                                kv_sum(pe, kvt, P if full else last_parts).then_inc(pe_k.step("sum"), 1)

                        run(pe, NG, 1, body)

                    @block.scalar
                    def _(act):
                        def body(t):
                            b = t - 1
                            if inside(b, NG):
                                act.wait_ge(pe_y.sem, pe_y.at("yT", b))
                                if b.follows(2):
                                    act.wait_ge(t_out.sems[(b - 2).slot], t_out.full(b - 2))
                                if b.follows(2):
                                    act.wait_ge(pe_k.sem, pe_k.at("v", b - 2))
                                act.activation(tT[b.slot][:, :], at["pq"][:, :], ACT.Relu,
                                                          bias=C["lb1"], scale=C["lg1"]).then_inc(act_t.step("tT"), 1)
                            if inside(t, NG):
                                attend_act(act, at, act_a, pe_a, dve_a, t)
                            if inside(b, NG):
                                act.wait_ge(pe_k.sem, pe_k.at("k", b))
                                if b.follows(1):
                                    act.wait_ge(dve_k.sem, dve_k.at("k", b - 1))
                                act.copy(flat(kvt["k_raw"][:, :, :]), kvt["pk"][:, :]).then_inc(act_k.step("k_raw"), 1)
                                act.wait_ge(dve_k.sem, dve_k.at("k_sq", b))
                                kv_root(act, kvt).then_inc(act_k.step("k_root"), 1)
                            if inside(t, NG):
                                attend_roots(act, at, act_a, pe_a, dve_a, t)

                        run(act, NG, 1, body)

                    @block.vector
                    def _(dve):
                        def body(t):
                            if inside(t, NG):
                                attend_guard(dve, at, dve_a, pe_a, act_a, t)
                            b = t - 1
                            if inside(b, NG):
                                if b.follows(1):
                                    dve.wait_ge(pe_k.sem, pe_k.at("sum", b - 1))
                                dve.wait_ge(act_k.sem, act_k.at("k_raw", b))
                                kv_guard(dve, kvt, dve_k, b)
                            if inside(t, NG):
                                attend_mix(dve, at, dve_a, pe_a, act_a, t)
                            if inside(b, NG):
                                dve.wait_ge(act_k.sem, act_k.at("k_root", b))
                                dve.wait_ge(pe_k.sem, pe_k.at("v", b))
                                kv_scale(dve, kvt, dve_k, b)
                            if inside(t, NG):
                                attend_normalize(dve, at, dve_a, pe_y, act_a, t)

                        run(dve, NG, 1, body)
                        dve.wait_ge(pe_k.sem, pe_k.at("sum", Turn(None, NG - 1)))
                        dve.tensor_copy(kv[1][:, :], kvt["sum"][:, 0:D + 1]).then_inc(kept, 1)
                        dve.wait_ge(kept, 1)

        def dense_third():
            ph = Phase("third")
            with ph.ctx:
                at = attend_tiles(ph)
                x, x2 = ph.sb("x", [P, K, D]), ph.sb("x2", [P, K, D])
                tT, sT = ph.one("tT", [P, ROWS]), ph.one("sT", [P, ROWS])
                xb = ph.one("xb", [P, K, D])
                xl, h = ph.sb("xl", [P, K, D]), ph.one("h", [P, K, D])
                z, zn, zg, xlb = (ph.one(n, [P, K, D]) for n in ("z", "zn", "zg", "xlb"))
                o = ph.sb("o", [P, K, D])
                x_norm, z_norm = norm_tiles(ph, "x"), norm_tiles(ph, "z")
                act_f = ph.steps("act_f", "dev", "z_dev")
                px, po = ph.bank("px"), ph.bank("po")
                c_in, x_in = ph.dmas("c_in"), ph.dmas("x_in", 2)
                xl_out, o_out = ph.dmas("xl_out"), ph.dmas("o_out")
                dve_a = ph.steps("dve_a", *ATTEND_STEPS)
                pe_a, act_a = ph.steps("pe_a", *ATTEND_PE_STEPS), ph.steps("act_a", *ATTEND_ACT_STEPS)
                pe_y, act_t = ph.steps("pe_y", "yT"), ph.steps("act_t", "tT")
                pe_f = ph.steps("pe_f", "x2T", "fc")
                dve_f = ph.steps("dve_f", "sT", "xl", "stats", "moments", "rstd", "h", "z", "z_stats",
                                 "z_moments", "z_rstd", "zn", "zg", "o")
                pool_f = ph.steps("pool_f", "xb", "xlb")

                with nc.Block() as block:
                    @block.sync
                    def _(sp):
                        def body(t):
                            if inside(t, NG):
                                if t.follows(2):
                                    sp.wait_ge(pe_a.sem, pe_a.at("rows", t - 2))
                                sp.dma_start(at["cT"][t.slot][:, :], block_of(t1_T, t)).then_inc(c_in.sems[t.slot], 16)
                                if t.follows(2):
                                    sp.wait_ge(pe_f.sem, pe_f.at("x2T", t - 2))
                                if t.follows(2):
                                    sp.wait_ge(pool_f.sem, pool_f.at("xb", t - 2))
                                sp.dma_start(flat(x[t.slot][:, :, :]), group(a["x"], t)).then_inc(x_in.sems[t.slot], 16)
                                sp.dma_start(flat(x2[t.slot][:, :, :]), group(g_rows[LAYERS], t)).then_inc(x_in.sems[t.slot], 16)
                            b = t - 1
                            if inside(b, NG):
                                sp.wait_ge(dve_f.sem, dve_f.at("xl", b))
                                sp.dma_start(group(xl_rows, b), flat(xl[b.slot][:, :, :])).then_inc(xl_out.sems[b.slot], 16)
                                sp.wait_ge(dve_f.sem, dve_f.at("o", b))
                                sp.dma_start(group(out, b), flat(o[b.slot][:, :, :])).then_inc(o_out.sems[b.slot], 16)

                        run(sp, NG, 1, body)
                        for t in (NG - 2, NG - 1):
                            sp.wait_ge(xl_out.sems[(Turn(None, t)).slot], xl_out.full(Turn(None, t)))
                            sp.wait_ge(o_out.sems[(Turn(None, t)).slot], o_out.full(Turn(None, t)))

                    @block.tensor
                    def _(pe):
                        def body(t):
                            b = t - 1
                            if inside(b, NG):
                                pe.wait_ge(dve_a.sem, dve_a.at("yn", b))
                                pe.wait_ge(act_a.sem, act_a.at("rows", b))
                                transposed(pe, at["pq"], at["yn"]).then_inc(pe_y.step("yT"), 1)
                                pe.wait_ge(x_in.sems[b.slot], x_in.full(b))
                                if b.follows(1):
                                    pe.wait_ge(dve_f.sem, dve_f.at("sT", b - 1))
                                transposed(pe, px, x2[b.slot]).then_inc(pe_f.step("x2T"), 1)
                                pe.wait_ge(act_t.sem, act_t.at("tT", b))
                            if inside(t, NG):
                                attend_project(pe, at, 1, c_in, pe_a, dve_a, act_a, t)
                            if inside(b, NG):
                                pe.wait_ge(dve_f.sem, dve_f.at("sT", b))
                                if b.follows(1):
                                    pe.wait_ge(dve_f.sem, dve_f.at("xl", b - 1))
                                for k in range(K):
                                    ins = pe.matmul(po[:, k * D:(k + 1) * D], sT[:, k * P:(k + 1) * P], W["fc_w"],
                                                    start=True, stop=True)
                                ins.then_inc(pe_f.step("fc"), 1)
                            if inside(t, NG):
                                attend_apply(pe, at, kv[1], pe_a, dve_a, act_a, t)

                        run(pe, NG, 1, body)

                    @block.scalar
                    def _(act):
                        def body(t):
                            b = t - 1
                            if inside(b, NG):
                                act.wait_ge(pe_y.sem, pe_y.at("yT", b))
                                if b.follows(1):
                                    act.wait_ge(dve_f.sem, dve_f.at("sT", b - 1))
                                act.activation(tT[:, :], at["pq"][:, :], ACT.Relu,
                                                          bias=C["lb2"], scale=C["lg2"]).then_inc(act_t.step("tT"), 1)
                            if inside(t, NG):
                                attend_act(act, at, act_a, pe_a, dve_a, t)
                                attend_roots(act, at, act_a, pe_a, dve_a, t)
                            if inside(b, NG):
                                act.wait_ge(dve_f.sem, dve_f.at("moments", b))
                                deviation(act, x_norm).then_inc(act_f.step("dev"), 1)
                                act.wait_ge(dve_f.sem, dve_f.at("z_moments", b))
                                deviation(act, z_norm).then_inc(act_f.step("z_dev"), 1)

                        run(act, NG, 1, body)

                    @block.gpsimd
                    def _(pool):
                        def body(t):
                            pool.wait_ge(x_in.sems[t.slot], x_in.full(t))
                            if t.follows(1):
                                pool.wait_ge(dve_f.sem, dve_f.at("xl", t - 1))
                            pool.tensor_tensor(xb[:, :, :], x[t.slot][:, :, :], R["fc_b"], ALU.add).then_inc(pool_f.step("xb"), 1)
                            pool.wait_ge(dve_f.sem, dve_f.at("xl", t))
                            if t.follows(1):
                                pool.wait_ge(dve_f.sem, dve_f.at("o", t - 1))
                            pool.tensor_tensor(xlb[:, :, :], xl[t.slot][:, :, :], R["beta"], ALU.add).then_inc(pool_f.step("xlb"), 1)

                        run(pool, NG, 0, body)

                    @block.vector
                    def _(dve):
                        def start(b):
                            dve.wait_ge(act_t.sem, act_t.at("tT", b))
                            dve.wait_ge(pe_f.sem, pe_f.at("x2T", b))
                            if b.follows(1):
                                dve.wait_ge(pe_f.sem, pe_f.at("fc", b - 1))
                            dve.tensor_tensor(sT[:, :], tT[:, :], px[:, :], ALU.add).then_inc(dve_f.step("sT"), 1)

                        def residual(b):
                            s = b.slot
                            dve.wait_ge(pe_f.sem, pe_f.at("fc", b))
                            dve.wait_ge(pool_f.sem, pool_f.at("xb", b))
                            if b.follows(2):
                                dve.wait_ge(xl_out.sems[(b - 2).slot], xl_out.full(b - 2))
                            if b.follows(2):
                                dve.wait_ge(pool_f.sem, pool_f.at("xlb", b - 2))
                            dve.tensor_tensor(xl[s][:, :, :], by_k(po[:, :]), xb[:, :, :], ALU.add).then_inc(dve_f.step("xl"), 1)
                            dve.wait_ge(dve_f.sem, dve_f.at("xl", b))
                            moments_of(dve, dve_f, b, xl[s], x_norm, ("stats", "moments"))

                        def final(b):
                            s = b.slot
                            dve.wait_ge(act_f.sem, act_f.at("dev", b))
                            inverted(dve, x_norm).then_inc(dve_f.step("rstd"), 1)
                            dve.wait_ge(dve_f.sem, dve_f.at("rstd", b))
                            normalize(dve, h, xl[s], x_norm).then_inc(dve_f.step("h"), 1)
                            dve.wait_ge(dve_f.sem, dve_f.at("h", b))
                            dve.scalar_tensor_tensor(z[:, :, :], h[:, :, :], 0.0, R["bo"], ALU.max,
                                                                ALU.add).then_inc(dve_f.step("z"), 1)
                            dve.wait_ge(dve_f.sem, dve_f.at("z", b))
                            moments_of(dve, dve_f, b, z, z_norm, ("z_stats", "z_moments"))
                            dve.wait_ge(act_f.sem, act_f.at("z_dev", b))
                            inverted(dve, z_norm).then_inc(dve_f.step("z_rstd"), 1)
                            dve.wait_ge(dve_f.sem, dve_f.at("z_rstd", b))
                            normalize(dve, zn, z, z_norm).then_inc(dve_f.step("zn"), 1)
                            dve.wait_ge(dve_f.sem, dve_f.at("zn", b))
                            dve.tensor_tensor(zg[:, :, :], zn[:, :, :], R["gamma"], ALU.mult).then_inc(dve_f.step("zg"), 1)
                            dve.wait_ge(dve_f.sem, dve_f.at("zg", b))
                            dve.wait_ge(pool_f.sem, pool_f.at("xlb", b))
                            if b.follows(2):
                                dve.wait_ge(o_out.sems[(b - 2).slot], o_out.full(b - 2))
                            dve.tensor_tensor(o[s][:, :, :], zg[:, :, :], xlb[:, :, :], ALU.add).then_inc(dve_f.step("o"), 1)

                        def body(t):
                            b = t - 1
                            if inside(t, NG):
                                attend_guard(dve, at, dve_a, pe_a, act_a, t)
                            if inside(b, NG):
                                start(b)
                            if inside(t, NG):
                                attend_mix(dve, at, dve_a, pe_a, act_a, t)
                            if inside(b, NG):
                                residual(b)
                            if inside(t, NG):
                                attend_normalize(dve, at, dve_a, pe_y, act_a, t)
                            if inside(b, NG):
                                final(b)

                        run(dve, NG, 1, body)

        def first_rows():
            ph = Phase("own")
            with ph.ctx:
                index, scale = ph.sb("index", [P, 6 * K], I32), ph.sb("scale", [P, 2 * K])
                g = ph.sb("g", [P, K, D])
                start = ph.sb("start", [P, K, 2, D])
                rec_in, stores = ph.dmas("rec_in", 2), ph.dmas("stores", 2)
                fetched = ph.dmas("fetched", K)
                go, blank = ph.sem("go"), ph.sem("blank")
                own = ph.steps("own", "own")

                with nc.Block() as block:
                    @block.sync
                    def _(sp):
                        def body(t):
                            s = t.slot
                            if inside(t, EG):
                                if t.follows(2):
                                    sp.wait_ge(own.sem, own.at("own", t - 2))
                                sp.dma_start(index[s][:, :], block_of(index_rec, t)).then_inc(rec_in.sems[t.slot], 16)
                                sp.dma_start(scale[s][:, :], block_of(scale_rec, t)).then_inc(rec_in.sems[t.slot], 16)
                            b = t - 1
                            if inside(b, EG):
                                sp.wait_ge(own.sem, own.at("own", b))
                                sp.dma_start(group(g0_e, b), flat(g[b.slot][:, :, :])).then_inc(stores.sems[b.slot], 16)
                                sp.dma_start(group(acc[0], b),
                                                          start[b.slot].rearrange("p k l d -> p (k l d)")).then_inc(stores.sems[b.slot], 16)

                        run(sp, EG, 1, body)
                        for t in (EG - 2, EG - 1):
                            sp.wait_ge(stores.sems[(Turn(None, t)).slot], stores.full(Turn(None, t)))

                    @block.gpsimd
                    def _(pool):
                        def body(t):
                            s = t.slot
                            pool.wait_ge(rec_in.sems[t.slot], rec_in.full(t))
                            if t.follows(2):
                                pool.wait_ge(stores.sems[(t - 2).slot], stores.full(t - 2))
                            for k in range(K):
                                indirect(pool, go, out=g[s][:, k, :], out_offset=None,
                                                       in_=g_rows[0][0:NP, :],
                                                       in_offset=rows_at(index[s][:, DST + k:DST + k + 1])).then_inc(fetched.sems[t.slot], 16)

                        run(pool, EG, 0, body)

                    @block.vector
                    def _(dve):
                        for s in range(2):
                            dve.memset(start[s][:, :, :, :], 0.0).then_inc(blank, 1)
                        dve.wait_ge(blank, 2)

                        def body(t):
                            s = t.slot
                            dve.wait_ge(rec_in.sems[t.slot], rec_in.full(t))
                            dve.wait_ge(fetched.sems[t.slot], fetched.full(t))
                            if t.follows(2):
                                dve.wait_ge(stores.sems[(t - 2).slot], stores.full(t - 2))
                            dve.tensor_tensor(start[s][:, :, 0, :], g[s][:, :, :],
                                                       over(scale[s][:, K:2 * K], D), ALU.mult).then_inc(own.step("own"), 1)

                        run(dve, EG, 0, body)

        def gather_messages(layer):
            ph = Phase(f"send{layer}")
            with ph.ctx:
                index, scale = ph.sb("index", [P, 6 * K], I32), ph.sb("scale", [P, 2 * K])
                dst_row = ph.sb("dst_row", [P, ROWS], I32)
                same = ph.sb("same", [P, K, P])
                g, m, total = ph.sb("g", [P, K, D]), ph.sb("m", [P, K, D]), ph.sb("total", [P, K, D])
                pm = [ph.bank(f"pm{i}") for i in range(2)]
                rec_in = ph.dmas("rec_in", 3)
                fetched = ph.dmas("fetched", K)
                added = [ph.sem(f"added{k}") for k in range(K)]
                go = ph.sem("go")
                made = ph.steps("made", "same", "m")
                summed, copied = ph.steps("summed", "sum"), ph.steps("copied", "total")
                sums = acc[layer].rearrange("e (l d) -> (e l) d", l=2)

                def added_wait(engine, t, ks=range(K)):
                    if t.known and t.number < 0:
                        return
                    for k in ks:
                        engine.wait_ge(added[k], 16 * t.number + 16)

                with nc.Block() as block:
                    @block.sync
                    def _(sp):
                        def body(t):
                            s = t.slot
                            if t.follows(2):
                                sp.wait_ge(made.sem, made.at("m", t - 2))
                            added_wait(sp, t - 2)
                            sp.dma_start(index[s][:, :], block_of(index_rec, t)).then_inc(rec_in.sems[t.slot], 16)
                            sp.dma_start(scale[s][:, :], block_of(scale_rec, t)).then_inc(rec_in.sems[t.slot], 16)
                            sp.dma_start(
                                dst_row[s][:, :],
                                a["dst"][bass.ds(t.number * ROWS, ROWS), :].rearrange("e o -> (e o)")
                                .partition_broadcast(P)).then_inc(rec_in.sems[t.slot], 16)

                        run(sp, EG, 0, body)

                    @block.gpsimd
                    def _(pool):
                        def body(t):
                            b = t - 1
                            if inside(t, EG):
                                pool.wait_ge(rec_in.sems[t.slot], rec_in.full(t))
                                if t.follows(2):
                                    pool.wait_ge(made.sem, made.at("m", t - 2))
                            if inside(b, EG):
                                pool.wait_ge(copied.sem, copied.at("total", b))
                            for k in range(K):
                                if inside(t, EG):
                                    indirect(
                                        pool, go, out=g[t.slot][:, k, :], out_offset=None, in_=g_rows[layer][0:NP, :],
                                        in_offset=rows_at(index[t.slot][:, SRC + k:SRC + k + 1])).then_inc(fetched.sems[t.slot], 16)
                                if inside(b, EG):
                                    added_wait(pool, b if k >= 2 else b - 1, [(k + 2) % K])
                                    indirect(pool, go, out=sums,
                                             out_offset=rows_at(index[b.slot][:, ADD_AT + k:ADD_AT + k + 1]),
                                             in_=total[b.slot][:, k, :], in_offset=None,
                                             compute_op=ALU.add).then_inc(added[k], 16)

                        run(pool, EG, 1, body)
                        added_wait(pool, Turn(None, EG - 1))

                    @block.vector
                    def _(dve):
                        def body(t):
                            s = t.slot
                            dve.wait_ge(rec_in.sems[t.slot], rec_in.full(t))
                            if t.follows(2):
                                dve.wait_ge(summed.sem, summed.at("sum", t - 2))
                            dve.tensor_tensor(
                                same[s][:, :, :], dst_row[s].rearrange("p (q k) -> p k q", k=K),
                                over(index[s][:, DST:DST + K], P), ALU.is_equal).then_inc(made.step("same"), 1)
                            dve.wait_ge(fetched.sems[t.slot], fetched.full(t))
                            dve.tensor_tensor(m[s][:, :, :], g[s][:, :, :],
                                                        over(scale[s][:, 0:K], D), ALU.mult).then_inc(made.step("m"), 1)

                        run(dve, EG, 0, body)

                    @block.tensor
                    def _(pe):
                        def body(t):
                            s = t.slot
                            pe.wait_ge(made.sem, made.at("m", t))
                            if t.follows(2):
                                pe.wait_ge(copied.sem, copied.at("total", t - 2))
                            for k in range(K):
                                ins = pe.matmul(pm[s][:, k * D:(k + 1) * D], same[s][:, k, :], m[s][:, k, :],
                                                start=True, stop=True)
                            ins.then_inc(summed.step("sum"), 1)

                        run(pe, EG, 0, body)

                    @block.scalar
                    def _(act):
                        def body(t):
                            s = t.slot
                            act.wait_ge(summed.sem, summed.at("sum", t))
                            added_wait(act, t - 2)
                            act.copy(flat(total[s][:, :, :]), pm[s][:, :]).then_inc(copied.step("total"), 1)

                        run(act, EG, 0, body)

        def update_nodes(layer):
            last = layer == LAYERS - 1
            ph = Phase(f"update{layer}")
            with ph.ctx:
                index, scale = ph.sb("index", [P, 6 * K], I32), ph.sb("scale", [P, 2 * K])
                parts, g0 = ph.sb("parts", [P, K, 2, D]), ph.sb("g0", [P, K, D])
                s0, s1 = ph.sb("s0", [P, K, D]), ph.sb("s1", [P, K, D])
                sT, uT = ph.sb("sT", [P, ROWS]), ph.sb("uT", [P, K, P])
                g = ph.sb("g", [P, K, D])
                start = ph.sb("start", [P, K, 2, D])
                ps, pc, pu = ([ph.bank(f"{n}{i}") for i in range(2)] for n in ("ps", "pc", "pu"))
                rec_in = ph.dmas("rec_in", 3)
                fetched, written, stores = ph.dmas("fetched", K), ph.dmas("written", K), ph.dmas("stores")
                go, blank = ph.sem("go"), ph.sem("blank")
                summed = ph.steps("summed", "s0", "s1")
                finished = ph.steps("finished", "g", "start")
                pe_s, pe_c, pe_u = ph.steps("pe_s", "sT"), ph.steps("pe_c", "c"), ph.steps("pe_u", "u")
                act_s, act_u = ph.steps("act_s", "sT"), ph.steps("act_u", "uT")

                with nc.Block() as block:
                    @block.sync
                    def _(sp):
                        def body(t):
                            s = t.slot
                            if inside(t, EG):
                                if t.follows(2):
                                    sp.wait_ge(finished.sem, finished.at("start", t - 2))
                                if t.follows(2):
                                    sp.wait_ge(written.sems[(t - 2).slot], written.full(t - 2))
                                sp.dma_start(index[s][:, :], block_of(index_rec, t)).then_inc(rec_in.sems[t.slot], 16)
                                sp.dma_start(scale[s][:, :], block_of(scale_rec, t)).then_inc(rec_in.sems[t.slot], 16)
                                sp.dma_start(flat(g0[s][:, :, :]), group(g0_e, t)).then_inc(rec_in.sems[t.slot], 16)
                            b = t - 1
                            if not last and inside(b, EG):
                                sp.wait_ge(finished.sem, finished.at("start", b))
                                sp.dma_start(group(acc[layer + 1], b),
                                                          start[b.slot].rearrange("p k l d -> p (k l d)")).then_inc(stores.sems[b.slot], 16)

                        run(sp, EG, 1, body)
                        if not last:
                            for t in (EG - 2, EG - 1):
                                sp.wait_ge(stores.sems[(Turn(None, t)).slot], stores.full(Turn(None, t)))

                    @block.gpsimd
                    def _(pool):
                        def body(t):
                            if inside(t, EG):
                                s = t.slot
                                pool.wait_ge(rec_in.sems[t.slot], rec_in.full(t))
                                if t.follows(2):
                                    pool.wait_ge(summed.sem, summed.at("s0", t - 2))
                                for k in range(K):
                                    indirect(
                                        pool, go, out=parts[s][:, k, :, :].rearrange("p l d -> p (l d)"),
                                        out_offset=None, in_=acc[layer],
                                        in_offset=rows_at(index[s][:, REP + k:REP + k + 1])).then_inc(fetched.sems[t.slot], 16)
                            b = t - 1
                            if inside(b, EG):
                                pool.wait_ge(finished.sem, finished.at("g", b))
                                if b.follows(1):
                                    pool.wait_ge(written.sems[(b - 1).slot], written.full(b - 1))
                                for k in range(K):
                                    indirect(
                                        pool, go, out=g_rows[layer + 1],
                                        out_offset=rows_at(index[b.slot][:, WRITE_AT + k:WRITE_AT + k + 1]),
                                        in_=g[b.slot][:, k, :], in_offset=None).then_inc(written.sems[b.slot], 16)

                        run(pool, EG, 1, body)
                        for t in (EG - 2, EG - 1):
                            pool.wait_ge(written.sems[(Turn(None, t)).slot], written.full(Turn(None, t)))

                    @block.vector
                    def _(dve):
                        for s in range(2):
                            dve.memset(start[s][:, :, :, :], 0.0).then_inc(blank, 1)
                        dve.wait_ge(blank, 2)

                        def body(t):
                            if inside(t, EG):
                                s = t.slot
                                dve.wait_ge(rec_in.sems[t.slot], rec_in.full(t))
                                dve.wait_ge(fetched.sems[t.slot], fetched.full(t))
                                dve.tensor_tensor(s0[s][:, :, :], parts[s][:, :, 0, :],
                                                              parts[s][:, :, 1, :], ALU.add).then_inc(summed.step("s0"), 1)
                                dve.wait_ge(summed.sem, summed.at("s0", t))
                                if t.follows(2):
                                    dve.wait_ge(pe_s.sem, pe_s.at("sT", t - 2))
                                dve.tensor_tensor(s1[s][:, :, :], s0[s][:, :, :],
                                                              over(scale[s][:, K:2 * K], D), ALU.mult).then_inc(summed.step("s1"), 1)
                            b = t - 1
                            if inside(b, EG):
                                s = b.slot
                                dve.wait_ge(pe_u.sem, pe_u.at("u", b))
                                if b.follows(2):
                                    dve.wait_ge(written.sems[(b - 2).slot], written.full(b - 2))
                                dve.tensor_tensor(g[s][:, :, :], by_k(pu[s][:, :]), g0[s][:, :, :],
                                                                ALU.add).then_inc(finished.step("g"), 1)
                                dve.wait_ge(finished.sem, finished.at("g", b))
                                if not last:
                                    if b.follows(2):
                                        dve.wait_ge(stores.sems[(b - 2).slot], stores.full(b - 2))
                                dve.tensor_tensor(start[s][:, :, 0, :], g[s][:, :, :],
                                                                over(scale[s][:, K:2 * K], D), ALU.mult).then_inc(finished.step("start"), 1)

                        run(dve, EG, 1, body)

                    @block.tensor
                    def _(pe):
                        def body(t):
                            s = t.slot
                            pe.wait_ge(summed.sem, summed.at("s1", t))
                            if t.follows(2):
                                pe.wait_ge(act_s.sem, act_s.at("sT", t - 2))
                            transposed(pe, ps[s], s1[s]).then_inc(pe_s.step("sT"), 1)
                            pe.wait_ge(act_s.sem, act_s.at("sT", t))
                            if t.follows(2):
                                pe.wait_ge(act_u.sem, act_u.at("uT", t - 2))
                            pe.matmul(pc[s][:, :], W[f"c{layer}"], sT[s][:, :], start=True, stop=True).then_inc(pe_c.step("c"), 1)
                            pe.wait_ge(act_u.sem, act_u.at("uT", t))
                            if t.follows(2):
                                pe.wait_ge(finished.sem, finished.at("g", t - 2))
                            transposed(pe, pu[s], uT[s]).then_inc(pe_u.step("u"), 1)

                        run(pe, EG, 0, body)

                    @block.scalar
                    def _(act):
                        def body(t):
                            s = t.slot
                            act.wait_ge(pe_s.sem, pe_s.at("sT", t))
                            if t.follows(2):
                                act.wait_ge(pe_c.sem, pe_c.at("c", t - 2))
                            act.copy(sT[s][:, :], ps[s][:, :]).then_inc(act_s.step("sT"), 1)
                            act.wait_ge(pe_c.sem, pe_c.at("c", t))
                            if t.follows(2):
                                act.wait_ge(pe_u.sem, pe_u.at("u", t - 2))
                            i = layer + 1
                            act.activation(flat(uT[s][:, :, :]), pc[s][:, :], ACT.Relu,
                                                      bias=bn_bias[:, i:i + 1], scale=bn_scale[:, i:i + 1]).then_inc(act_u.step("uT"), 1)

                        run(act, EG, 0, body)

        def edge_scores():
            ph = Phase("score")
            with ph.ctx:
                index = ph.sb("index", [P, 6 * K], I32)
                dst_row = ph.sb("dst_row", [P, ROWS], I32)
                attr = ph.sb("attr", [65, ROWS])
                dist, nodevec = ph.sb("dist", [2, ROWS]), ph.sb("nodevec", [2, ROWS])
                xs, xd = ph.sb("xs", [P, K, D]), ph.sb("xd", [P, K, D])
                s_norm, d_norm = norm_tiles(ph, "s"), norm_tiles(ph, "d")
                act_n = ph.steps("act_n", "s_dev", "d_dev")
                hs, hd, h = ph.one("hs", [P, K, D]), ph.one("hd", [P, K, D]), ph.sb("h", [P, K, D])
                hsT, hdT = ph.one("hsT", [P, ROWS]), ph.one("hdT", [P, ROWS])
                q, v = ph.one("q", [P, K, D]), ph.sb("v", [P, K, D])
                qk, dot = ph.one("qk", [P, K * HEADS, HEAD_DIM]), ph.one("dot", [P, K * HEADS])
                cT, dT = ph.one("cT", [33, ROWS]), ph.one("dT", [17, ROWS])
                neg, e0, e1, cons = (ph.one(n, [P, K * HEADS]) for n in ("neg", "e0", "e1", "cons"))
                sc0, sc1, score = (ph.one(n, [P, K * HEADS]) for n in ("sc0", "sc1", "score"))
                same, off = ph.one("same", [P, K, P]), ph.one("off", [P, K, P])
                masked = ph.sb("masked", [P, HEADS, P])
                top, less, w = (ph.one(n, [P, K * HEADS]) for n in ("top", "less", "w"))
                old, new = ph.one("old", [P, K, 2, HEADS]), ph.one("new", [P, K, 2, HEADS])
                drop, shrink = ph.one("drop", [P, 2, K, HEADS]), ph.one("shrink", [P, 2, K, HEADS])
                part = ph.one("part", [P, 2, K, HEADS])
                ph_t, pq, pk, pv = ph.bank("ph"), ph.bank("pq"), ph.bank("pk"), ph.bank("pv")
                psm = ph.bank("psm")
                pb = ph.bank("pb", 2)
                ph_m = ph.bank("pm")
                rec_in, fetched = ph.dmas("rec_in", 5), ph.dmas("fetched", 2 * K)
                stores = ph.dmas("stores", 3)
                old_in = [ph.sem(f"old_in{k}") for k in range(K)]
                new_out = [ph.sem(f"new_out{k}") for k in range(K)]
                go, blank = ph.sem("go"), ph.sem("blank")
                dve_h = ph.steps("dve_h", "s_stats", "s_moments", "d_stats", "d_moments", "s_rstd", "hs",
                                 "d_rstd", "hd", "h")
                dve_s = ph.steps("dve_s", "same", "off", "qk", "dot", "neg", "e1", "cons", "sc0", "sc1", "score",
                                 "masked0", "top0", "masked1", "top1", "masked2", "top2", "masked3", "top3",
                                 "less", "newtop", "drop", "part", "new")
                pe_h = ph.steps("pe_h", "hsT", "q", "hdT", "k", "v", "c", "d", "small", "b0", "b1", "b2", "b3",
                                "wsum")
                act_h = ph.steps("act_h", "hsT", "q", "hdT", "v", "cT", "dT", "e0", "w", "shrink")

                def lane_wait(engine, sems, t, k):
                    if not (t.known and t.number < 0):
                        engine.wait_ge(sems[k], 16 * t.number + 16)

                with nc.Block() as block:
                    @block.sync
                    def _(sp):
                        sp.wait_ge(blank, 2)

                        def body(t):
                            s = t.slot
                            if inside(t, EG):
                                if t.follows(2):
                                    sp.wait_ge(dve_s.sem, dve_s.at("same", t - 2))
                                if t.follows(2):
                                    sp.wait_ge(pe_h.sem, pe_h.at("small", t - 2))
                                for k in range(K):
                                    lane_wait(sp, new_out, t - 2, k)
                                sp.dma_start(index[s][:, :], block_of(index_rec, t)).then_inc(rec_in.sems[t.slot], 16)
                                sp.dma_start(
                                    dst_row[s][:, :],
                                    a["dst"][bass.ds(t.number * ROWS, ROWS), :].rearrange("e o -> (e o)")
                                    .partition_broadcast(P)).then_inc(rec_in.sems[t.slot], 16)
                                sp.dma_start(attr[s][:, :], block_of(a["attr"], t, 65)).then_inc(rec_in.sems[t.slot], 16)
                                sp.dma_start(dist[s][:, :], block_of(a["dist"], t, 2)).then_inc(rec_in.sems[t.slot], 16)
                                sp.dma_start(
                                    nodevec[s][0:1, :],
                                    nodevec_e[bass.ds(t.number * ROWS, ROWS), :].rearrange("(o e) u -> o (e u)", o=1)).then_inc(rec_in.sems[t.slot], 16)
                            b = t - 1
                            if inside(b, EG):
                                s = b.slot
                                sp.wait_ge(dve_h.sem, dve_h.at("h", b))
                                sp.dma_start(group(xl_e, b), flat(xd[s][:, :, :])).then_inc(stores.sems[b.slot], 16)
                                sp.dma_start(group(h_e, b), flat(h[s][:, :, :])).then_inc(stores.sems[b.slot], 16)
                                sp.wait_ge(act_h.sem, act_h.at("v", b))
                                sp.dma_start(group(v_e, b), flat(v[s][:, :, :])).then_inc(stores.sems[b.slot], 16)

                        run(sp, EG, 1, body)
                        for t in (EG - 2, EG - 1):
                            sp.wait_ge(stores.sems[(Turn(None, t)).slot], stores.full(Turn(None, t)))

                    @block.gpsimd
                    def _(pool):
                        def body(t):
                            if inside(t, EG):
                                s = t.slot
                                pool.wait_ge(rec_in.sems[t.slot], rec_in.full(t))
                                if t.follows(2):
                                    pool.wait_ge(dve_h.sem, dve_h.at("hs", t - 2))
                                if t.follows(2):
                                    pool.wait_ge(stores.sems[(t - 2).slot], stores.full(t - 2))
                            b = t - 1
                            for k in range(K):
                                if inside(t, EG):
                                    for tile, col in ((xs, SRC), (xd, DST)):
                                        indirect(
                                            pool, go, out=tile[t.slot][:, k, :], out_offset=None, in_=xl_rows,
                                            in_offset=rows_at(index[t.slot][:, col + k:col + k + 1])).then_inc(fetched.sems[t.slot], 16)
                            if inside(b, EG):
                                if b.follows(1):
                                    pool.wait_ge(dve_s.sem, dve_s.at("part", b - 1))
                                for k in range(K):
                                    lane_wait(pool, new_out, b - 1, k)
                                    at = rows_at(index[b.slot][:, SOFT_AT + k:SOFT_AT + k + 1])
                                    indirect(pool, go, out=old[:, k, :, :].rearrange("p t h -> p (t h)"),
                                             out_offset=None, in_=soft, in_offset=at).then_inc(old_in[k], 16)
                                pool.wait_ge(dve_s.sem, dve_s.at("new", b))
                                for k in range(K):
                                    at = rows_at(index[b.slot][:, SOFT_AT + k:SOFT_AT + k + 1])
                                    indirect(pool, go, out=soft, out_offset=at,
                                             in_=new[:, k, :, :].rearrange("p t h -> p (t h)"),
                                             in_offset=None).then_inc(new_out[k], 16)

                        run(pool, EG, 1, body)
                        for k in range(K):
                            lane_wait(pool, new_out, Turn(None, EG - 1), k)

                    @block.vector
                    def _(dve):
                        for s in range(2):
                            dve.memset(nodevec[s][:, :], 1.0).then_inc(blank, 1)

                        def norms(t):
                            s = t.slot
                            dve.wait_ge(fetched.sems[t.slot], fetched.full(t))
                            moments_of(dve, dve_h, t, xs[s], s_norm, ("s_stats", "s_moments"))
                            moments_of(dve, dve_h, t, xd[s], d_norm, ("d_stats", "d_moments"))
                            dve.wait_ge(act_n.sem, act_n.at("s_dev", t))
                            inverted(dve, s_norm).then_inc(dve_h.step("s_rstd"), 1)
                            dve.wait_ge(dve_h.sem, dve_h.at("s_rstd", t))
                            if t.follows(1):
                                dve.wait_ge(pe_h.sem, pe_h.at("hsT", t - 1))
                            normalize(dve, hs, xs[s], s_norm).then_inc(dve_h.step("hs"), 1)
                            dve.wait_ge(act_n.sem, act_n.at("d_dev", t))
                            inverted(dve, d_norm).then_inc(dve_h.step("d_rstd"), 1)
                            dve.wait_ge(dve_h.sem, dve_h.at("d_rstd", t))
                            if t.follows(1):
                                dve.wait_ge(pe_h.sem, pe_h.at("hdT", t - 1))
                            normalize(dve, hd, xd[s], d_norm).then_inc(dve_h.step("hd"), 1)
                            dve.wait_ge(dve_h.sem, dve_h.at("hd", t))
                            if t.follows(2):
                                dve.wait_ge(stores.sems[(t - 2).slot], stores.full(t - 2))
                            dve.tensor_scalar(h[s][:, :, :], hd[:, :, :], 0.0, None, ALU.max).then_inc(dve_h.step("h"), 1)

                        def scores(t):
                            s = t.slot
                            dve.wait_ge(rec_in.sems[t.slot], rec_in.full(t))
                            if t.follows(1):
                                dve.wait_ge(pe_h.sem, pe_h.at("wsum", t - 1))
                            dve.tensor_tensor(
                                same[:, :, :], dst_row[s].rearrange("p (q k) -> p k q", k=K),
                                over(index[s][:, DST:DST + K], P), ALU.is_equal).then_inc(dve_s.step("same"), 1)
                            dve.wait_ge(dve_s.sem, dve_s.at("same", t))
                            dve.tensor_scalar(off[:, :, :], same[:, :, :], -1.0, -LOWEST, ALU.add,
                                                         ALU.mult).then_inc(dve_s.step("off"), 1)
                            dve.wait_ge(act_h.sem, act_h.at("q", t))
                            dve.wait_ge(pe_h.sem, pe_h.at("k", t))
                            dve.tensor_tensor(qk.rearrange("p m d -> p (m d)"), flat(q[:, :, :]),
                                                         pk[:, :], ALU.mult).then_inc(dve_s.step("qk"), 1)
                            dve.wait_ge(dve_s.sem, dve_s.at("qk", t))
                            dve.tensor_reduce(dot[:, :], qk[:, :, :], AX_X, ALU.add).then_inc(dve_s.step("dot"), 1)
                            dve.wait_ge(pe_h.sem, pe_h.at("small", t))
                            if t.follows(1):
                                dve.wait_ge(act_h.sem, act_h.at("e0", t - 1))
                            dve.tensor_scalar(neg[:, :], psm[:, 32:64], -1.0, EXP_MAX, ALU.mult,
                                                         ALU.min).then_inc(dve_s.step("neg"), 1)
                            dve.wait_ge(act_h.sem, act_h.at("e0", t))
                            dve.tensor_scalar(e1[:, :], e0[:, :], 1.0, None, ALU.add).then_inc(dve_s.step("e1"), 1)
                            dve.wait_ge(dve_s.sem, dve_s.at("e1", t))
                            dve.reciprocal(cons[:, :], e1[:, :]).then_inc(dve_s.step("cons"), 1)
                            dve.wait_ge(pe_h.sem, pe_h.at("small", t))
                            dve.scalar_tensor_tensor(sc0[:, :], dot[:, :], HEAD_DIM ** -0.5,
                                                                psm[:, 0:32], ALU.mult, ALU.add).then_inc(dve_s.step("sc0"), 1)
                            dve.wait_ge(dve_s.sem, dve_s.at("sc0", t))
                            dve.tensor_tensor(sc1[:, :], sc0[:, :], cons[:, :], ALU.mult).then_inc(dve_s.step("sc1"), 1)
                            dve.wait_ge(dve_s.sem, dve_s.at("sc1", t))
                            if t.follows(1):
                                dve.wait_ge(pe_h.sem, pe_h.at("b3", t - 1))
                            dve.tensor_tensor(score[:, :], sc1[:, :], psm[:, 64:96], ALU.add).then_inc(dve_s.step("score"), 1)
                            for k in range(K):
                                if k >= 2:
                                    dve.wait_ge(dve_s.sem, dve_s.at(f"top{k - 2}", t))
                                dve.wait_ge(pe_h.sem, pe_h.at(f"b{k}", t))
                                dve.tensor_tensor(
                                    masked[k % 2][:, :, :], pb[:, :].rearrange("p (h q) -> p h q", h=HEADS),
                                    off[:, k, :].unsqueeze(1).to_broadcast([P, HEADS, P]), ALU.add).then_inc(dve_s.step(f"masked{k}"), 1)
                                dve.wait_ge(dve_s.sem, dve_s.at(f"masked{k}", t))
                                dve.tensor_reduce(top[:, k * HEADS:(k + 1) * HEADS], masked[k % 2][:, :, :],
                                                             AX_X, ALU.max).then_inc(dve_s.step(f"top{k}"), 1)
                            dve.wait_ge(dve_s.sem, dve_s.at("top3", t))
                            dve.tensor_tensor(less[:, :], score[:, :], top[:, :], ALU.subtract).then_inc(dve_s.step("less"), 1)
                            for k in range(K):
                                lane_wait(dve, old_in, t, k)
                                lane_wait(dve, new_out, t - 1, k)
                            tops = top[:, :].rearrange("p (k h) -> p k h", k=K)
                            dve.tensor_tensor(new[:, :, 0, :], old[:, :, 0, :], tops, ALU.max).then_inc(dve_s.step("newtop"), 1)
                            dve.wait_ge(dve_s.sem, dve_s.at("newtop", t))
                            dve.tensor_tensor(drop[:, 0, :, :], old[:, :, 0, :], new[:, :, 0, :], ALU.subtract)
                            dve.tensor_tensor(drop[:, 1, :, :], tops, new[:, :, 0, :], ALU.subtract).then_inc(dve_s.step("drop"), 1)
                            dve.wait_ge(act_h.sem, act_h.at("shrink", t))
                            dve.wait_ge(pe_h.sem, pe_h.at("wsum", t))
                            dve.tensor_tensor(part[:, 0, :, :], old[:, :, 1, :], shrink[:, 0, :, :], ALU.mult)
                            dve.tensor_tensor(
                                part[:, 1, :, :], psm[:, 96:128].rearrange("p (k h) -> p k h", k=K),
                                shrink[:, 1, :, :], ALU.mult).then_inc(dve_s.step("part"), 1)
                            dve.wait_ge(dve_s.sem, dve_s.at("part", t))
                            dve.tensor_tensor(new[:, :, 1, :], part[:, 0, :, :], part[:, 1, :, :],
                                                         ALU.add).then_inc(dve_s.step("new"), 1)

                        def body(t):
                            if inside(t, EG):
                                norms(t)
                            if inside(t - 1, EG):
                                scores(t - 1)

                        run(dve, EG, 1, body)

                    @block.scalar
                    def _(act):
                        def body(t):
                            b = t - 1
                            if inside(t, EG):
                                act.wait_ge(dve_h.sem, dve_h.at("s_moments", t))
                                deviation(act, s_norm).then_inc(act_n.step("s_dev"), 1)
                                act.wait_ge(dve_h.sem, dve_h.at("d_moments", t))
                                deviation(act, d_norm).then_inc(act_n.step("d_dev"), 1)
                            if inside(b, EG):
                                s = b.slot
                                act.wait_ge(pe_h.sem, pe_h.at("hsT", b))
                                act.activation(hsT[:, :], ph_t[:, :], ACT.Relu).then_inc(act_h.step("hsT"), 1)
                                act.wait_ge(pe_h.sem, pe_h.at("q", b))
                                if b.follows(1):
                                    act.wait_ge(dve_s.sem, dve_s.at("qk", b - 1))
                                act.copy(flat(q[:, :, :]), pq[:, :]).then_inc(act_h.step("q"), 1)
                                act.wait_ge(pe_h.sem, pe_h.at("hdT", b))
                                act.activation(hdT[:, :], ph_t[:, :], ACT.Relu).then_inc(act_h.step("hdT"), 1)
                                act.wait_ge(pe_h.sem, pe_h.at("v", b))
                                if b.follows(2):
                                    act.wait_ge(stores.sems[(b - 2).slot], stores.full(b - 2))
                                act.copy(flat(v[s][:, :, :]), pv[:, :]).then_inc(act_h.step("v"), 1)
                                act.wait_ge(pe_h.sem, pe_h.at("c", b))
                                act.activation(cT[:, :], pq[0:33, :], ACT.Relu).then_inc(act_h.step("cT"), 1)
                                act.wait_ge(pe_h.sem, pe_h.at("d", b))
                                act.activation(dT[:, :], ph_t[0:17, :], ACT.Relu).then_inc(act_h.step("dT"), 1)
                                act.wait_ge(dve_s.sem, dve_s.at("neg", b))
                                if b.follows(1):
                                    act.wait_ge(dve_s.sem, dve_s.at("e1", b - 1))
                                act.activation(e0[:, :], neg[:, :], ACT.Exp).then_inc(act_h.step("e0"), 1)
                                act.wait_ge(dve_s.sem, dve_s.at("less", b))
                                act.activation(w[:, :], less[:, :], ACT.Exp).then_inc(act_h.step("w"), 1)
                                act.wait_ge(dve_s.sem, dve_s.at("drop", b))
                                act.activation(shrink[:, :, :, :], drop[:, :, :, :], ACT.Exp).then_inc(act_h.step("shrink"), 1)

                        run(act, EG, 1, body)

                    @block.tensor
                    def _(pe):
                        def biased(bank, left, w, bias):
                            pe.matmul(bank[:, :], ones[0:1, :], flat(R[bias])[0:1, :], start=True, stop=False,
                                      skip_group_check=True)
                            for k in range(K):
                                ins = pe.matmul(bank[:, k * D:(k + 1) * D], left[:, k * P:(k + 1) * P], W[w],
                                                start=False, stop=True, skip_group_check=True)
                            return ins

                        def body(t):
                            b = t - 1
                            if inside(b, EG):
                                s = b.slot
                                pe.wait_ge(dve_h.sem, dve_h.at("hs", b))
                                if b.follows(1):
                                    pe.wait_ge(act_h.sem, act_h.at("dT", b - 1))
                                transposed(pe, ph_t, hs).then_inc(pe_h.step("hsT"), 1)
                                pe.wait_ge(act_h.sem, act_h.at("hsT", b))
                                if b.follows(1):
                                    pe.wait_ge(act_h.sem, act_h.at("cT", b - 1))
                                biased(pq, hsT, "l1_q", "bq").then_inc(pe_h.step("q"), 1)
                                pe.wait_ge(dve_h.sem, dve_h.at("hd", b))
                                transposed(pe, ph_t, hd).then_inc(pe_h.step("hdT"), 1)
                                pe.wait_ge(act_h.sem, act_h.at("hdT", b))
                                if b.follows(1):
                                    pe.wait_ge(dve_s.sem, dve_s.at("qk", b - 1))
                                biased(pk, hdT, "l1_k", "bk").then_inc(pe_h.step("k"), 1)
                                if b.follows(1):
                                    pe.wait_ge(act_h.sem, act_h.at("v", b - 1))
                                biased(pv, hdT, "l1_v", "bv").then_inc(pe_h.step("v"), 1)
                                pe.wait_ge(act_h.sem, act_h.at("q", b))
                                pe.wait_ge(rec_in.sems[b.slot], rec_in.full(b))
                                pe.matmul(pq[0:33, :], c1w[:, :], nodevec[s][:, :], start=True, stop=True).then_inc(pe_h.step("c"), 1)
                                pe.matmul(ph_t[0:17, :], d1w[:, :], dist[s][:, :], start=True, stop=True).then_inc(pe_h.step("d"), 1)
                                if b.follows(1):
                                    pe.wait_ge(dve_s.sem, dve_s.at("score", b - 1))
                                if b.follows(1):
                                    pe.wait_ge(dve_s.sem, dve_s.at("part", b - 1))
                                pe.wait_ge(act_h.sem, act_h.at("dT", b))
                                for k in range(K):
                                    h8 = slice(k * HEADS, (k + 1) * HEADS)
                                    pe.matmul(psm[:, 0:32][:, h8], attr[s].rearrange("c (q k) -> c k q", k=K)[:, k, :],
                                              ew[:, :], start=True, stop=True)
                                    pe.matmul(psm[:, 32:64][:, h8], cT.rearrange("c (q k) -> c k q", k=K)[:, k, :],
                                              c2w[:, :], start=True, stop=True)
                                    ins = pe.matmul(psm[:, 64:96][:, h8], dT.rearrange("c (q k) -> c k q", k=K)[:, k, :],
                                                    d2w[:, :], start=True, stop=True)
                                ins.then_inc(pe_h.step("small"), 1)
                                pe.wait_ge(dve_s.sem, dve_s.at("score", b))
                                for k in range(K):
                                    if k:
                                        pe.wait_ge(dve_s.sem, dve_s.at(f"masked{k - 1}", b))
                                    for h in range(HEADS):
                                        at = k * HEADS + h
                                        ins = pe.transpose(pb[:, h * P:(h + 1) * P],
                                                           score[:, at:at + 1].to_broadcast([P, P]), ident[:, :])
                                    ins.then_inc(pe_h.step(f"b{k}"), 1)
                                pe.wait_ge(act_h.sem, act_h.at("w", b))
                                for k in range(K):
                                    ins = pe.matmul(psm[:, 96 + k * HEADS:96 + (k + 1) * HEADS], same[:, k, :],
                                                    w[:, k * HEADS:(k + 1) * HEADS], start=True, stop=True)
                                ins.then_inc(pe_h.step("wsum"), 1)

                        run(pe, EG, 1, body)

        def edge_output():
            ph = Phase("final")
            with ph.ctx:
                index = ph.sb("index", [P, 6 * K], I32)
                lanes = ph.sb("lanes", [P, K, K, 2, HEADS])
                v, h, x = ph.sb("v", [P, K, D]), ph.sb("h", [P, K, D]), ph.sb("x", [P, K, D])
                top, drop, shrink = (ph.one("top", [P, K, HEADS]), ph.one("drop", [P, K, K, HEADS]),
                                     ph.one("shrink", [P, K, K, HEADS]))
                part, total, inverse = (ph.one("part", [P, K, K, HEADS]), ph.one("total", [P, K, HEADS]),
                                        ph.one("inverse", [P, K, HEADS]))
                weight, agg, aT = (ph.one("weight", [P, K, HEADS]), ph.sb("agg", [P, K, D]),
                                   ph.sb("aT", [P, ROWS]))
                z, zn, zg, zb = (ph.one(n, [P, K, D]) for n in ("z", "zn", "zg", "zb"))
                o = ph.sb("o", [P, K, D])
                z_norm, act_z = norm_tiles(ph, "z"), ph.steps("act_z", "dev")
                pa, po = [ph.bank(f"pa{i}") for i in range(2)], [ph.bank(f"po{i}") for i in range(2)]
                rec_in, fetched, written = ph.dmas("rec_in", 4), ph.dmas("fetched", K), ph.dmas("written", K)
                go = ph.sem("go")
                dve_w = ph.steps("dve_w", "top", "drop", "part", "total", "inverse", "weight", "agg")
                dve_o = ph.steps("dve_o", "z", "stats", "moments", "rstd", "zn", "zg", "zb", "o")
                act_e, act_a = ph.steps("act_e", "shrink"), ph.steps("act_a", "aT")
                pe_a, pe_o = ph.steps("pe_a", "aT"), ph.steps("pe_o", "o")

                with nc.Block() as block:
                    @block.sync
                    def _(sp):
                        def body(t):
                            s = t.slot
                            if t.follows(2):
                                sp.wait_ge(dve_o.sem, dve_o.at("o", t - 2))
                            if t.follows(2):
                                sp.wait_ge(written.sems[(t - 2).slot], written.full(t - 2))
                            sp.dma_start(index[s][:, :], block_of(index_rec, t)).then_inc(rec_in.sems[t.slot], 16)
                            for tile, table in ((v, v_e), (h, h_e), (x, xl_e)):
                                sp.dma_start(flat(tile[s][:, :, :]), group(table, t)).then_inc(rec_in.sems[t.slot], 16)

                        run(sp, EG, 0, body)

                    @block.gpsimd
                    def _(pool):
                        def body(t):
                            if inside(t, EG):
                                s = t.slot
                                pool.wait_ge(rec_in.sems[t.slot], rec_in.full(t))
                                if t.follows(2):
                                    pool.wait_ge(dve_w.sem, dve_w.at("part", t - 2))
                                for k in range(K):
                                    indirect(
                                        pool, go, out=lanes[s][:, k, :, :, :].rearrange("p l t h -> p (l t h)"),
                                        out_offset=None,
                                        in_=soft[0:EP * K, :].rearrange("(e l) c -> e (l c)", l=K),
                                        in_offset=rows_at(index[s][:, REP + k:REP + k + 1])).then_inc(fetched.sems[t.slot], 16)
                            b = t - 1
                            if inside(b, EG):
                                pool.wait_ge(dve_o.sem, dve_o.at("o", b))
                                if b.follows(1):
                                    pool.wait_ge(written.sems[(b - 1).slot], written.full(b - 1))
                                for k in range(K):
                                    indirect(
                                        pool, go, out=out,
                                        out_offset=rows_at(index[b.slot][:, WRITE_AT + k:WRITE_AT + k + 1]),
                                        in_=o[b.slot][:, k, :], in_offset=None).then_inc(written.sems[b.slot], 16)

                        run(pool, EG, 1, body)
                        for t in (EG - 2, EG - 1):
                            pool.wait_ge(written.sems[(Turn(None, t)).slot], written.full(Turn(None, t)))

                    @block.vector
                    def _(dve):
                        def weigh(t):
                            s = t.slot
                            dve.wait_ge(rec_in.sems[t.slot], rec_in.full(t))
                            dve.wait_ge(fetched.sems[t.slot], fetched.full(t))
                            tops = lanes[s][:, :, :, 0, :]
                            dve.tensor_reduce(top[:, :, :], tops.rearrange("p k l h -> p k h l"), AX_X,
                                                         ALU.max).then_inc(dve_w.step("top"), 1)
                            dve.wait_ge(dve_w.sem, dve_w.at("top", t))
                            if t.follows(1):
                                dve.wait_ge(act_e.sem, act_e.at("shrink", t - 1))
                            for k in range(K):
                                ins = dve.tensor_tensor(
                                    drop[:, k, :, :], lanes[s][:, k, :, 0, :],
                                    top[:, k, :].unsqueeze(1).to_broadcast([P, K, HEADS]), ALU.subtract)
                            ins.then_inc(dve_w.step("drop"), 1)
                            dve.wait_ge(act_e.sem, act_e.at("shrink", t))
                            dve.tensor_tensor(part[:, :, :, :], lanes[s][:, :, :, 1, :],
                                                         shrink[:, :, :, :], ALU.mult).then_inc(dve_w.step("part"), 1)
                            dve.wait_ge(dve_w.sem, dve_w.at("part", t))
                            dve.tensor_reduce(total[:, :, :], part[:, :, :, :].rearrange("p k l h -> p k h l"),
                                                         AX_X, ALU.add).then_inc(dve_w.step("total"), 1)
                            dve.wait_ge(dve_w.sem, dve_w.at("total", t))
                            dve.reciprocal(inverse[:, :, :], total[:, :, :]).then_inc(dve_w.step("inverse"), 1)
                            dve.wait_ge(dve_w.sem, dve_w.at("inverse", t))
                            dve.tensor_tensor(weight[:, :, :], total[:, :, :], inverse[:, :, :],
                                                         ALU.mult).then_inc(dve_w.step("weight"), 1)
                            dve.wait_ge(dve_w.sem, dve_w.at("weight", t))
                            if t.follows(2):
                                dve.wait_ge(pe_a.sem, pe_a.at("aT", t - 2))
                            dve.tensor_tensor(
                                agg[s].rearrange("p k (h e) -> p (k h) e", h=HEADS),
                                v[s].rearrange("p k (h e) -> p (k h) e", h=HEADS),
                                over(weight.rearrange("p k h -> p (k h)"), HEAD_DIM), ALU.mult).then_inc(dve_w.step("agg"), 1)

                        def finish(t):
                            s = t.slot
                            dve.wait_ge(pe_o.sem, pe_o.at("o", t))
                            dve.tensor_tensor(z[:, :, :], by_k(po[s][:, :]), h[s][:, :, :], ALU.add).then_inc(dve_o.step("z"), 1)
                            dve.wait_ge(dve_o.sem, dve_o.at("z", t))
                            moments_of(dve, dve_o, t, z, z_norm, ("stats", "moments"))
                            dve.wait_ge(act_z.sem, act_z.at("dev", t))
                            inverted(dve, z_norm).then_inc(dve_o.step("rstd"), 1)
                            dve.wait_ge(dve_o.sem, dve_o.at("rstd", t))
                            normalize(dve, zn, z, z_norm).then_inc(dve_o.step("zn"), 1)
                            dve.wait_ge(dve_o.sem, dve_o.at("zn", t))
                            dve.tensor_tensor(zg[:, :, :], zn[:, :, :], R["gamma"], ALU.mult).then_inc(dve_o.step("zg"), 1)
                            dve.wait_ge(dve_o.sem, dve_o.at("zg", t))
                            dve.tensor_tensor(zb[:, :, :], zg[:, :, :], R["beta"], ALU.add).then_inc(dve_o.step("zb"), 1)
                            dve.wait_ge(dve_o.sem, dve_o.at("zb", t))
                            if t.follows(2):
                                dve.wait_ge(written.sems[(t - 2).slot], written.full(t - 2))
                            dve.tensor_tensor(o[s][:, :, :], zb[:, :, :], x[s][:, :, :], ALU.add).then_inc(dve_o.step("o"), 1)

                        def body(t):
                            if inside(t, EG):
                                weigh(t)
                            if inside(t - 1, EG):
                                finish(t - 1)

                        run(dve, EG, 1, body)

                    @block.scalar
                    def _(act):
                        def body(t):
                            if inside(t, EG):
                                act.wait_ge(dve_w.sem, dve_w.at("drop", t))
                                if t.follows(1):
                                    act.wait_ge(dve_w.sem, dve_w.at("part", t - 1))
                                act.activation(shrink[:, :, :, :], drop[:, :, :, :], ACT.Exp).then_inc(act_e.step("shrink"), 1)
                                act.wait_ge(pe_a.sem, pe_a.at("aT", t))
                                if t.follows(2):
                                    act.wait_ge(pe_o.sem, pe_o.at("o", t - 2))
                                act.copy(aT[t.slot][:, :], pa[t.slot][:, :]).then_inc(act_a.step("aT"), 1)
                            b = t - 1
                            if inside(b, EG):
                                act.wait_ge(dve_o.sem, dve_o.at("moments", b))
                                deviation(act, z_norm).then_inc(act_z.step("dev"), 1)

                        run(act, EG, 1, body)

                    @block.tensor
                    def _(pe):
                        def body(t):
                            s = t.slot
                            pe.wait_ge(dve_w.sem, dve_w.at("agg", t))
                            if t.follows(2):
                                pe.wait_ge(act_a.sem, act_a.at("aT", t - 2))
                            transposed(pe, pa[s], agg[s]).then_inc(pe_a.step("aT"), 1)
                            if t.follows(2):
                                pe.wait_ge(dve_o.sem, dve_o.at("z", t - 2))
                            pe.wait_ge(act_a.sem, act_a.at("aT", t))
                            pe.matmul(po[s][:, :], ones[0:1, :], flat(R["bo"])[0:1, :], start=True, stop=False,
                                      skip_group_check=True)
                            for k in range(K):
                                ins = pe.matmul(po[s][:, k * D:(k + 1) * D], aT[s][:, k * P:(k + 1) * P], W["l1_o"],
                                                start=False, stop=True, skip_group_check=True)
                            ins.then_inc(pe_o.step("o"), 1)

                        run(pe, EG, 0, body)

        index_edges()
        dense_first()
        first_rows()
        for layer in range(LAYERS):
            gather_messages(layer)
            update_nodes(layer)
        dense_second()
        dense_third()
        edge_scores()
        edge_output()


def kernel(**inputs):
    import numpy as np
    import concourse.bacc as bacc
    from concourse.bass_utils import run_bass_kernel_spmd

    def arr(name):
        return np.ascontiguousarray(inputs[name])

    n_nodes, n_edges = inputs["x"].shape[0], inputs["src"].shape[0]
    NG = -(-n_nodes // (2 * ROWS)) * 2
    EG = -(-n_edges // (2 * ROWS)) * 2
    NP, EP, SPARE = NG * ROWS, EG * ROWS, ROWS
    assert n_nodes < NP

    def padded(rows, n, fill=0):
        out = np.full((n, *rows.shape[1:]), fill, rows.dtype)
        out[:rows.shape[0]] = rows
        return out

    def groups_T(rows):
        c = rows.shape[1]
        out = np.ones((EG, c + 1, ROWS), np.float32)
        out[:, :c] = padded(rows, EP).reshape(EG, ROWS, c).transpose(0, 2, 1)
        return out.reshape(EG * (c + 1), ROWS)

    def with_one(w, b):
        c = w.shape[1]
        out = np.zeros((2, c + 1), np.float32)
        out[0, :c], out[1, :c], out[1, c] = w[0], b, 1
        return out

    def stacked(w, b):
        return np.concatenate([w, b[None]], 0)

    conv, qkv = arr("L0_gnn_conv_w"), arr("L0_gnn_qkv_w")
    bng, bnb, lng, lnb = (arr("L0_gnn_" + n) for n in ("bn_g", "bn_b", "t_ln_g", "t_ln_b"))
    conv_b = arr("L0_gnn_conv_b")
    columns = [arr("L0_gnn_g_fc_b"), conv_b[0], conv_b[1], conv_b[2], *bng, *bnb, *lng, *lnb]
    k = np.arange(K, dtype=np.float32)[None]
    p = np.arange(P, dtype=np.float32)[:, None]
    spare = k * P + p
    data = {
        "x": padded(arr("x"), NP),
        "node_vec": padded(arr("node_vec1"), NP + SPARE),
        "src": padded(arr("src").reshape(-1, 1), EP, n_nodes),
        "dst": padded(arr("dst").reshape(-1, 1), EP, n_nodes),
        "attr": groups_T(arr("edge_attr_64")),
        "dist": groups_T(arr("edge_weight1")),
        "edge_no": np.arange(1, EP + 1, dtype=np.float32)[:, None],
        "t_w": arr("L0_gnn_t_fc_w"), "g_w": arr("L0_gnn_g_fc_w"), "fc_w": arr("L0_gnn_fc_w"),
        "wq0": qkv[0, 0], "wk0": qkv[0, 1], "wv0": qkv[0, 2],
        "wq1": qkv[1, 0], "wk1": qkv[1, 1], "wv1": qkv[1, 2],
        "c0": conv[0], "c1": conv[1], "c2": conv[2],
        "l1_q": arr("L1_gnn_Wq"), "l1_k": arr("L1_gnn_Wk"), "l1_v": arr("L1_gnn_Wv"), "l1_o": arr("L1_gnn_Wo"),
        "t_b": arr("L0_gnn_t_fc_b"), "fc_b": arr("L0_gnn_fc_b"), "bq": arr("L1_gnn_bq"), "bk": arr("L1_gnn_bk"),
        "bv": arr("L1_gnn_bv"), "bo": arr("L1_gnn_bo"), "gamma": arr("L1_gnn_gamma"), "beta": arr("L1_gnn_beta"),
        "cols": np.stack(columns, 1),
        "c1w": with_one(arr("L1_gnn_Wc1"), arr("L1_gnn_bc1")), "c2w": stacked(arr("L1_gnn_Wc2"), arr("L1_gnn_bc2")),
        "d1w": with_one(arr("L1_gnn_Wd1"), arr("L1_gnn_bd1")), "d2w": stacked(arr("L1_gnn_Wd2"), arr("L1_gnn_bd2")),
        "ew": stacked(arr("L1_gnn_We"), arr("L1_gnn_be")),
        "ident": np.eye(P, dtype=np.float32),
        "before": np.tril(np.ones((P, P), np.float32), -1),
        "spare_node": NP + spare,
        "lane": np.concatenate([k + 0 * p, k % 2 - spare - 2 * EP, k - spare - K * EP, spare], 1),
    }
    nc = bacc.Bacc("TRN2", target_bir_lowering=False, num_devices=1)
    arrays, args = {}, {"n_nodes": n_nodes}
    for name, value in data.items():
        value = np.ascontiguousarray(value)
        arrays[f"in_{name}"] = value
        args[name] = nc.dram_tensor(f"in_{name}", value.shape, mybir.dt.from_np(value.dtype),
                                    kind="ExternalInput").ap()
    out = nc.dram_tensor("out_0", (NP + SPARE, D), F32, kind="ExternalOutput").ap()
    graph_kernel(nc, args, out)
    r = run_bass_kernel_spmd(nc, [arrays], core_ids=[0])
    return r.results[0]["out_0"][:n_nodes]
```

```python
from contextlib import ExitStack

import concourse.bass as bass
from concourse import mybir

ALU = mybir.AluOpType
ACT = mybir.ActivationFunctionType
F32 = mybir.dt.float32
I32 = mybir.dt.int32
AX_X = mybir.AxisListType.X

P = 128
K = 4
ROWS = P * K
D = 128
HEADS = 8
HEAD_DIM = D // HEADS
LAYERS = 3
EPS_LN = 1e-5
EPS_BN = 1e-5
EPS_Q = 1e-6
EXP_MAX = 87.0
LOWEST = -1e30
REC = 16
SRC, DST, REP, ADD_AT, SOFT_AT, WRITE_AT = range(0, 6 * K, K)


class Turn:

    def __init__(self, reg, offset):
        self.reg, self.offset = reg, offset
        self.slot = offset % 2

    def __sub__(self, n):
        return Turn(self.reg, self.offset - n)

    @property
    def known(self):
        return self.reg is None

    def follows(self, n):
        return not self.known or self.number >= n

    def __add__(self, n):
        return self - -n

    @property
    def count(self):
        return self.number + 1

    @property
    def number(self):
        return self.offset if self.reg is None else 2 * self.reg + self.offset

    @property
    def half(self):
        return self.offset // 2 if self.reg is None else self.reg + self.offset // 2


class Steps:

    def __init__(self, sem, *names):
        self.sem, self.names = sem, names

    def sem_of(self, name):
        return self.sem

    def step(self, name):
        assert name in self.names
        return self.sem

    def at(self, name, turn):
        return turn.number * len(self.names) + self.names.index(name) + 1


class Marks:

    def __init__(self, sems):
        self.sems = sems

    def __getitem__(self, name):
        return self.sems[name]

    sem_of = step = __getitem__

    def at(self, name, turn):
        return turn.count


class Landed:

    def __init__(self, sems, each=1):
        self.sems, self.each = sems, each

    def full(self, turn):
        return 16 * self.each * turn.half + 16 * self.each


def run(engine, groups, lag, body):
    head = (2 + lag + 1) // 2 * 2
    for t in range(min(head, groups + lag)):
        body(Turn(None, t))
    if groups > head:
        with engine.Fori(head // 2, groups // 2) as i:
            for odd in range(2):
                body(Turn(i, odd))
    for t in range(max(groups, head), groups + lag):
        body(Turn(None, t))


def inside(turn, groups):
    return not turn.known or 0 <= turn.number < groups


def graph_kernel(nc, a, out):
    n_nodes = a["n_nodes"]
    NG = a["x"].shape[0] // ROWS
    EG = a["src"].shape[0] // ROWS
    NP, EP = NG * ROWS, EG * ROWS
    SPARE = ROWS
    last_nodes = n_nodes - (NG - 1) * ROWS
    assert NG % 2 == 0 and EG % 2 == 0 and 0 < last_nodes <= ROWS and last_nodes % K == 0
    last_parts = last_nodes // K

    def dram(name, shape, dtype=F32):
        return nc.dram_tensor(name, shape, dtype, kind="Internal").ap()

    node_rec = dram("node_rec", [NP + SPARE, REC])
    g_rows = [dram(f"g{i}_rows", [NP + SPARE, D]) for i in range(LAYERS + 1)]
    t0_T = dram("t0_T", [NG * P, ROWS])
    t1_T = dram("t1_T", [NG * P, ROWS])
    xl_rows = dram("xl_rows", [NP, D])
    first_e = dram("first_e", [EG * P, K])
    index_rec = dram("index_rec", [EG * P, 6 * K], I32)
    scale_rec = dram("scale_rec", [EG * P, 2 * K])
    nodevec_e = dram("nodevec_e", [EP, 1])
    g0_e = dram("g0_e", [EP, D])
    acc = [dram(f"acc{i}", [EP + SPARE // 2, 2 * D]) for i in range(LAYERS)]
    soft = dram("soft", [EP * K + SPARE, 2 * HEADS])
    v_e = dram("v_e", [EP, D])
    h_e = dram("h_e", [EP, D])
    xl_e = dram("xl_e", [EP, D])

    def group(table, turn):
        return table[bass.ds(turn.number * ROWS, ROWS), :].rearrange("(p k) d -> p (k d)", p=P)

    def block_of(table, turn, rows=P):
        return table[bass.ds(turn.number * rows, rows), :]

    def indirect(pool, go, **args):
        pool.sem_inc(go)
        return pool.indirect_dma_start(**args)

    def rows_at(column):
        return bass.IndirectOffsetOnAxis(ap=column, axis=0)

    with ExitStack() as whole:
        def keep(name, shape, dtype=F32):
            return whole.enter_context(nc.sbuf_tensor(name, shape, dtype))

        names = ("t_w", "wq0", "wk0", "wv0", "wq1", "wk1", "wv1", "g_w", "c0", "c1", "c2", "fc_w",
                 "l1_q", "l1_k", "l1_v", "l1_o")
        weights = keep("weights", [P, len(names), D])
        W = {n: weights[:, i, :] for i, n in enumerate(names)}
        rows_names = ("t_b", "fc_b", "bq", "bk", "bv", "bo", "gamma", "beta")
        wide = keep("wide", [P, len(rows_names), K, D])
        R = {n: wide[:, i, :, :] for i, n in enumerate(rows_names)}
        col_names = ("g_b", "cb0", "cb1", "cb2", "bg0", "bg1", "bg2", "bg3", "bb0", "bb1", "bb2", "bb3",
                     "lg0", "lg1", "lg2", "lb0", "lb1", "lb2")
        cols = keep("cols", [P, len(col_names)])
        C = {n: cols[:, i:i + 1] for i, n in enumerate(col_names)}
        bn_bias = keep("bn_bias", [P, LAYERS + 1])
        bn_scale = keep("bn_scale", [P, LAYERS + 1])
        ident = keep("ident", [P, P])
        before = keep("before", [P, K, P])
        spare_node = keep("spare_node", [P, K])
        lane = keep("lane", [P, 4 * K])
        ones = keep("ones", [P, P])
        c1w = keep("c1w", [2, 33])
        c2w = keep("c2w", [33, HEADS])
        d1w = keep("d1w", [2, 17])
        d2w = keep("d2w", [17, HEADS])
        ew = keep("ew", [65, HEADS])
        zeros = keep("zeros", [P, K, D])
        eps = keep("eps", [P, 2])
        kv = [keep(f"kv{i}", [P, D + 1]) for i in range(2)]
        passed = whole.enter_context(nc.semaphore("passed"))

        with ExitStack() as ctx:
            def sem(name):
                return ctx.enter_context(nc.semaphore(name))

            fill = ctx.enter_context(nc.sbuf_tensor("fill", [P, (NP + SPARE) // P, REC], F32))
            nodevec = ctx.enter_context(nc.sbuf_tensor("nodevec", [P, (NP + SPARE) // P], F32))
            nosoft = ctx.enter_context(nc.sbuf_tensor("nosoft", [P, (EP * K + SPARE) // P, 2, HEADS], F32))
            landed, filled, stored, scaled = sem("landed"), sem("filled"), sem("stored"), sem("scaled")
            cleared = sem("cleared")
            n_loads = len(names) + K * len(rows_names) + 10 + K
            with nc.Block() as block:
                @block.sync
                def _(sp):
                    n = 0
                    for name in names:
                        sp.dma_start(W[name], a[name]).then_inc(landed, 16)
                        n += 1
                    for name in rows_names:
                        for k in range(K):
                            sp.dma_start(R[name][:, k, :], a[name].partition_broadcast(P)).then_inc(landed, 16)
                            n += 1
                    sp.dma_start(cols[:, :], a["cols"]).then_inc(landed, 16)
                    for tile, name in ((ident, "ident"), (spare_node, "spare_node"), (lane, "lane"),
                                       (c1w, "c1w"), (c2w, "c2w"), (d1w, "d1w"), (d2w, "d2w"), (ew, "ew")):
                        sp.dma_start(tile[:, :], a[name]).then_inc(landed, 16)
                    for k in range(K):
                        sp.dma_start(before[:, k, :], a["before"]).then_inc(landed, 16)
                    sp.dma_start(nodevec[:, :], a["node_vec"].rearrange("(p n) o -> p (n o)", p=P)).then_inc(landed, 16)
                    n += 10 + K
                    assert n == n_loads
                    sp.wait_ge(filled, 1)
                    sp.dma_start(node_rec.rearrange("(p n) r -> p (n r)", p=P),
                                 fill[:, :, :].rearrange("p n r -> p (n r)")).then_inc(stored, 16)
                    sp.wait_ge(cleared, 7)
                    sp.dma_start(soft.rearrange("(p n) r -> p (n r)", p=P),
                                 nosoft[:, :, :, :].rearrange("p n t h -> p (n t h)")).then_inc(stored, 16)
                    for table in acc:
                        sp.dma_start(table[EP:EP + SPARE // 2, :].rearrange("(p n) d -> p (n d)", p=P),
                                     zeros[:, :, :].rearrange("p k d -> p (k d)")).then_inc(stored, 16)
                    sp.wait_ge(stored, 16 * (2 + LAYERS))


                @block.vector
                def _(dve):
                    dve.memset(fill[:, :, :], 0.0).then_inc(cleared, 1)
                    dve.memset(nosoft[:, :, 0, :], LOWEST).then_inc(cleared, 1)
                    dve.memset(nosoft[:, :, 1, :], 0.0).then_inc(cleared, 1)
                    dve.memset(zeros[:, :, :], 0.0).then_inc(cleared, 1)
                    dve.memset(ones[:, :], 1.0).then_inc(cleared, 1)
                    dve.memset(eps[:, 0:1], EPS_LN).then_inc(cleared, 1)
                    dve.memset(eps[:, 1:2], 4 * EPS_LN).then_inc(cleared, 1)
                    dve.wait_ge(cleared, 7)
                    dve.wait_ge(landed, 16 * n_loads)
                    dve.tensor_copy(fill[:, :, 8], nodevec[:, :]).then_inc(filled, 1)
                    for w in ("wq0", "wk0", "wq1", "wk1"):
                        dve.tensor_scalar(W[w], W[w], 1.0 / EPS_Q, None, ALU.mult)
                    dve.tensor_scalar(W["fc_w"], W["fc_w"], 0.5, None, ALU.mult)
                    at = col_names.index("bg0")
                    dve.tensor_scalar(bn_scale[:, :], cols[:, at:at + 4], (1.0 + EPS_BN) ** -0.5, None,
                                      ALU.mult).then_inc(scaled, 1)
                    dve.wait_ge(scaled, 1)
                    dve.tensor_tensor(bn_bias[:, :], cols[:, 0:4], bn_scale[:, :], ALU.mult).then_inc(scaled, 1)
                    dve.wait_ge(scaled, 2)
                    at = col_names.index("bb0")
                    dve.tensor_tensor(bn_bias[:, :], bn_bias[:, :], cols[:, at:at + 4], ALU.add)


        class Phase:

            def __init__(self, name):
                self.name, self.ctx, self.sems = name, ExitStack(), []
                self.ctx.callback(self.clear)

            def clear(self):
                nc.clear_and_free_semaphores(self.sems)
                nc.all_engine_barrier()

            def sb(self, name, shape, dtype=F32):
                return [self.ctx.enter_context(nc.sbuf_tensor(f"{self.name}_{name}{i}", shape, dtype))
                        for i in range(2)]

            def one(self, name, shape, dtype=F32):
                return self.ctx.enter_context(nc.sbuf_tensor(f"{self.name}_{name}", shape, dtype))

            def bank(self, name, banks=1):
                return self.ctx.enter_context(nc.psum_tensor(f"{self.name}_{name}", [P, 512 * banks], F32))

            def sem(self, name):
                self.sems.append(nc.alloc_semaphore(name=f"{self.name}_{name}"))
                return self.sems[-1]

            def steps(self, name, *steps):
                return Steps(self.sem(name), *steps)

            def marks(self, *names):
                return Marks({name: self.sem(name) for name in names})

            def dmas(self, name, each=1):
                return Landed([self.sem(f"{name}{i}") for i in range(2)], each)

        def by_k(tile):
            return tile.rearrange("p (k d) -> p k d", k=K)

        def flat(tile):
            return tile.rearrange("p k d -> p (k d)")

        def over(column, n):
            return column.unsqueeze(2).to_broadcast([P, column.shape[1], n])

        def moments_of(dve, steps, turn, src, norm, names):
            for k in range(K):
                ins = dve.bn_stats(norm["stats"][:, k, :], src[:, k, :])
            ins.then_inc(steps.step(names[0]), 1)
            dve.wait_ge(steps.sem_of(names[0]), steps.at(names[0], turn))
            dve.sem_inc(passed)
            for k in range(K):
                ins = dve.bn_aggr(norm["moments"][:, k, :], norm["stats"][:, k, :])
            ins.then_inc(steps.step(names[1]), 1)

        def deviation(act, norm, column=0):
            return act.activation(norm["dev"][:, :], norm["moments"][:, :, 1], ACT.Sqrt,
                                  bias=eps[:, column:column + 1])

        def norm_tiles(ph, name):
            return {"stats": ph.one(f"{name}_stats", [P, K, 6]), "moments": ph.one(f"{name}_moments", [P, K, 2]),
                    "dev": ph.one(f"{name}_dev", [P, K]), "rstd": ph.one(f"{name}_rstd", [P, K]),
                    "bias": ph.one(f"{name}_bias", [P, K])}

        def normalize(dve, dst, src, norm):
            for k in range(K):
                ins = dve.tensor_scalar(dst[:, k, :], src[:, k, :], norm["moments"][:, k, 0:1],
                                        norm["rstd"][:, k:k + 1], ALU.subtract, ALU.mult)
            return ins

        def inverted(dve, norm):
            return dve.reciprocal(norm["rstd"][:, :], norm["dev"][:, :])

        def transposed(pe, dst, src):
            for k in range(K):
                ins = pe.transpose(dst[:, k * P:(k + 1) * P], src[:, k, :], ident[:, :])
            return ins

        def index_edges():
            ph = Phase("count")
            with ph.ctx:
                dst_col, dst_row = ph.sb("dst_col", [P, K], I32), ph.sb("dst_row", [P, ROWS], I32)
                edge_no = ph.sb("edge_no", [P, K])
                same, earlier = ph.one("same", [P, K, P]), ph.one("earlier", [P, K, P])
                n_earlier, first = ph.one("n_earlier", [P, K]), ph.sb("first", [P, K])
                count = ph.sb("count", [P, K])
                dst_f, node, at = ph.one("dst_f", [P, K]), ph.one("node", [P, K]), ph.one("at", [P, K])
                count_at, edge_at = ph.sb("count_at", [P, K], I32), ph.sb("edge_at", [P, K], I32)
                cols_in, first_out = ph.dmas("cols_in", 3), ph.dmas("first_out")
                found = ph.steps("found", "same", "earlier", "n_earlier", "count", "first", "dst_f", "less",
                                 "picked", "node", "scaled", "count_at", "edge_at")
                counted = [ph.sem(f"counted{k}") for k in range(K)]
                named = [ph.sem(f"named{k}") for k in range(K)]
                go = ph.sem("go")
                rec = node_rec.rearrange("n (r o) -> (n r) o", o=1)

                def done_with(engine, turn):
                    if turn.known and turn.number < 0:
                        return
                    for k in range(K):
                        engine.wait_ge(counted[k], turn.number * 16 + 16)
                        engine.wait_ge(named[k], turn.number * 16 + 16)

                with nc.Block() as block:
                    @block.sync
                    def _(sp):
                        def body(t):
                            s = t.slot
                            if t.follows(2):
                                sp.wait_ge(found.sem, found.at("edge_at", t - 2))
                            done_with(sp, t - 2)
                            sp.dma_start(dst_col[s][:, :], group(a["dst"], t)).then_inc(cols_in.sems[t.slot], 16)
                            sp.dma_start(edge_no[s][:, :], group(a["edge_no"], t)).then_inc(cols_in.sems[t.slot], 16)
                            sp.dma_start(
                                dst_row[s][:, :],
                                a["dst"][bass.ds(t.number * ROWS, ROWS), :].rearrange("e o -> (e o)")
                                .partition_broadcast(P)).then_inc(cols_in.sems[t.slot], 16)

                        run(sp, EG, 0, body)

                    @block.scalar
                    def _(act):
                        def body(t):
                            s = t.slot
                            act.wait_ge(found.sem, found.at("first", t))
                            act.dma_start(block_of(first_e, t), first[s][:, :]).then_inc(first_out.sems[t.slot], 16)

                        run(act, EG, 0, body)
                        act.wait_ge(first_out.sems[(Turn(None, EG - 2)).slot], first_out.full(Turn(None, EG - 2)))
                        act.wait_ge(first_out.sems[(Turn(None, EG - 1)).slot], first_out.full(Turn(None, EG - 1)))

                    @block.vector
                    def _(dve):
                        def body(t):
                            s = t.slot
                            dve.wait_ge(cols_in.sems[t.slot], cols_in.full(t))
                            done_with(dve, t - 2)
                            if t.follows(2):
                                dve.wait_ge(first_out.sems[(t - 2).slot], first_out.full(t - 2))
                            dve.tensor_tensor(
                                same[:, :, :], dst_row[s].rearrange("p (q k) -> p k q", k=K),
                                over(dst_col[s][:, :], P), ALU.is_equal).then_inc(found.step("same"), 1)
                            dve.wait_ge(found.sem, found.at("same", t))
                            dve.tensor_tensor(earlier[:, :, :], same[:, :, :], before[:, :, :],
                                                         ALU.mult).then_inc(found.step("earlier"), 1)
                            dve.wait_ge(found.sem, found.at("earlier", t))
                            dve.tensor_reduce(n_earlier[:, :], earlier[:, :, :], AX_X, ALU.add).then_inc(found.step("n_earlier"), 1)
                            dve.tensor_reduce(count[s][:, :], same[:, :, :], AX_X, ALU.add).then_inc(found.step("count"), 1)
                            dve.wait_ge(found.sem, found.at("n_earlier", t))
                            dve.tensor_scalar(first[s][:, :], n_earlier[:, :], 0.0, None,
                                                         ALU.is_equal).then_inc(found.step("first"), 1)
                            dve.tensor_copy(dst_f[:, :], dst_col[s][:, :]).then_inc(found.step("dst_f"), 1)
                            dve.wait_ge(found.sem, found.at("dst_f", t))
                            dve.tensor_tensor(node[:, :], dst_f[:, :], spare_node[:, :],
                                                         ALU.subtract).then_inc(found.step("less"), 1)
                            dve.wait_ge(found.sem, found.at("less", t))
                            dve.tensor_tensor(node[:, :], node[:, :], first[s][:, :], ALU.mult).then_inc(found.step("picked"), 1)
                            dve.wait_ge(found.sem, found.at("picked", t))
                            dve.tensor_tensor(node[:, :], node[:, :], spare_node[:, :], ALU.add).then_inc(found.step("node"), 1)
                            dve.wait_ge(found.sem, found.at("node", t))
                            dve.scalar_tensor_tensor(at[:, :], node[:, :], float(REC), lane[:, 0:K],
                                                                ALU.mult, ALU.add).then_inc(found.step("scaled"), 1)
                            dve.wait_ge(found.sem, found.at("scaled", t))
                            dve.tensor_copy(count_at[s][:, :], at[:, :]).then_inc(found.step("count_at"), 1)
                            dve.tensor_scalar(edge_at[s][:, :], at[:, :], float(K), None, ALU.add).then_inc(found.step("edge_at"), 1)

                        run(dve, EG, 0, body)

                    @block.gpsimd
                    def _(pool):
                        def body(t):
                            s = t.slot
                            pool.wait_ge(found.sem, found.at("edge_at", t))
                            pool.wait_ge(cols_in.sems[t.slot], cols_in.full(t))
                            for k in range(K):
                                if not (t.known and t.number == 0):
                                    pool.wait_ge(counted[k], t.number * 16)
                                    pool.wait_ge(named[k], t.number * 16)
                                indirect(pool, go, out=rec, out_offset=rows_at(count_at[s][:, k:k + 1]),
                                         in_=count[s][:, k:k + 1], in_offset=None,
                                         compute_op=ALU.add).then_inc(counted[k], 16)
                                indirect(pool, go, out=rec, out_offset=rows_at(edge_at[s][:, k:k + 1]),
                                         in_=edge_no[s][:, k:k + 1], in_offset=None).then_inc(named[k], 16)

                        run(pool, EG, 0, body)
                        done_with(pool, Turn(None, EG - 1))

            ph = Phase("recs")
            with ph.ctx:
                src_col, dst_col = ph.sb("src_col", [P, K], I32), ph.sb("dst_col", [P, K], I32)
                edge_no, first = ph.sb("edge_no", [P, K]), ph.sb("first", [P, K])
                src_rec, dst_rec = ph.sb("src_rec", [P, K, REC]), ph.sb("dst_rec", [P, K, REC])
                degree, root = ph.one("degree", [P, 2 * K]), ph.one("root", [P, 2 * K])
                scale = ph.sb("scale", [P, 2 * K])
                rep, mine, dst_f = ph.one("rep", [P, K]), ph.one("mine", [P, K]), ph.one("dst_f", [P, K])
                to_add, to_soft, to_write = (ph.one(n, [P, K]) for n in ("to_add", "to_soft", "to_write"))
                index, nodevec = ph.sb("index", [P, 6 * K], I32), ph.sb("nodevec", [P, K])
                cols_in, out_dmas = ph.dmas("cols_in", 4), ph.dmas("out", 3)
                fetched = [[ph.sem(f"fetched{i}{k}") for k in range(2)] for i in range(2)]
                go = ph.sem("go")
                made = ph.steps("made", "sums", "scale", "rep1", "rep", "mine", "dst_f", "a0", "a1",
                                "a2", "b0", "b1", "b2", "all")
                rooted = ph.steps("rooted", "root")

                def fetched_wait(engine, t):
                    if t.known and t.number < 0:
                        return
                    for i in range(2):
                        engine.wait_ge(fetched[i][t.slot], 64 * t.half + 64)

                with nc.Block() as block:
                    @block.sync
                    def _(sp):
                        def body(t):
                            s = t.slot
                            if t.follows(2):
                                sp.wait_ge(made.sem, made.at("all", t - 2))
                            for tile, table in ((src_col, "src"), (dst_col, "dst"), (edge_no, "edge_no")):
                                sp.dma_start(tile[s][:, :], group(a[table], t)).then_inc(cols_in.sems[t.slot], 16)
                            sp.dma_start(first[s][:, :], block_of(first_e, t)).then_inc(cols_in.sems[t.slot], 16)

                        run(sp, EG, 0, body)

                    @block.gpsimd
                    def _(pool):
                        def body(t):
                            s = t.slot
                            pool.wait_ge(cols_in.sems[t.slot], cols_in.full(t))
                            if t.follows(2):
                                pool.wait_ge(made.sem, made.at("all", t - 2))
                            for i, (rec, col) in enumerate(((src_rec, src_col), (dst_rec, dst_col))):
                                for k in range(K):
                                    indirect(pool, go, out=rec[s][:, k, :], out_offset=None, in_=node_rec,
                                             in_offset=rows_at(col[s][:, k:k + 1])).then_inc(fetched[i][s], 16)

                        run(pool, EG, 0, body)

                    @block.vector
                    def _(dve):
                        def body(t):
                            s = t.slot
                            dve.wait_ge(cols_in.sems[t.slot], cols_in.full(t))
                            fetched_wait(dve, t)
                            if t.follows(2):
                                dve.wait_ge(out_dmas.sems[(t - 2).slot], out_dmas.full(t - 2))
                            dve.tensor_reduce(degree[:, 0:K], src_rec[s][:, :, 0:K], AX_X, ALU.add)
                            dve.tensor_reduce(degree[:, K:2 * K], dst_rec[s][:, :, 0:K], AX_X,
                                                        ALU.add).then_inc(made.step("sums"), 1)
                            dve.wait_ge(made.sem, made.at("sums", t))
                            dve.wait_ge(rooted.sem, rooted.at("root", t))
                            dve.reciprocal(scale[s][:, :], root[:, :]).then_inc(made.step("scale"), 1)
                            dve.tensor_reduce(rep[:, :], dst_rec[s][:, :, K:2 * K], AX_X, ALU.max).then_inc(made.step("rep1"), 1)
                            dve.wait_ge(made.sem, made.at("rep1", t))
                            dve.tensor_scalar(rep[:, :], rep[:, :], -1.0, None, ALU.add).then_inc(made.step("rep"), 1)
                            dve.wait_ge(made.sem, made.at("rep", t))
                            dve.scalar_tensor_tensor(mine[:, :], rep[:, :], 1.0, edge_no[s][:, :],
                                                               ALU.add, ALU.is_equal).then_inc(made.step("mine"), 1)
                            dve.tensor_copy(dst_f[:, :], dst_col[s][:, :]).then_inc(made.step("dst_f"), 1)
                            dve.wait_ge(made.sem, made.at("dst_f", t))
                            dve.scalar_tensor_tensor(to_add[:, :], rep[:, :], 2.0, lane[:, K:2 * K],
                                                     ALU.mult, ALU.add)
                            dve.scalar_tensor_tensor(to_soft[:, :], rep[:, :], float(K), lane[:, 2 * K:3 * K],
                                                     ALU.mult, ALU.add)
                            dve.tensor_tensor(to_write[:, :], dst_f[:, :], spare_node[:, :],
                                                        ALU.subtract).then_inc(made.step("a0"), 1)
                            dve.wait_ge(made.sem, made.at("a0", t))
                            dve.tensor_tensor(to_add[:, :], to_add[:, :], first[s][:, :], ALU.mult)
                            dve.tensor_tensor(to_soft[:, :], to_soft[:, :], first[s][:, :], ALU.mult)
                            dve.tensor_tensor(to_write[:, :], to_write[:, :], mine[:, :], ALU.mult).then_inc(made.step("a1"), 1)
                            dve.wait_ge(made.sem, made.at("a1", t))
                            dve.scalar_tensor_tensor(index[s][:, ADD_AT:ADD_AT + K], to_add[:, :],
                                                     float(2 * EP), lane[:, 3 * K:4 * K], ALU.add, ALU.add)
                            dve.scalar_tensor_tensor(index[s][:, SOFT_AT:SOFT_AT + K], to_soft[:, :],
                                                     float(K * EP), lane[:, 3 * K:4 * K], ALU.add, ALU.add)
                            dve.tensor_tensor(index[s][:, WRITE_AT:WRITE_AT + K], to_write[:, :],
                                                        spare_node[:, :], ALU.add).then_inc(made.step("a2"), 1)
                            dve.tensor_copy(index[s][:, REP:REP + K], rep[:, :]).then_inc(made.step("b0"), 1)
                            dve.tensor_copy(index[s][:, SRC:SRC + K], src_col[s][:, :]).then_inc(made.step("b1"), 1)
                            dve.tensor_copy(index[s][:, DST:DST + K], dst_col[s][:, :]).then_inc(made.step("b2"), 1)
                            dve.tensor_copy(nodevec[s][:, :], dst_rec[s][:, :, 8]).then_inc(made.step("all"), 1)

                        run(dve, EG, 0, body)

                    @block.scalar
                    def _(act):
                        def body(t):
                            s = t.slot
                            act.wait_ge(made.sem, made.at("sums", t))
                            act.activation(root[:, :], degree[:, :], ACT.Sqrt, bias=ones[:, 0:1]).then_inc(rooted.step("root"), 1)
                            act.wait_ge(made.sem, made.at("all", t))
                            act.dma_start(block_of(index_rec, t), index[s][:, :]).then_inc(out_dmas.sems[t.slot], 16)
                            act.dma_start(block_of(scale_rec, t), scale[s][:, :]).then_inc(out_dmas.sems[t.slot], 16)
                            act.dma_start(group(nodevec_e, t), nodevec[s][:, :]).then_inc(out_dmas.sems[t.slot], 16)

                        run(act, EG, 0, body)
                        act.wait_ge(out_dmas.sems[(Turn(None, EG - 2)).slot], out_dmas.full(Turn(None, EG - 2)))
                        act.wait_ge(out_dmas.sems[(Turn(None, EG - 1)).slot], out_dmas.full(Turn(None, EG - 1)))

        KV_MARKS = ("k", "v", "k_raw", "k_full", "k_sq", "k_root", "k_norm", "v_scaled", "sum")

        def kv_tiles(ph):
            tiles = {name: ph.one(name, [P, K, D]) for name in ("k_raw", "k", "k_sq")}
            tiles.update({name: ph.one(name, [P, K]) for name in ("k_norm", "k_dev")})
            tiles.update({name: ph.bank(f"p_{name}") for name in ("key", "value", "sum")})
            return {**tiles, "v": ph.one("v", [P, K, D + 1]), "sum": tiles["sum"]}

        def k_project(pe, kvt, done, cur, wk, t):
            pe.wait_ge(done["tT"], t.count)
            if t.follows(1):
                pe.wait_ge(done["k_raw"], (t - 1).count)
            for k in range(K):
                ins = pe.matmul(kvt["key"][:, k * D:(k + 1) * D], cur[:, k * P:(k + 1) * P], W[wk],
                                start=True, stop=True)
            ins.then_inc(done["k"], 1)

        def v_project(pe, kvt, done, cur, wv, t):
            if t.follows(1):
                pe.wait_ge(done["v_scaled"], (t - 1).count)
            for k in range(K):
                ins = pe.matmul(kvt["value"][:, k * D:(k + 1) * D], cur[:, k * P:(k + 1) * P], W[wv],
                                start=True, stop=True)
            ins.then_inc(done["v"], 1)

        def kv_sum(pe, kvt, done, t):
            pe.wait_ge(done["v_scaled"], t.count)
            rows = last_parts if t.known and t.number == NG - 1 else P
            for k in range(K):
                ins = pe.matmul(kvt["sum"][:, 0:D + 1], kvt["k"][0:rows, k, :], kvt["v"][0:rows, k, :],
                                start=t.known and t.number == 0 and k == 0, stop=False, skip_group_check=True)
            ins.then_inc(done["sum"], 1)

        def k_copy(act, kvt, done, t):
            act.wait_ge(done["k"], t.count)
            if t.follows(1):
                act.wait_ge(done["k_full"], (t - 1).count)
            act.copy(flat(kvt["k_raw"][:, :, :]), kvt["key"][:, :]).then_inc(done["k_raw"], 1)

        def kv_guard(dve, kvt, done, t):
            raw = kvt["k_raw"][:, :, :]
            dve.wait_ge(done["k_raw"], t.count)
            if t.follows(1):
                dve.wait_ge(done["sum"], (t - 1).count)
            dve.scalar_tensor_tensor(kvt["k"][:, :, :], raw, 0.0, raw, ALU.is_equal,
                                     ALU.add).then_inc(done["k_full"], 1)
            dve.wait_ge(done["k_full"], t.count)
            for k in range(K):
                ins = dve.tensor_tensor_reduce(kvt["k_sq"][:, k, :], kvt["k"][:, k, :], kvt["k"][:, k, :], 1.0, 0.0,
                                               ALU.mult, ALU.add, kvt["k_norm"][:, k:k + 1])
            ins.then_inc(done["k_sq"], 1)

        def kv_root(act, kvt, done, t):
            act.wait_ge(done["k_sq"], t.count)
            act.activation(kvt["k_dev"][:, :], kvt["k_norm"][:, :], ACT.Sqrt).then_inc(done["k_root"], 1)

        def kv_scale(dve, kvt, done, t):
            dve.wait_ge(done["k_root"], t.count)
            dve.reciprocal(kvt["v"][:, :, D], kvt["k_dev"][:, :]).then_inc(done["k_norm"], 1)
            dve.wait_ge(done["k_norm"], t.count)
            dve.wait_ge(done["v"], t.count)
            dve.tensor_tensor(kvt["v"][:, :, 0:D], by_k(kvt["value"][:, :]), over(kvt["v"][:, :, D], D),
                              ALU.mult).then_inc(done["v_scaled"], 1)

        def dense_first():
            ph = Phase("first")
            with ph.ctx:
                x, x_norm, y_norm = ph.sb("x", [P, K, D]), norm_tiles(ph, "x"), norm_tiles(ph, "y")
                xn, hT = ph.sb("xn", [P, K, D]), ph.sb("hT", [P, ROWS])
                gT = [ph.sb(f"g{i}T", [P, K, P]) for i in range(LAYERS + 1)]
                u = [ph.one(f"u{i}", [P, K, P]) for i in range(LAYERS)]
                rows_out = [ph.sb(f"rows{i}", [P, ROWS]) for i in range(LAYERS + 1)]
                y, yn, tT = ph.one("y", [P, K, D]), ph.sb("yn", [P, K, D]), ph.sb("tT", [P, ROWS])
                p_cols, pt, pr = ph.bank("p_cols"), ph.bank("pt"), ph.bank("pr")
                pg, pc = ph.bank("pg"), ph.bank("pc")
                kvt = kv_tiles(ph)
                x_in, t_out = ph.dmas("x_in"), ph.dmas("t_out")
                g_out = [ph.dmas(f"g{i}_out") for i in range(LAYERS + 1)]
                done = ph.marks("x_stats", "x_moments", "x_dev", "x_rstd", "xn", "xT", "hT", "g", "g0T", "c0", "u0",
                                "g1T", "c1", "u1", "g2T", "c2", "u2", "g3T", "g0r", "g1r", "g2r", "g3r", "g0o",
                                "g1o", "g2o", "g3o", "t", "y", "y_stats", "y_moments", "y_dev", "y_rstd", "yn",
                                "yT", "tT", *KV_MARKS, "kept")

                with nc.Block() as block:
                    @block.sync
                    def _(sp):
                        def store_rows(b, i):
                            sp.wait_ge(done[f"g{i}o"], b.count)
                            sp.dma_start(group(g_rows[i], b), rows_out[i][b.slot][:, :]).then_inc(
                                g_out[i].sems[b.slot], 16)

                        def body(t):
                            if inside(t, NG):
                                if t.follows(2):
                                    sp.wait_ge(done["xn"], (t - 2).count)
                                sp.dma_start(flat(x[t.slot][:, :, :]), group(a["x"], t)).then_inc(
                                    x_in.sems[t.slot], 16)
                            if inside(t - 3, NG):
                                store_rows(t - 3, 0)
                                store_rows(t - 3, 1)
                                store_rows(t - 3, 2)
                                b = t - 3
                                sp.wait_ge(done["tT"], b.count)
                                sp.dma_start(block_of(t0_T, b), tT[b.slot][:, :]).then_inc(t_out.sems[b.slot], 16)
                            if inside(t - 4, NG):
                                store_rows(t - 4, 3)

                        run(sp, NG, 4, body)
                        for t in (Turn(None, NG - 2), Turn(None, NG - 1)):
                            for stream in (*g_out, t_out):
                                sp.wait_ge(stream.sems[t.slot], stream.full(t))

                    @block.vector
                    def _(dve):
                        def x_stats(t):
                            if t.follows(1):
                                dve.wait_ge(done["xn"], (t - 1).count)
                            dve.wait_ge(x_in.sems[t.slot], x_in.full(t))
                            moments_of(dve, done, t, x[t.slot], x_norm, ("x_stats", "x_moments"))

                        def x_scale(t):
                            dve.wait_ge(done["x_dev"], t.count)
                            inverted(dve, x_norm).then_inc(done["x_rstd"], 1)
                            dve.wait_ge(done["x_rstd"], t.count)
                            if t.follows(2):
                                dve.wait_ge(done["xT"], (t - 2).count)
                            normalize(dve, xn[t.slot], x[t.slot], x_norm).then_inc(done["xn"], 1)

                        def y_stats(b):
                            dve.wait_ge(done["t"], b.count)
                            if b.follows(1):
                                dve.wait_ge(done["yn"], (b - 1).count)
                            dve.tensor_tensor(y[:, :, :], by_k(pt[:, :]), R["t_b"], ALU.add).then_inc(done["y"], 1)
                            dve.wait_ge(done["y"], b.count)
                            moments_of(dve, done, b, y, y_norm, ("y_stats", "y_moments"))

                        def y_scale(b):
                            dve.wait_ge(done["y_dev"], b.count)
                            inverted(dve, y_norm).then_inc(done["y_rstd"], 1)
                            dve.wait_ge(done["y_rstd"], b.count)
                            if b.follows(2):
                                dve.wait_ge(done["yT"], (b - 2).count)
                            normalize(dve, yn[b.slot], y, y_norm).then_inc(done["yn"], 1)

                        def body(t):
                            if inside(t - 1, NG):
                                x_scale(t - 1)
                            if inside(t - 3, NG):
                                kv_guard(dve, kvt, done, t - 3)
                            if inside(t, NG):
                                x_stats(t)
                            if inside(t - 3, NG):
                                kv_scale(dve, kvt, done, t - 3)
                            if inside(t - 1, NG):
                                y_stats(t - 1)
                                y_scale(t - 1)

                        run(dve, NG, 3, body)
                        dve.wait_ge(done["sum"], NG)
                        dve.tensor_copy(kv[0][:, :], kvt["sum"][:, 0:D + 1]).then_inc(done["kept"], 1)
                        dve.wait_ge(done["kept"], 1)

                    @block.gpsimd
                    def _(pool):
                        def add(b, i):
                            pool.wait_ge(done[f"u{i - 1}"], b.count)
                            pool.wait_ge(done["g0T"], b.count)
                            if b.follows(2):
                                pool.wait_ge(done[f"g{i}r"], (b - 2).count)
                            if b.follows(2) and i < LAYERS:
                                pool.wait_ge(done[f"c{i}"], (b - 2).count)
                            pool.tensor_tensor(gT[i][b.slot][:, :, :], u[i - 1][:, :, :], gT[0][b.slot][:, :, :],
                                               ALU.add).then_inc(done[f"g{i}T"], 1)

                        def body(t):
                            if inside(t - 3, NG):
                                add(t - 3, 3)
                            if inside(t - 2, NG):
                                add(t - 2, 1)
                                add(t - 2, 2)

                        run(pool, NG, 3, body)

                    @block.scalar
                    def _(act):
                        def out_rows(b, i):
                            act.wait_ge(done[f"g{i}r"], b.count)
                            if b.follows(2):
                                act.wait_ge(g_out[i].sems[b.slot], g_out[i].full(b - 2))
                            act.copy(rows_out[i][b.slot][:, :], pr[:, :]).then_inc(done[f"g{i}o"], 1)

                        def convolved(b, i):
                            act.wait_ge(done[f"c{i}"], b.count)
                            if b.follows(1):
                                act.wait_ge(done[f"g{i + 1}T"], (b - 1).count)
                            act.activation(flat(u[i][:, :, :]), (pc if i else pg)[:, :], ACT.Relu,
                                           bias=bn_bias[:, i + 1:i + 2],
                                           scale=bn_scale[:, i + 1:i + 2]).then_inc(done[f"u{i}"], 1)

                        def g_first(b):
                            act.wait_ge(done["g"], b.count)
                            if b.follows(2):
                                act.wait_ge(done["g3T"], (b - 2).count)
                                act.wait_ge(done["g0r"], (b - 2).count)
                                act.wait_ge(done["c0"], (b - 2).count)
                            act.activation(flat(gT[0][b.slot][:, :, :]), pg[:, :], ACT.Relu,
                                           bias=bn_bias[:, 0:1], scale=bn_scale[:, 0:1]).then_inc(done["g0T"], 1)

                        def h_first(b):
                            act.wait_ge(done["xT"], b.count)
                            if b.follows(2):
                                act.wait_ge(done["t"], (b - 2).count)
                            act.activation(hT[b.slot][:, :], p_cols[:, :], ACT.Relu).then_inc(done["hT"], 1)

                        def t_first(b):
                            act.wait_ge(done["yT"], b.count)
                            if b.follows(2):
                                act.wait_ge(t_out.sems[b.slot], t_out.full(b - 2))
                                act.wait_ge(done["v"], (b - 2).count)
                            act.activation(tT[b.slot][:, :], p_cols[:, :], ACT.Relu,
                                           bias=C["lb0"], scale=C["lg0"]).then_inc(done["tT"], 1)

                        def body(t):
                            if inside(t - 1, NG):
                                act.wait_ge(done["x_moments"], (t - 1).count)
                                deviation(act, x_norm).then_inc(done["x_dev"], 1)
                            if inside(t - 2, NG):
                                out_rows(t - 2, 0)
                                convolved(t - 2, 1)
                            if inside(t - 3, NG):
                                out_rows(t - 3, 3)
                            if inside(t - 2, NG):
                                t_first(t - 2)
                            if inside(t - 1, NG):
                                h_first(t - 1)
                            if inside(t - 2, NG):
                                out_rows(t - 2, 1)
                            if inside(t - 3, NG):
                                kv_root(act, kvt, done, t - 3)
                            if inside(t - 2, NG):
                                convolved(t - 2, 2)
                            if inside(t - 1, NG):
                                g_first(t - 1)
                                convolved(t - 1, 0)
                            if inside(t - 2, NG):
                                out_rows(t - 2, 2)
                            if inside(t - 1, NG):
                                act.wait_ge(done["y_moments"], (t - 1).count)
                                deviation(act, y_norm).then_inc(done["y_dev"], 1)
                            if inside(t - 2, NG):
                                k_copy(act, kvt, done, t - 2)

                        run(act, NG, 3, body)

                    @block.tensor
                    def _(pe):
                        def product(bank, w, right):
                            return pe.matmul(bank[:, :], W[w], right, start=True, stop=True)

                        def to_rows(b, i):
                            pe.wait_ge(done[f"g{i}T"], b.count)
                            transposed(pe, pr, gT[i][b.slot]).then_inc(done[f"g{i}r"], 1)

                        def body(t):
                            d, c, b = t - 3, t - 2, t - 1
                            if inside(d, NG):
                                if inside(d + 1, NG):
                                    pe.wait_ge(done["g0o"], (d + 1).count)
                                else:
                                    pe.wait_ge(done["g2o"], d.count)
                                to_rows(d, 3)
                            if inside(c, NG):
                                pe.wait_ge(done["yn"], c.count)
                                pe.wait_ge(done["hT"], c.count)
                                transposed(pe, p_cols, yn[c.slot]).then_inc(done["yT"], 1)
                            if inside(t - 4, NG):
                                kv_sum(pe, kvt, done, t - 4)
                            if inside(c, NG):
                                if c.follows(1):
                                    pe.wait_ge(done["g3o"], (c - 1).count)
                                else:
                                    pe.wait_ge(done["g0o"], c.count)
                                to_rows(c, 1)
                            if inside(b, NG):
                                pe.wait_ge(done["xn"], b.count)
                                if b.follows(1):
                                    pe.wait_ge(done["tT"], (b - 1).count)
                                transposed(pe, p_cols, xn[b.slot]).then_inc(done["xT"], 1)
                            if inside(c, NG):
                                pe.wait_ge(done["g2T"], c.count)
                                pe.wait_ge(done["u1"], c.count)
                                product(pc, "c2", flat(gT[2][c.slot][:, :, :])).then_inc(done["c2"], 1)
                            if inside(b, NG):
                                pe.wait_ge(done["hT"], b.count)
                                if b.follows(1):
                                    pe.wait_ge(done["u0"], (b - 1).count)
                                product(pg, "g_w", hT[b.slot][:, :]).then_inc(done["g"], 1)
                                if b.follows(1):
                                    pe.wait_ge(done["y"], (b - 1).count)
                                for k in range(K):
                                    ins = pe.matmul(pt[:, k * D:(k + 1) * D], hT[b.slot][:, k * P:(k + 1) * P],
                                                    W["t_w"], start=True, stop=True)
                                ins.then_inc(done["t"], 1)
                                pe.wait_ge(done["g0T"], b.count)
                                product(pg, "c0", flat(gT[0][b.slot][:, :, :])).then_inc(done["c0"], 1)
                            if inside(c, NG):
                                pe.wait_ge(done["g1o"], c.count)
                                to_rows(c, 2)
                                k_project(pe, kvt, done, tT[c.slot], "wk0", c)
                                v_project(pe, kvt, done, tT[c.slot], "wv0", c)
                            if inside(b, NG):
                                if b.follows(1):
                                    pe.wait_ge(done["g2o"], (b - 1).count)
                                to_rows(b, 0)
                                pe.wait_ge(done["g1T"], b.count)
                                if b.follows(1):
                                    pe.wait_ge(done["u2"], (b - 1).count)
                                product(pc, "c1", flat(gT[1][b.slot][:, :, :])).then_inc(done["c1"], 1)

                        run(pe, NG, 4, body)
        ATTEND_MARKS = ("q", "rows", "u", "norms", "q_raw", "q_full", "q_sq", "q_dev", "rows_out", "rq", "shares",
                        "share", "rden", "wkv", "weights", "t", "y", "y_stats", "y_moments", "y_dev", "y_rstd",
                        "y_bias", "yn", "yT", "tT")

        def attend_tiles(ph):
            tiles = {name: ph.sb(name, [P, K, D]) for name in ("qT", "rows", "yn")}
            tiles.update({name: ph.one(name, [P, K, D]) for name in ("q_raw", "q_sq", "t", "y")})
            tiles.update({name: ph.one(name, [P, K]) for name in ("rq", "den", "rden", "wkv", "wv", "q_dev")})
            tiles.update({name: ph.bank(name) for name in ("pq", "pn", "pv", "pu")})
            return {**tiles, "cT": ph.sb("cT", [P, ROWS]), "norm": norm_tiles(ph, "y")}

        def biased_rstd(dve, done, t, norm, dev, rstd, bias, used):
            dve.wait_ge(done[dev], t.count)
            if t.follows(1):
                dve.wait_ge(done[used], (t - 1).count)
            inverted(dve, norm).then_inc(done[rstd], 1)
            dve.wait_ge(done[rstd], t.count)
            dve.scalar_tensor_tensor(norm["bias"][:, :], norm["moments"][:, :, 0], -1.0, norm["rstd"][:, :],
                                     ALU.mult, ALU.mult).then_inc(done[bias], 1)

        def scaled_rows(act, dst, src, norm, function):
            for k in range(K):
                ins = act.activation(dst[:, k, :], src[:, k, :], function, bias=norm["bias"][:, k:k + 1],
                                     scale=norm["rstd"][:, k:k + 1])
            return ins

        def pe_q(pe, at, layer, c_in, done, t):
            pe.wait_ge(c_in.sems[t.slot], c_in.full(t))
            if t.follows(2):
                pe.wait_ge(done["tT"], (t - 2).count)
            elif t.follows(1):
                pe.wait_ge(done["rows_out"], (t - 1).count)
            pe.matmul(at["pq"][:, :], W[f"wq{layer}"], at["cT"][t.slot][:, :], start=True,
                      stop=True).then_inc(done["q"], 1)

        def pe_rows(pe, at, done, t):
            pe.wait_ge(done["q_raw"], t.count)
            transposed(pe, at["pq"], by_k(at["cT"][t.slot][:, :])).then_inc(done["rows"], 1)

        def pe_yT(pe, at, done, b):
            if inside(b + 1, NG):
                pe.wait_ge(done["rows_out"], (b + 1).count)
            if b.known and b.number == NG - 1:
                pe.wait_ge(done["rows_out"], b.count)
                pe.wait_ge(done["tT"], (b - 1).count)
            pe.wait_ge(done["yn"], b.count)
            transposed(pe, at["pq"], at["yn"][b.slot]).then_inc(done["yT"], 1)

        def pe_v(pe, at, layer, done, t):
            if t.follows(1):
                pe.wait_ge(done["y"], (t - 1).count)
            for k in range(K):
                ins = pe.matmul(at["pv"][:, k * D:(k + 1) * D], at["cT"][t.slot][:, k * P:(k + 1) * P],
                                W[f"wv{layer}"], start=True, stop=True)
            ins.then_inc(done["av"], 1)

        def pe_u(pe, at, kvs, done, t):
            pe.wait_ge(done["q_full"], t.count)
            if t.follows(1):
                pe.wait_ge(done["t"], (t - 1).count)
            for k in range(K):
                ins = pe.matmul(at["pu"][:, k * D:(k + 1) * D], at["qT"][t.slot][:, k, :], kvs[:, 0:D],
                                start=True, stop=True)
            ins.then_inc(done["u"], 1)

        def pe_norms(pe, at, kvs, done, t):
            pe.wait_ge(done["q_full"], t.count)
            pe.wait_ge(done["q_sq"], t.count)
            if t.follows(1):
                pe.wait_ge(done["shares"], (t - 1).count)
            for k in range(K):
                pe.matmul(at["pn"][:, K + k:K + k + 1], at["qT"][t.slot][:, k, :], kvs[:, D:D + 1],
                          start=True, stop=True)
                ins = pe.matmul(at["pn"][:, k:k + 1], at["q_sq"][:, k, :], ones[:, 0:1], start=True, stop=True)
            ins.then_inc(done["norms"], 1)

        def act_q_raw(act, at, done, t):
            act.wait_ge(done["q"], t.count)
            if t.follows(1):
                act.wait_ge(done["q_full"], (t - 1).count)
            act.copy(flat(at["q_raw"][:, :, :]), at["pq"][:, :]).then_inc(done["q_raw"], 1)

        def act_rows(act, at, done, t):
            act.wait_ge(done["rows"], t.count)
            if t.follows(2):
                act.wait_ge(done["t"], (t - 2).count)
            act.copy(flat(at["rows"][t.slot][:, :, :]), at["pq"][:, :]).then_inc(done["rows_out"], 1)

        def act_q_sq(act, at, done, t):
            act.wait_ge(done["q_full"], t.count)
            if t.follows(1):
                act.wait_ge(done["norms"], (t - 1).count)
            act.activation(at["q_sq"][:, :, :], at["qT"][t.slot][:, :, :], ACT.Square).then_inc(done["q_sq"], 1)

        def act_q_dev(act, at, done, t):
            act.wait_ge(done["norms"], t.count)
            if t.follows(1):
                act.wait_ge(done["rq"], (t - 1).count)
            act.activation(at["q_dev"][:, :], at["pn"][:, 0:K], ACT.Sqrt).then_inc(done["q_dev"], 1)

        def act_y_dev(act, at, done, b):
            act.wait_ge(done["y_moments"], b.count)
            deviation(act, at["norm"], 1).then_inc(done["y_dev"], 1)

        def act_yn(act, at, done, b):
            act.wait_ge(done["y_bias"], b.count)
            if b.follows(2):
                act.wait_ge(done["yT"], (b - 2).count)
            scaled_rows(act, at["yn"][b.slot], at["y"], at["norm"], ACT.Identity).then_inc(done["yn"], 1)

        def dve_q_full(dve, at, done, t):
            dve.wait_ge(done["q_raw"], t.count)
            if t.follows(2):
                dve.wait_ge(done["u"], (t - 2).count)
                dve.wait_ge(done["norms"], (t - 2).count)
            raw = at["q_raw"][:, :, :]
            dve.scalar_tensor_tensor(at["qT"][t.slot][:, :, :], raw, 0.0, raw, ALU.is_equal,
                                        ALU.add).then_inc(done["q_full"], 1)

        def dve_weights(dve, at, done, t):
            dve.wait_ge(done["q_dev"], t.count)
            dve.reciprocal(at["rq"][:, :], at["q_dev"][:, :]).then_inc(done["rq"], 1)
            dve.wait_ge(done["rq"], t.count)
            dve.tensor_tensor(at["den"][:, :], at["pn"][:, K:2 * K], at["rq"][:, :], ALU.mult).then_inc(done["shares"], 1)
            dve.wait_ge(done["shares"], t.count)
            dve.tensor_scalar(at["den"][:, :], at["den"][:, :], float(n_nodes), None, ALU.add).then_inc(done["share"], 1)
            dve.wait_ge(done["share"], t.count)
            dve.reciprocal(at["rden"][:, :], at["den"][:, :]).then_inc(done["rden"], 1)
            dve.wait_ge(done["rden"], t.count)
            if t.follows(1):
                dve.wait_ge(done["y"], (t - 1).count)
            dve.tensor_tensor(at["wkv"][:, :], at["rq"][:, :], at["rden"][:, :], ALU.mult).then_inc(done["wkv"], 1)
            dve.tensor_scalar(at["wv"][:, :], at["rden"][:, :], float(n_nodes), None, ALU.mult).then_inc(done["weights"], 1)

        def dve_t(dve, at, done, t):
            dve.wait_ge(done["weights"], t.count)
            dve.wait_ge(done["u"], t.count)
            dve.wait_ge(done["rows_out"], t.count)
            for k in range(K):
                ins = dve.scalar_tensor_tensor(at["t"][:, k, :], at["pu"][:, k * D:(k + 1) * D], at["wkv"][:, k:k + 1],
                                               at["rows"][t.slot][:, k, :], ALU.mult, ALU.add)
            ins.then_inc(done["t"], 1)

        def dve_y(dve, at, done, b):
            dve.wait_ge(done["t"], b.count)
            dve.wait_ge(done["av"], b.count)
            if b.follows(1):
                dve.wait_ge(done["yn"], (b - 1).count)
            for k in range(K):
                ins = dve.scalar_tensor_tensor(at["y"][:, k, :], at["pv"][:, k * D:(k + 1) * D], at["wv"][:, k:k + 1],
                                               at["t"][:, k, :], ALU.mult, ALU.add)
            ins.then_inc(done["y"], 1)
            dve.wait_ge(done["y"], b.count)
            moments_of(dve, done, b, at["y"], at["norm"], ("y_stats", "y_moments"))

        def dve_y_rstd(dve, at, done, b):
            biased_rstd(dve, done, b, at["norm"], "y_dev", "y_rstd", "y_bias", "yn")

        def dense_second():
            ph = Phase("second")
            with ph.ctx:
                at, kvt = attend_tiles(ph), kv_tiles(ph)
                tT = ph.sb("tT", [P, ROWS])
                c_in, t_out = ph.dmas("c_in"), ph.dmas("t_out")
                done = ph.marks(*dict.fromkeys(ATTEND_MARKS + KV_MARKS + ("av", "kept")))

                with nc.Block() as block:
                    @block.sync
                    def _(sp):
                        def body(t):
                            if inside(t, NG):
                                if t.follows(2):
                                    sp.wait_ge(done["av"], (t - 2).count)
                                    sp.wait_ge(done["rows"], (t - 2).count)
                                sp.dma_start(at["cT"][t.slot][:, :], block_of(t0_T, t)).then_inc(c_in.sems[t.slot], 16)
                            b = t - 3
                            if inside(b, NG):
                                sp.wait_ge(done["tT"], b.count)
                                sp.dma_start(block_of(t1_T, b), tT[b.slot][:, :]).then_inc(t_out.sems[b.slot], 16)

                        run(sp, NG, 3, body)
                        for t in (Turn(None, NG - 2), Turn(None, NG - 1)):
                            sp.wait_ge(t_out.sems[t.slot], t_out.full(t))

                    @block.tensor
                    def _(pe):
                        def body(t):
                            if inside(t - 2, NG):
                                k_project(pe, kvt, done, tT[t.slot], "wk1", t - 2)
                            if inside(t, NG):
                                pe_q(pe, at, 0, c_in, done, t)
                                pe_rows(pe, at, done, t)
                            if inside(t - 3, NG):
                                kv_sum(pe, kvt, done, t - 3)
                            if inside(t - 2, NG):
                                v_project(pe, kvt, done, tT[t.slot], "wv1", t - 2)
                            if inside(t, NG):
                                pe_u(pe, at, kv[0], done, t)
                                pe_norms(pe, at, kv[0], done, t)
                            if inside(t - 1, NG):
                                pe_yT(pe, at, done, t - 1)
                            if inside(t, NG):
                                pe_v(pe, at, 0, done, t)

                        run(pe, NG, 3, body)

                    @block.scalar
                    def _(act):
                        def body(t):
                            c = t - 2
                            if inside(c, NG):
                                act.wait_ge(done["yT"], c.count)
                                if c.follows(2):
                                    act.wait_ge(t_out.sems[c.slot], t_out.full(c - 2))
                                    act.wait_ge(done["v"], (c - 2).count)
                                act.activation(tT[c.slot][:, :], at["pq"][:, :], ACT.Relu,
                                               bias=C["lb1"], scale=C["lg1"]).then_inc(done["tT"], 1)
                            if inside(t, NG):
                                act_q_raw(act, at, done, t)
                            if inside(c, NG):
                                k_copy(act, kvt, done, c)
                            if inside(t, NG):
                                act_rows(act, at, done, t)
                            if inside(t - 1, NG):
                                act_y_dev(act, at, done, t - 1)
                            if inside(t, NG):
                                act_q_sq(act, at, done, t)
                            if inside(t - 1, NG):
                                act_yn(act, at, done, t - 1)
                            if inside(c, NG):
                                kv_root(act, kvt, done, c)
                            if inside(t, NG):
                                act_q_dev(act, at, done, t)

                        run(act, NG, 2, body)

                    @block.vector
                    def _(dve):
                        def body(t):
                            b, c = t - 1, t - 2
                            if inside(b, NG):
                                dve_weights(dve, at, done, b)
                                dve_t(dve, at, done, b)
                                dve_y(dve, at, done, b)
                            if inside(t, NG):
                                dve_q_full(dve, at, done, t)
                            if inside(c, NG):
                                kv_guard(dve, kvt, done, c)
                            if inside(b, NG):
                                dve_y_rstd(dve, at, done, b)
                            if inside(c, NG):
                                kv_scale(dve, kvt, done, c)

                        run(dve, NG, 2, body)
                        dve.wait_ge(done["sum"], NG)
                        dve.tensor_copy(kv[1][:, :], kvt["sum"][:, 0:D + 1]).then_inc(done["kept"], 1)
                        dve.wait_ge(done["kept"], 1)

        def dense_third():
            ph = Phase("third")
            with ph.ctx:
                at = attend_tiles(ph)
                x, x2 = ph.sb("x", [P, K, D]), ph.sb("x2", [P, K, D])
                tT, sT = ph.one("tT", [P, ROWS]), ph.one("sT", [P, ROWS])
                xb, xl = ph.one("xb", [P, K, D]), ph.sb("xl", [P, K, D])
                h, z, zn, zg, q_zero = (ph.one(n, [P, K, D]) for n in ("h", "z", "zn", "zg", "q_zero"))
                xlb, o = ph.sb("xlb", [P, K, D]), ph.sb("o", [P, K, D])
                x_norm, z_norm = norm_tiles(ph, "x"), norm_tiles(ph, "z")
                px, po = ph.bank("px"), ph.bank("po")
                c_in, x_in, x2_in = ph.dmas("c_in"), ph.dmas("x_in"), ph.dmas("x2_in")
                xl_out, o_out = ph.dmas("xl_out"), ph.dmas("o_out")
                done = ph.marks(*ATTEND_MARKS, "av", "x2T", "fc", "sT", "xb", "xl", "xl_stats", "xl_moments", "dev",
                                "rstd", "bias", "h", "z", "z_stats", "z_moments", "z_dev", "z_rstd", "z_bias", "zn",
                                "zg", "xlb", "o", "q_zero")

                with nc.Block() as block:
                    @block.sync
                    def _(sp):
                        def body(t):
                            if inside(t, NG):
                                if t.follows(2):
                                    sp.wait_ge(done["av"], (t - 2).count)
                                    sp.wait_ge(done["rows"], (t - 2).count)
                                sp.dma_start(at["cT"][t.slot][:, :], block_of(t1_T, t)).then_inc(c_in.sems[t.slot], 16)
                            b = t - 1
                            if inside(b, NG):
                                if b.follows(2):
                                    sp.wait_ge(done["x2T"], (b - 2).count)
                                sp.dma_start(flat(x2[b.slot][:, :, :]), group(g_rows[LAYERS], b)).then_inc(
                                    x2_in.sems[b.slot], 16)
                                if b.follows(2):
                                    sp.wait_ge(done["xb"], (b - 2).count)
                                sp.dma_start(flat(x[b.slot][:, :, :]), group(a["x"], b)).then_inc(
                                    x_in.sems[b.slot], 16)
                            d = t - 3
                            if inside(d, NG):
                                sp.wait_ge(done["xl"], d.count)
                                sp.dma_start(group(xl_rows, d), flat(xl[d.slot][:, :, :])).then_inc(
                                    xl_out.sems[d.slot], 16)
                            f = t - 5
                            if inside(f, NG):
                                sp.wait_ge(done["o"], f.count)
                                sp.dma_start(group(out, f), flat(o[f.slot][:, :, :])).then_inc(o_out.sems[f.slot], 16)

                        run(sp, NG, 5, body)
                        for t in (Turn(None, NG - 2), Turn(None, NG - 1)):
                            sp.wait_ge(xl_out.sems[t.slot], xl_out.full(t))
                            sp.wait_ge(o_out.sems[t.slot], o_out.full(t))

                    @block.tensor
                    def _(pe):
                        def body(t):
                            b, c = t - 1, t - 2
                            if inside(b, NG):
                                pe_v(pe, at, 1, done, b)
                            if inside(t, NG):
                                pe_q(pe, at, 1, c_in, done, t)
                            if inside(b, NG):
                                pe.wait_ge(x2_in.sems[b.slot], x2_in.full(b))
                                if b.follows(1):
                                    pe.wait_ge(done["sT"], (b - 1).count)
                                transposed(pe, px, x2[b.slot]).then_inc(done["x2T"], 1)
                            if inside(c, NG):
                                pe.wait_ge(done["sT"], c.count)
                                if c.follows(1):
                                    pe.wait_ge(done["xl"], (c - 1).count)
                                for k in range(K):
                                    ins = pe.matmul(po[:, k * D:(k + 1) * D], sT[:, k * P:(k + 1) * P], W["fc_w"],
                                                    start=True, stop=True)
                                ins.then_inc(done["fc"], 1)
                            if inside(t, NG):
                                pe_rows(pe, at, done, t)
                                pe_norms(pe, at, kv[1], done, t)
                                pe_u(pe, at, kv[1], done, t)
                            if inside(b, NG):
                                pe_yT(pe, at, done, b)

                        run(pe, NG, 2, body)

                    @block.scalar
                    def _(act):
                        def body(t):
                            b, c, d = t - 1, t - 2, t - 3
                            if inside(t, NG):
                                act_q_raw(act, at, done, t)
                                act_q_sq(act, at, done, t)
                            if inside(b, NG):
                                act_y_dev(act, at, done, b)
                            if inside(t, NG):
                                act_rows(act, at, done, t)
                                act_q_dev(act, at, done, t)
                            if inside(c, NG):
                                act.wait_ge(done["xl_moments"], c.count)
                                deviation(act, x_norm).then_inc(done["dev"], 1)
                            if inside(b, NG):
                                act_yn(act, at, done, b)
                            if inside(d, NG):
                                act.wait_ge(done["z_moments"], d.count)
                                deviation(act, z_norm).then_inc(done["z_dev"], 1)
                            if inside(b, NG):
                                act.wait_ge(done["yT"], b.count)
                                if b.follows(1):
                                    act.wait_ge(done["sT"], (b - 1).count)
                                act.activation(tT[:, :], at["pq"][:, :], ACT.Relu,
                                               bias=C["lb2"], scale=C["lg2"]).then_inc(done["tT"], 1)
                            if inside(c, NG):
                                act.wait_ge(done["bias"], c.count)
                                if c.follows(1):
                                    act.wait_ge(done["z"], (c - 1).count)
                                scaled_rows(act, h, xl[c.slot], x_norm, ACT.Relu).then_inc(done["h"], 1)
                            if inside(d, NG):
                                act.wait_ge(done["z_bias"], d.count)
                                if d.follows(1):
                                    act.wait_ge(done["zg"], (d - 1).count)
                                scaled_rows(act, zn, z, z_norm, ACT.Identity).then_inc(done["zn"], 1)

                        run(act, NG, 3, body)

                    @block.gpsimd
                    def _(pool):
                        def body(t):
                            b, d, e = t - 1, t - 3, t - 4
                            if inside(e, NG):
                                pool.wait_ge(done["xl"], e.count)
                                if e.follows(2):
                                    pool.wait_ge(done["o"], (e - 2).count)
                                pool.tensor_tensor(xlb[e.slot][:, :, :], xl[e.slot][:, :, :], R["beta"],
                                                   ALU.add).then_inc(done["xlb"], 1)
                            if inside(d, NG):
                                pool.wait_ge(done["h"], d.count)
                                if d.follows(1):
                                    pool.wait_ge(done["zn"], (d - 1).count)
                                pool.tensor_tensor(z[:, :, :], h[:, :, :], R["bo"], ALU.add).then_inc(done["z"], 1)
                            if inside(t, NG):
                                pool.wait_ge(done["q_raw"], t.count)
                                if t.follows(2):
                                    pool.wait_ge(done["u"], (t - 2).count)
                                    pool.wait_ge(done["norms"], (t - 2).count)
                                    pool.wait_ge(done["q_sq"], (t - 2).count)
                                pool.sem_inc(passed)
                                pool.tensor_scalar(q_zero[:, :, :], at["q_raw"][:, :, :], 0.0, None,
                                                   ALU.is_equal).then_inc(done["q_zero"], 1)
                                pool.wait_ge(done["q_zero"], t.count)
                                pool.tensor_tensor(at["qT"][t.slot][:, :, :], at["q_raw"][:, :, :], q_zero[:, :, :],
                                                   ALU.add).then_inc(done["q_full"], 1)
                            if inside(e, NG):
                                pool.wait_ge(done["zn"], e.count)
                                if e.follows(1):
                                    pool.wait_ge(done["o"], (e - 1).count)
                                pool.tensor_tensor(zg[:, :, :], zn[:, :, :], R["gamma"],
                                                   ALU.mult).then_inc(done["zg"], 1)
                            if inside(b, NG):
                                pool.wait_ge(x_in.sems[b.slot], x_in.full(b))
                                if b.follows(1):
                                    pool.wait_ge(done["xl"], (b - 1).count)
                                pool.tensor_tensor(xb[:, :, :], x[b.slot][:, :, :], R["fc_b"],
                                                   ALU.add).then_inc(done["xb"], 1)

                        run(pool, NG, 4, body)

                    @block.vector
                    def _(dve):
                        def body(t):
                            b, c, d, e = t - 1, t - 2, t - 3, t - 4
                            if inside(b, NG):
                                dve_y(dve, at, done, b)
                            if inside(c, NG):
                                dve.wait_ge(done["fc"], c.count)
                                dve.wait_ge(done["xb"], c.count)
                                if c.follows(2):
                                    dve.wait_ge(xl_out.sems[c.slot], xl_out.full(c - 2))
                                    dve.wait_ge(done["xlb"], (c - 2).count)
                                dve.tensor_tensor(xl[c.slot][:, :, :], by_k(po[:, :]), xb[:, :, :],
                                                  ALU.add).then_inc(done["xl"], 1)
                                dve.wait_ge(done["xl"], c.count)
                                if c.follows(1):
                                    dve.wait_ge(done["h"], (c - 1).count)
                                moments_of(dve, done, c, xl[c.slot], x_norm, ("xl_stats", "xl_moments"))
                            if inside(b, NG):
                                dve_y_rstd(dve, at, done, b)
                            if inside(d, NG):
                                dve.wait_ge(done["z"], d.count)
                                moments_of(dve, done, d, z, z_norm, ("z_stats", "z_moments"))
                            if inside(t, NG):
                                dve_weights(dve, at, done, t)
                            if inside(c, NG):
                                biased_rstd(dve, done, c, x_norm, "dev", "rstd", "bias", "h")
                            if inside(t, NG):
                                dve_t(dve, at, done, t)
                            if inside(d, NG):
                                biased_rstd(dve, done, d, z_norm, "z_dev", "z_rstd", "z_bias", "zn")
                            if inside(b, NG):
                                dve.wait_ge(done["tT"], b.count)
                                dve.wait_ge(done["x2T"], b.count)
                                if b.follows(1):
                                    dve.wait_ge(done["fc"], (b - 1).count)
                                dve.tensor_tensor(sT[:, :], tT[:, :], px[:, :], ALU.add).then_inc(done["sT"], 1)
                            if inside(e, NG):
                                dve.wait_ge(done["zg"], e.count)
                                dve.wait_ge(done["xlb"], e.count)
                                if e.follows(2):
                                    dve.wait_ge(o_out.sems[e.slot], o_out.full(e - 2))
                                dve.tensor_tensor(o[e.slot][:, :, :], zg[:, :, :], xlb[e.slot][:, :, :],
                                                  ALU.add).then_inc(done["o"], 1)

                        run(dve, NG, 4, body)

        def first_rows():
            ph = Phase("own")
            with ph.ctx:
                index, scale = ph.sb("index", [P, 6 * K], I32), ph.sb("scale", [P, 2 * K])
                g = ph.sb("g", [P, K, D])
                start = ph.sb("start", [P, K, 2, D])
                rec_in, stores = ph.dmas("rec_in", 2), ph.dmas("stores", 2)
                fetched = ph.dmas("fetched", K)
                go, blank = ph.sem("go"), ph.sem("blank")
                own = ph.steps("own", "own")

                with nc.Block() as block:
                    @block.sync
                    def _(sp):
                        def body(t):
                            s = t.slot
                            if inside(t, EG):
                                if t.follows(2):
                                    sp.wait_ge(own.sem, own.at("own", t - 2))
                                sp.dma_start(index[s][:, :], block_of(index_rec, t)).then_inc(rec_in.sems[t.slot], 16)
                                sp.dma_start(scale[s][:, :], block_of(scale_rec, t)).then_inc(rec_in.sems[t.slot], 16)
                            b = t - 1
                            if inside(b, EG):
                                sp.wait_ge(own.sem, own.at("own", b))
                                sp.dma_start(group(g0_e, b), flat(g[b.slot][:, :, :])).then_inc(stores.sems[b.slot], 16)
                                sp.dma_start(group(acc[0], b),
                                                          start[b.slot].rearrange("p k l d -> p (k l d)")).then_inc(stores.sems[b.slot], 16)

                        run(sp, EG, 1, body)
                        for t in (EG - 2, EG - 1):
                            sp.wait_ge(stores.sems[(Turn(None, t)).slot], stores.full(Turn(None, t)))

                    @block.gpsimd
                    def _(pool):
                        def body(t):
                            s = t.slot
                            pool.wait_ge(rec_in.sems[t.slot], rec_in.full(t))
                            if t.follows(2):
                                pool.wait_ge(stores.sems[(t - 2).slot], stores.full(t - 2))
                            for k in range(K):
                                indirect(pool, go, out=g[s][:, k, :], out_offset=None,
                                                       in_=g_rows[0][0:NP, :],
                                                       in_offset=rows_at(index[s][:, DST + k:DST + k + 1])).then_inc(fetched.sems[t.slot], 16)

                        run(pool, EG, 0, body)

                    @block.vector
                    def _(dve):
                        for s in range(2):
                            dve.memset(start[s][:, :, :, :], 0.0).then_inc(blank, 1)
                        dve.wait_ge(blank, 2)

                        def body(t):
                            s = t.slot
                            dve.wait_ge(rec_in.sems[t.slot], rec_in.full(t))
                            dve.wait_ge(fetched.sems[t.slot], fetched.full(t))
                            if t.follows(2):
                                dve.wait_ge(stores.sems[(t - 2).slot], stores.full(t - 2))
                            dve.tensor_tensor(start[s][:, :, 0, :], g[s][:, :, :],
                                                       over(scale[s][:, K:2 * K], D), ALU.mult).then_inc(own.step("own"), 1)

                        run(dve, EG, 0, body)

        def gather_messages(layer):
            ph = Phase(f"send{layer}")
            with ph.ctx:
                index, scale = ph.sb("index", [P, 6 * K], I32), ph.sb("scale", [P, 2 * K])
                dst_row = ph.sb("dst_row", [P, ROWS], I32)
                same = ph.sb("same", [P, K, P])
                g, m, total = ph.sb("g", [P, K, D]), ph.sb("m", [P, K, D]), ph.sb("total", [P, K, D])
                pm = [ph.bank(f"pm{i}") for i in range(2)]
                rec_in = ph.dmas("rec_in", 3)
                fetched = ph.dmas("fetched", K)
                added = [ph.sem(f"added{k}") for k in range(K)]
                go = ph.sem("go")
                made = ph.steps("made", "same", "m")
                summed, copied = ph.steps("summed", "sum"), ph.steps("copied", "total")
                sums = acc[layer].rearrange("e (l d) -> (e l) d", l=2)

                def added_wait(engine, t, ks=range(K)):
                    if t.known and t.number < 0:
                        return
                    for k in ks:
                        engine.wait_ge(added[k], 16 * t.number + 16)

                with nc.Block() as block:
                    @block.sync
                    def _(sp):
                        def body(t):
                            s = t.slot
                            if t.follows(2):
                                sp.wait_ge(made.sem, made.at("m", t - 2))
                            added_wait(sp, t - 2)
                            sp.dma_start(index[s][:, :], block_of(index_rec, t)).then_inc(rec_in.sems[t.slot], 16)
                            sp.dma_start(scale[s][:, :], block_of(scale_rec, t)).then_inc(rec_in.sems[t.slot], 16)
                            sp.dma_start(
                                dst_row[s][:, :],
                                a["dst"][bass.ds(t.number * ROWS, ROWS), :].rearrange("e o -> (e o)")
                                .partition_broadcast(P)).then_inc(rec_in.sems[t.slot], 16)

                        run(sp, EG, 0, body)

                    @block.gpsimd
                    def _(pool):
                        def body(t):
                            b = t - 1
                            if inside(t, EG):
                                pool.wait_ge(rec_in.sems[t.slot], rec_in.full(t))
                                if t.follows(2):
                                    pool.wait_ge(made.sem, made.at("m", t - 2))
                            if inside(b, EG):
                                pool.wait_ge(copied.sem, copied.at("total", b))
                            for k in range(K):
                                if inside(t, EG):
                                    indirect(
                                        pool, go, out=g[t.slot][:, k, :], out_offset=None, in_=g_rows[layer][0:NP, :],
                                        in_offset=rows_at(index[t.slot][:, SRC + k:SRC + k + 1])).then_inc(fetched.sems[t.slot], 16)
                                if inside(b, EG):
                                    added_wait(pool, b if k >= 2 else b - 1, [(k + 2) % K])
                                    indirect(pool, go, out=sums,
                                             out_offset=rows_at(index[b.slot][:, ADD_AT + k:ADD_AT + k + 1]),
                                             in_=total[b.slot][:, k, :], in_offset=None,
                                             compute_op=ALU.add).then_inc(added[k], 16)

                        run(pool, EG, 1, body)
                        added_wait(pool, Turn(None, EG - 1))

                    @block.vector
                    def _(dve):
                        def body(t):
                            s = t.slot
                            dve.wait_ge(rec_in.sems[t.slot], rec_in.full(t))
                            if t.follows(2):
                                dve.wait_ge(summed.sem, summed.at("sum", t - 2))
                            dve.tensor_tensor(
                                same[s][:, :, :], dst_row[s].rearrange("p (q k) -> p k q", k=K),
                                over(index[s][:, DST:DST + K], P), ALU.is_equal).then_inc(made.step("same"), 1)
                            dve.wait_ge(fetched.sems[t.slot], fetched.full(t))
                            dve.tensor_tensor(m[s][:, :, :], g[s][:, :, :],
                                                        over(scale[s][:, 0:K], D), ALU.mult).then_inc(made.step("m"), 1)

                        run(dve, EG, 0, body)

                    @block.tensor
                    def _(pe):
                        def body(t):
                            s = t.slot
                            pe.wait_ge(made.sem, made.at("m", t))
                            if t.follows(2):
                                pe.wait_ge(copied.sem, copied.at("total", t - 2))
                            for k in range(K):
                                ins = pe.matmul(pm[s][:, k * D:(k + 1) * D], same[s][:, k, :], m[s][:, k, :],
                                                start=True, stop=True)
                            ins.then_inc(summed.step("sum"), 1)

                        run(pe, EG, 0, body)

                    @block.scalar
                    def _(act):
                        def body(t):
                            s = t.slot
                            act.wait_ge(summed.sem, summed.at("sum", t))
                            added_wait(act, t - 2)
                            act.copy(flat(total[s][:, :, :]), pm[s][:, :]).then_inc(copied.step("total"), 1)

                        run(act, EG, 0, body)

        def update_nodes(layer):
            last = layer == LAYERS - 1
            ph = Phase(f"update{layer}")
            with ph.ctx:
                index, scale = ph.sb("index", [P, 6 * K], I32), ph.sb("scale", [P, 2 * K])
                parts, g0 = ph.sb("parts", [P, K, 2, D]), ph.sb("g0", [P, K, D])
                s0, s1 = ph.sb("s0", [P, K, D]), ph.sb("s1", [P, K, D])
                sT, uT = ph.sb("sT", [P, ROWS]), ph.sb("uT", [P, K, P])
                g = ph.sb("g", [P, K, D])
                start = ph.sb("start", [P, K, 2, D])
                ps, pc, pu = ([ph.bank(f"{n}{i}") for i in range(2)] for n in ("ps", "pc", "pu"))
                rec_in = ph.dmas("rec_in", 3)
                fetched, written, stores = ph.dmas("fetched", K), ph.dmas("written", K), ph.dmas("stores")
                go, blank = ph.sem("go"), ph.sem("blank")
                summed = ph.steps("summed", "s0", "s1")
                finished = ph.steps("finished", "g", "start")
                pe_s, pe_c, pe_u = ph.steps("pe_s", "sT"), ph.steps("pe_c", "c"), ph.steps("pe_u", "u")
                act_s, act_u = ph.steps("act_s", "sT"), ph.steps("act_u", "uT")

                with nc.Block() as block:
                    @block.sync
                    def _(sp):
                        def body(t):
                            s = t.slot
                            if inside(t, EG):
                                if t.follows(2):
                                    sp.wait_ge(finished.sem, finished.at("start", t - 2))
                                if t.follows(2):
                                    sp.wait_ge(written.sems[(t - 2).slot], written.full(t - 2))
                                sp.dma_start(index[s][:, :], block_of(index_rec, t)).then_inc(rec_in.sems[t.slot], 16)
                                sp.dma_start(scale[s][:, :], block_of(scale_rec, t)).then_inc(rec_in.sems[t.slot], 16)
                                sp.dma_start(flat(g0[s][:, :, :]), group(g0_e, t)).then_inc(rec_in.sems[t.slot], 16)
                            b = t - 1
                            if not last and inside(b, EG):
                                sp.wait_ge(finished.sem, finished.at("start", b))
                                sp.dma_start(group(acc[layer + 1], b),
                                                          start[b.slot].rearrange("p k l d -> p (k l d)")).then_inc(stores.sems[b.slot], 16)

                        run(sp, EG, 1, body)
                        if not last:
                            for t in (EG - 2, EG - 1):
                                sp.wait_ge(stores.sems[(Turn(None, t)).slot], stores.full(Turn(None, t)))

                    @block.gpsimd
                    def _(pool):
                        def body(t):
                            if inside(t, EG):
                                s = t.slot
                                pool.wait_ge(rec_in.sems[t.slot], rec_in.full(t))
                                if t.follows(2):
                                    pool.wait_ge(summed.sem, summed.at("s0", t - 2))
                                for k in range(K):
                                    indirect(
                                        pool, go, out=parts[s][:, k, :, :].rearrange("p l d -> p (l d)"),
                                        out_offset=None, in_=acc[layer],
                                        in_offset=rows_at(index[s][:, REP + k:REP + k + 1])).then_inc(fetched.sems[t.slot], 16)
                            b = t - 1
                            if inside(b, EG):
                                pool.wait_ge(finished.sem, finished.at("g", b))
                                if b.follows(1):
                                    pool.wait_ge(written.sems[(b - 1).slot], written.full(b - 1))
                                for k in range(K):
                                    indirect(
                                        pool, go, out=g_rows[layer + 1],
                                        out_offset=rows_at(index[b.slot][:, WRITE_AT + k:WRITE_AT + k + 1]),
                                        in_=g[b.slot][:, k, :], in_offset=None).then_inc(written.sems[b.slot], 16)

                        run(pool, EG, 1, body)
                        for t in (EG - 2, EG - 1):
                            pool.wait_ge(written.sems[(Turn(None, t)).slot], written.full(Turn(None, t)))

                    @block.vector
                    def _(dve):
                        for s in range(2):
                            dve.memset(start[s][:, :, :, :], 0.0).then_inc(blank, 1)
                        dve.wait_ge(blank, 2)

                        def body(t):
                            if inside(t, EG):
                                s = t.slot
                                dve.wait_ge(rec_in.sems[t.slot], rec_in.full(t))
                                dve.wait_ge(fetched.sems[t.slot], fetched.full(t))
                                dve.tensor_tensor(s0[s][:, :, :], parts[s][:, :, 0, :],
                                                              parts[s][:, :, 1, :], ALU.add).then_inc(summed.step("s0"), 1)
                                dve.wait_ge(summed.sem, summed.at("s0", t))
                                if t.follows(2):
                                    dve.wait_ge(pe_s.sem, pe_s.at("sT", t - 2))
                                dve.tensor_tensor(s1[s][:, :, :], s0[s][:, :, :],
                                                              over(scale[s][:, K:2 * K], D), ALU.mult).then_inc(summed.step("s1"), 1)
                            b = t - 1
                            if inside(b, EG):
                                s = b.slot
                                dve.wait_ge(pe_u.sem, pe_u.at("u", b))
                                if b.follows(2):
                                    dve.wait_ge(written.sems[(b - 2).slot], written.full(b - 2))
                                dve.tensor_tensor(g[s][:, :, :], by_k(pu[s][:, :]), g0[s][:, :, :],
                                                                ALU.add).then_inc(finished.step("g"), 1)
                                dve.wait_ge(finished.sem, finished.at("g", b))
                                if not last:
                                    if b.follows(2):
                                        dve.wait_ge(stores.sems[(b - 2).slot], stores.full(b - 2))
                                dve.tensor_tensor(start[s][:, :, 0, :], g[s][:, :, :],
                                                                over(scale[s][:, K:2 * K], D), ALU.mult).then_inc(finished.step("start"), 1)

                        run(dve, EG, 1, body)

                    @block.tensor
                    def _(pe):
                        def body(t):
                            s = t.slot
                            pe.wait_ge(summed.sem, summed.at("s1", t))
                            if t.follows(2):
                                pe.wait_ge(act_s.sem, act_s.at("sT", t - 2))
                            transposed(pe, ps[s], s1[s]).then_inc(pe_s.step("sT"), 1)
                            pe.wait_ge(act_s.sem, act_s.at("sT", t))
                            if t.follows(2):
                                pe.wait_ge(act_u.sem, act_u.at("uT", t - 2))
                            pe.matmul(pc[s][:, :], W[f"c{layer}"], sT[s][:, :], start=True, stop=True).then_inc(pe_c.step("c"), 1)
                            pe.wait_ge(act_u.sem, act_u.at("uT", t))
                            if t.follows(2):
                                pe.wait_ge(finished.sem, finished.at("g", t - 2))
                            transposed(pe, pu[s], uT[s]).then_inc(pe_u.step("u"), 1)

                        run(pe, EG, 0, body)

                    @block.scalar
                    def _(act):
                        def body(t):
                            s = t.slot
                            act.wait_ge(pe_s.sem, pe_s.at("sT", t))
                            if t.follows(2):
                                act.wait_ge(pe_c.sem, pe_c.at("c", t - 2))
                            act.copy(sT[s][:, :], ps[s][:, :]).then_inc(act_s.step("sT"), 1)
                            act.wait_ge(pe_c.sem, pe_c.at("c", t))
                            if t.follows(2):
                                act.wait_ge(pe_u.sem, pe_u.at("u", t - 2))
                            i = layer + 1
                            act.activation(flat(uT[s][:, :, :]), pc[s][:, :], ACT.Relu,
                                                      bias=bn_bias[:, i:i + 1], scale=bn_scale[:, i:i + 1]).then_inc(act_u.step("uT"), 1)

                        run(act, EG, 0, body)

        def edge_scores():
            ph = Phase("score")
            with ph.ctx:
                index = ph.sb("index", [P, 6 * K], I32)
                dst_row = ph.sb("dst_row", [P, ROWS], I32)
                attr = ph.sb("attr", [65, ROWS])
                dist, nodevec = ph.sb("dist", [2, ROWS]), ph.sb("nodevec", [2, ROWS])
                xs, xd = ph.sb("xs", [P, K, D]), ph.sb("xd", [P, K, D])
                s_norm, d_norm = norm_tiles(ph, "s"), norm_tiles(ph, "d")
                act_n = ph.steps("act_n", "s_dev", "d_dev")
                hs, hd, h = ph.one("hs", [P, K, D]), ph.one("hd", [P, K, D]), ph.sb("h", [P, K, D])
                hsT, hdT = ph.one("hsT", [P, ROWS]), ph.one("hdT", [P, ROWS])
                q, v = ph.one("q", [P, K, D]), ph.sb("v", [P, K, D])
                qk, dot = ph.one("qk", [P, K * HEADS, HEAD_DIM]), ph.one("dot", [P, K * HEADS])
                cT, dT = ph.one("cT", [33, ROWS]), ph.one("dT", [17, ROWS])
                neg, e0, e1, cons = (ph.one(n, [P, K * HEADS]) for n in ("neg", "e0", "e1", "cons"))
                sc0, sc1, score = (ph.one(n, [P, K * HEADS]) for n in ("sc0", "sc1", "score"))
                same, off = ph.one("same", [P, K, P]), ph.one("off", [P, K, P])
                masked = ph.sb("masked", [P, HEADS, P])
                top, less, w = (ph.one(n, [P, K * HEADS]) for n in ("top", "less", "w"))
                old, new = ph.one("old", [P, K, 2, HEADS]), ph.one("new", [P, K, 2, HEADS])
                drop, shrink = ph.one("drop", [P, 2, K, HEADS]), ph.one("shrink", [P, 2, K, HEADS])
                part = ph.one("part", [P, 2, K, HEADS])
                ph_t, pq, pk, pv = ph.bank("ph"), ph.bank("pq"), ph.bank("pk"), ph.bank("pv")
                psm = ph.bank("psm")
                pb = ph.bank("pb", 2)
                ph_m = ph.bank("pm")
                rec_in, fetched = ph.dmas("rec_in", 5), ph.dmas("fetched", 2 * K)
                stores = ph.dmas("stores", 3)
                old_in = [ph.sem(f"old_in{k}") for k in range(K)]
                new_out = [ph.sem(f"new_out{k}") for k in range(K)]
                go, blank = ph.sem("go"), ph.sem("blank")
                dve_h = ph.steps("dve_h", "s_stats", "s_moments", "d_stats", "d_moments", "s_rstd", "hs",
                                 "d_rstd", "hd", "h")
                dve_s = ph.steps("dve_s", "same", "off", "qk", "dot", "neg", "e1", "cons", "sc0", "sc1", "score",
                                 "masked0", "top0", "masked1", "top1", "masked2", "top2", "masked3", "top3",
                                 "less", "newtop", "drop", "part", "new")
                pe_h = ph.steps("pe_h", "hsT", "q", "hdT", "k", "v", "c", "d", "small", "b0", "b1", "b2", "b3",
                                "wsum")
                act_h = ph.steps("act_h", "hsT", "q", "hdT", "v", "cT", "dT", "e0", "w", "shrink")

                def lane_wait(engine, sems, t, k):
                    if not (t.known and t.number < 0):
                        engine.wait_ge(sems[k], 16 * t.number + 16)

                with nc.Block() as block:
                    @block.sync
                    def _(sp):
                        sp.wait_ge(blank, 2)

                        def body(t):
                            s = t.slot
                            if inside(t, EG):
                                if t.follows(2):
                                    sp.wait_ge(dve_s.sem, dve_s.at("same", t - 2))
                                if t.follows(2):
                                    sp.wait_ge(pe_h.sem, pe_h.at("small", t - 2))
                                for k in range(K):
                                    lane_wait(sp, new_out, t - 2, k)
                                sp.dma_start(index[s][:, :], block_of(index_rec, t)).then_inc(rec_in.sems[t.slot], 16)
                                sp.dma_start(
                                    dst_row[s][:, :],
                                    a["dst"][bass.ds(t.number * ROWS, ROWS), :].rearrange("e o -> (e o)")
                                    .partition_broadcast(P)).then_inc(rec_in.sems[t.slot], 16)
                                sp.dma_start(attr[s][:, :], block_of(a["attr"], t, 65)).then_inc(rec_in.sems[t.slot], 16)
                                sp.dma_start(dist[s][:, :], block_of(a["dist"], t, 2)).then_inc(rec_in.sems[t.slot], 16)
                                sp.dma_start(
                                    nodevec[s][0:1, :],
                                    nodevec_e[bass.ds(t.number * ROWS, ROWS), :].rearrange("(o e) u -> o (e u)", o=1)).then_inc(rec_in.sems[t.slot], 16)
                            b = t - 1
                            if inside(b, EG):
                                s = b.slot
                                sp.wait_ge(dve_h.sem, dve_h.at("h", b))
                                sp.dma_start(group(xl_e, b), flat(xd[s][:, :, :])).then_inc(stores.sems[b.slot], 16)
                                sp.dma_start(group(h_e, b), flat(h[s][:, :, :])).then_inc(stores.sems[b.slot], 16)
                                sp.wait_ge(act_h.sem, act_h.at("v", b))
                                sp.dma_start(group(v_e, b), flat(v[s][:, :, :])).then_inc(stores.sems[b.slot], 16)

                        run(sp, EG, 1, body)
                        for t in (EG - 2, EG - 1):
                            sp.wait_ge(stores.sems[(Turn(None, t)).slot], stores.full(Turn(None, t)))

                    @block.gpsimd
                    def _(pool):
                        def body(t):
                            if inside(t, EG):
                                s = t.slot
                                pool.wait_ge(rec_in.sems[t.slot], rec_in.full(t))
                                if t.follows(2):
                                    pool.wait_ge(dve_h.sem, dve_h.at("hs", t - 2))
                                if t.follows(2):
                                    pool.wait_ge(stores.sems[(t - 2).slot], stores.full(t - 2))
                            b = t - 1
                            for k in range(K):
                                if inside(t, EG):
                                    for tile, col in ((xs, SRC), (xd, DST)):
                                        indirect(
                                            pool, go, out=tile[t.slot][:, k, :], out_offset=None, in_=xl_rows,
                                            in_offset=rows_at(index[t.slot][:, col + k:col + k + 1])).then_inc(fetched.sems[t.slot], 16)
                            if inside(b, EG):
                                if b.follows(1):
                                    pool.wait_ge(dve_s.sem, dve_s.at("part", b - 1))
                                for k in range(K):
                                    lane_wait(pool, new_out, b - 1, k)
                                    at = rows_at(index[b.slot][:, SOFT_AT + k:SOFT_AT + k + 1])
                                    indirect(pool, go, out=old[:, k, :, :].rearrange("p t h -> p (t h)"),
                                             out_offset=None, in_=soft, in_offset=at).then_inc(old_in[k], 16)
                                pool.wait_ge(dve_s.sem, dve_s.at("new", b))
                                for k in range(K):
                                    at = rows_at(index[b.slot][:, SOFT_AT + k:SOFT_AT + k + 1])
                                    indirect(pool, go, out=soft, out_offset=at,
                                             in_=new[:, k, :, :].rearrange("p t h -> p (t h)"),
                                             in_offset=None).then_inc(new_out[k], 16)

                        run(pool, EG, 1, body)
                        for k in range(K):
                            lane_wait(pool, new_out, Turn(None, EG - 1), k)

                    @block.vector
                    def _(dve):
                        for s in range(2):
                            dve.memset(nodevec[s][:, :], 1.0).then_inc(blank, 1)

                        def norms(t):
                            s = t.slot
                            dve.wait_ge(fetched.sems[t.slot], fetched.full(t))
                            moments_of(dve, dve_h, t, xs[s], s_norm, ("s_stats", "s_moments"))
                            moments_of(dve, dve_h, t, xd[s], d_norm, ("d_stats", "d_moments"))
                            dve.wait_ge(act_n.sem, act_n.at("s_dev", t))
                            inverted(dve, s_norm).then_inc(dve_h.step("s_rstd"), 1)
                            dve.wait_ge(dve_h.sem, dve_h.at("s_rstd", t))
                            if t.follows(1):
                                dve.wait_ge(pe_h.sem, pe_h.at("hsT", t - 1))
                            normalize(dve, hs, xs[s], s_norm).then_inc(dve_h.step("hs"), 1)
                            dve.wait_ge(act_n.sem, act_n.at("d_dev", t))
                            inverted(dve, d_norm).then_inc(dve_h.step("d_rstd"), 1)
                            dve.wait_ge(dve_h.sem, dve_h.at("d_rstd", t))
                            if t.follows(1):
                                dve.wait_ge(pe_h.sem, pe_h.at("hdT", t - 1))
                            normalize(dve, hd, xd[s], d_norm).then_inc(dve_h.step("hd"), 1)
                            dve.wait_ge(dve_h.sem, dve_h.at("hd", t))
                            if t.follows(2):
                                dve.wait_ge(stores.sems[(t - 2).slot], stores.full(t - 2))
                            dve.tensor_scalar(h[s][:, :, :], hd[:, :, :], 0.0, None, ALU.max).then_inc(dve_h.step("h"), 1)

                        def scores(t):
                            s = t.slot
                            dve.wait_ge(rec_in.sems[t.slot], rec_in.full(t))
                            if t.follows(1):
                                dve.wait_ge(pe_h.sem, pe_h.at("wsum", t - 1))
                            dve.tensor_tensor(
                                same[:, :, :], dst_row[s].rearrange("p (q k) -> p k q", k=K),
                                over(index[s][:, DST:DST + K], P), ALU.is_equal).then_inc(dve_s.step("same"), 1)
                            dve.wait_ge(dve_s.sem, dve_s.at("same", t))
                            dve.tensor_scalar(off[:, :, :], same[:, :, :], -1.0, -LOWEST, ALU.add,
                                                         ALU.mult).then_inc(dve_s.step("off"), 1)
                            dve.wait_ge(act_h.sem, act_h.at("q", t))
                            dve.wait_ge(pe_h.sem, pe_h.at("k", t))
                            dve.tensor_tensor(qk.rearrange("p m d -> p (m d)"), flat(q[:, :, :]),
                                                         pk[:, :], ALU.mult).then_inc(dve_s.step("qk"), 1)
                            dve.wait_ge(dve_s.sem, dve_s.at("qk", t))
                            dve.tensor_reduce(dot[:, :], qk[:, :, :], AX_X, ALU.add).then_inc(dve_s.step("dot"), 1)
                            dve.wait_ge(pe_h.sem, pe_h.at("small", t))
                            if t.follows(1):
                                dve.wait_ge(act_h.sem, act_h.at("e0", t - 1))
                            dve.tensor_scalar(neg[:, :], psm[:, 32:64], -1.0, EXP_MAX, ALU.mult,
                                                         ALU.min).then_inc(dve_s.step("neg"), 1)
                            dve.wait_ge(act_h.sem, act_h.at("e0", t))
                            dve.tensor_scalar(e1[:, :], e0[:, :], 1.0, None, ALU.add).then_inc(dve_s.step("e1"), 1)
                            dve.wait_ge(dve_s.sem, dve_s.at("e1", t))
                            dve.reciprocal(cons[:, :], e1[:, :]).then_inc(dve_s.step("cons"), 1)
                            dve.wait_ge(pe_h.sem, pe_h.at("small", t))
                            dve.scalar_tensor_tensor(sc0[:, :], dot[:, :], HEAD_DIM ** -0.5,
                                                                psm[:, 0:32], ALU.mult, ALU.add).then_inc(dve_s.step("sc0"), 1)
                            dve.wait_ge(dve_s.sem, dve_s.at("sc0", t))
                            dve.tensor_tensor(sc1[:, :], sc0[:, :], cons[:, :], ALU.mult).then_inc(dve_s.step("sc1"), 1)
                            dve.wait_ge(dve_s.sem, dve_s.at("sc1", t))
                            if t.follows(1):
                                dve.wait_ge(pe_h.sem, pe_h.at("b3", t - 1))
                            dve.tensor_tensor(score[:, :], sc1[:, :], psm[:, 64:96], ALU.add).then_inc(dve_s.step("score"), 1)
                            for k in range(K):
                                if k >= 2:
                                    dve.wait_ge(dve_s.sem, dve_s.at(f"top{k - 2}", t))
                                dve.wait_ge(pe_h.sem, pe_h.at(f"b{k}", t))
                                dve.tensor_tensor(
                                    masked[k % 2][:, :, :], pb[:, :].rearrange("p (h q) -> p h q", h=HEADS),
                                    off[:, k, :].unsqueeze(1).to_broadcast([P, HEADS, P]), ALU.add).then_inc(dve_s.step(f"masked{k}"), 1)
                                dve.wait_ge(dve_s.sem, dve_s.at(f"masked{k}", t))
                                dve.tensor_reduce(top[:, k * HEADS:(k + 1) * HEADS], masked[k % 2][:, :, :],
                                                             AX_X, ALU.max).then_inc(dve_s.step(f"top{k}"), 1)
                            dve.wait_ge(dve_s.sem, dve_s.at("top3", t))
                            dve.tensor_tensor(less[:, :], score[:, :], top[:, :], ALU.subtract).then_inc(dve_s.step("less"), 1)
                            for k in range(K):
                                lane_wait(dve, old_in, t, k)
                                lane_wait(dve, new_out, t - 1, k)
                            tops = top[:, :].rearrange("p (k h) -> p k h", k=K)
                            dve.tensor_tensor(new[:, :, 0, :], old[:, :, 0, :], tops, ALU.max).then_inc(dve_s.step("newtop"), 1)
                            dve.wait_ge(dve_s.sem, dve_s.at("newtop", t))
                            dve.tensor_tensor(drop[:, 0, :, :], old[:, :, 0, :], new[:, :, 0, :], ALU.subtract)
                            dve.tensor_tensor(drop[:, 1, :, :], tops, new[:, :, 0, :], ALU.subtract).then_inc(dve_s.step("drop"), 1)
                            dve.wait_ge(act_h.sem, act_h.at("shrink", t))
                            dve.wait_ge(pe_h.sem, pe_h.at("wsum", t))
                            dve.tensor_tensor(part[:, 0, :, :], old[:, :, 1, :], shrink[:, 0, :, :], ALU.mult)
                            dve.tensor_tensor(
                                part[:, 1, :, :], psm[:, 96:128].rearrange("p (k h) -> p k h", k=K),
                                shrink[:, 1, :, :], ALU.mult).then_inc(dve_s.step("part"), 1)
                            dve.wait_ge(dve_s.sem, dve_s.at("part", t))
                            dve.tensor_tensor(new[:, :, 1, :], part[:, 0, :, :], part[:, 1, :, :],
                                                         ALU.add).then_inc(dve_s.step("new"), 1)

                        def body(t):
                            if inside(t, EG):
                                norms(t)
                            if inside(t - 1, EG):
                                scores(t - 1)

                        run(dve, EG, 1, body)

                    @block.scalar
                    def _(act):
                        def body(t):
                            b = t - 1
                            if inside(t, EG):
                                act.wait_ge(dve_h.sem, dve_h.at("s_moments", t))
                                deviation(act, s_norm).then_inc(act_n.step("s_dev"), 1)
                                act.wait_ge(dve_h.sem, dve_h.at("d_moments", t))
                                deviation(act, d_norm).then_inc(act_n.step("d_dev"), 1)
                            if inside(b, EG):
                                s = b.slot
                                act.wait_ge(pe_h.sem, pe_h.at("hsT", b))
                                act.activation(hsT[:, :], ph_t[:, :], ACT.Relu).then_inc(act_h.step("hsT"), 1)
                                act.wait_ge(pe_h.sem, pe_h.at("q", b))
                                if b.follows(1):
                                    act.wait_ge(dve_s.sem, dve_s.at("qk", b - 1))
                                act.copy(flat(q[:, :, :]), pq[:, :]).then_inc(act_h.step("q"), 1)
                                act.wait_ge(pe_h.sem, pe_h.at("hdT", b))
                                act.activation(hdT[:, :], ph_t[:, :], ACT.Relu).then_inc(act_h.step("hdT"), 1)
                                act.wait_ge(pe_h.sem, pe_h.at("v", b))
                                if b.follows(2):
                                    act.wait_ge(stores.sems[(b - 2).slot], stores.full(b - 2))
                                act.copy(flat(v[s][:, :, :]), pv[:, :]).then_inc(act_h.step("v"), 1)
                                act.wait_ge(pe_h.sem, pe_h.at("c", b))
                                act.activation(cT[:, :], pq[0:33, :], ACT.Relu).then_inc(act_h.step("cT"), 1)
                                act.wait_ge(pe_h.sem, pe_h.at("d", b))
                                act.activation(dT[:, :], ph_t[0:17, :], ACT.Relu).then_inc(act_h.step("dT"), 1)
                                act.wait_ge(dve_s.sem, dve_s.at("neg", b))
                                if b.follows(1):
                                    act.wait_ge(dve_s.sem, dve_s.at("e1", b - 1))
                                act.activation(e0[:, :], neg[:, :], ACT.Exp).then_inc(act_h.step("e0"), 1)
                                act.wait_ge(dve_s.sem, dve_s.at("less", b))
                                act.activation(w[:, :], less[:, :], ACT.Exp).then_inc(act_h.step("w"), 1)
                                act.wait_ge(dve_s.sem, dve_s.at("drop", b))
                                act.activation(shrink[:, :, :, :], drop[:, :, :, :], ACT.Exp).then_inc(act_h.step("shrink"), 1)

                        run(act, EG, 1, body)

                    @block.tensor
                    def _(pe):
                        def biased(bank, left, w, bias):
                            pe.matmul(bank[:, :], ones[0:1, :], flat(R[bias])[0:1, :], start=True, stop=False,
                                      skip_group_check=True)
                            for k in range(K):
                                ins = pe.matmul(bank[:, k * D:(k + 1) * D], left[:, k * P:(k + 1) * P], W[w],
                                                start=False, stop=True, skip_group_check=True)
                            return ins

                        def body(t):
                            b = t - 1
                            if inside(b, EG):
                                s = b.slot
                                pe.wait_ge(dve_h.sem, dve_h.at("hs", b))
                                if b.follows(1):
                                    pe.wait_ge(act_h.sem, act_h.at("dT", b - 1))
                                transposed(pe, ph_t, hs).then_inc(pe_h.step("hsT"), 1)
                                pe.wait_ge(act_h.sem, act_h.at("hsT", b))
                                if b.follows(1):
                                    pe.wait_ge(act_h.sem, act_h.at("cT", b - 1))
                                biased(pq, hsT, "l1_q", "bq").then_inc(pe_h.step("q"), 1)
                                pe.wait_ge(dve_h.sem, dve_h.at("hd", b))
                                transposed(pe, ph_t, hd).then_inc(pe_h.step("hdT"), 1)
                                pe.wait_ge(act_h.sem, act_h.at("hdT", b))
                                if b.follows(1):
                                    pe.wait_ge(dve_s.sem, dve_s.at("qk", b - 1))
                                biased(pk, hdT, "l1_k", "bk").then_inc(pe_h.step("k"), 1)
                                if b.follows(1):
                                    pe.wait_ge(act_h.sem, act_h.at("v", b - 1))
                                biased(pv, hdT, "l1_v", "bv").then_inc(pe_h.step("v"), 1)
                                pe.wait_ge(act_h.sem, act_h.at("q", b))
                                pe.wait_ge(rec_in.sems[b.slot], rec_in.full(b))
                                pe.matmul(pq[0:33, :], c1w[:, :], nodevec[s][:, :], start=True, stop=True).then_inc(pe_h.step("c"), 1)
                                pe.matmul(ph_t[0:17, :], d1w[:, :], dist[s][:, :], start=True, stop=True).then_inc(pe_h.step("d"), 1)
                                if b.follows(1):
                                    pe.wait_ge(dve_s.sem, dve_s.at("score", b - 1))
                                if b.follows(1):
                                    pe.wait_ge(dve_s.sem, dve_s.at("part", b - 1))
                                pe.wait_ge(act_h.sem, act_h.at("dT", b))
                                for k in range(K):
                                    h8 = slice(k * HEADS, (k + 1) * HEADS)
                                    pe.matmul(psm[:, 0:32][:, h8], attr[s].rearrange("c (q k) -> c k q", k=K)[:, k, :],
                                              ew[:, :], start=True, stop=True)
                                    pe.matmul(psm[:, 32:64][:, h8], cT.rearrange("c (q k) -> c k q", k=K)[:, k, :],
                                              c2w[:, :], start=True, stop=True)
                                    ins = pe.matmul(psm[:, 64:96][:, h8], dT.rearrange("c (q k) -> c k q", k=K)[:, k, :],
                                                    d2w[:, :], start=True, stop=True)
                                ins.then_inc(pe_h.step("small"), 1)
                                pe.wait_ge(dve_s.sem, dve_s.at("score", b))
                                for k in range(K):
                                    if k:
                                        pe.wait_ge(dve_s.sem, dve_s.at(f"masked{k - 1}", b))
                                    for h in range(HEADS):
                                        at = k * HEADS + h
                                        ins = pe.transpose(pb[:, h * P:(h + 1) * P],
                                                           score[:, at:at + 1].to_broadcast([P, P]), ident[:, :])
                                    ins.then_inc(pe_h.step(f"b{k}"), 1)
                                pe.wait_ge(act_h.sem, act_h.at("w", b))
                                for k in range(K):
                                    ins = pe.matmul(psm[:, 96 + k * HEADS:96 + (k + 1) * HEADS], same[:, k, :],
                                                    w[:, k * HEADS:(k + 1) * HEADS], start=True, stop=True)
                                ins.then_inc(pe_h.step("wsum"), 1)

                        run(pe, EG, 1, body)

        def edge_output():
            ph = Phase("final")
            with ph.ctx:
                index = ph.sb("index", [P, 6 * K], I32)
                lanes = ph.sb("lanes", [P, K, K, 2, HEADS])
                v, h, x = ph.sb("v", [P, K, D]), ph.sb("h", [P, K, D]), ph.sb("x", [P, K, D])
                top, drop, shrink = (ph.one("top", [P, K, HEADS]), ph.one("drop", [P, K, K, HEADS]),
                                     ph.one("shrink", [P, K, K, HEADS]))
                part, total, inverse = (ph.one("part", [P, K, K, HEADS]), ph.one("total", [P, K, HEADS]),
                                        ph.one("inverse", [P, K, HEADS]))
                weight, agg, aT = (ph.one("weight", [P, K, HEADS]), ph.sb("agg", [P, K, D]),
                                   ph.sb("aT", [P, ROWS]))
                z, zn, zg, zb = (ph.one(n, [P, K, D]) for n in ("z", "zn", "zg", "zb"))
                o = ph.sb("o", [P, K, D])
                z_norm, act_z = norm_tiles(ph, "z"), ph.steps("act_z", "dev")
                pa, po = [ph.bank(f"pa{i}") for i in range(2)], [ph.bank(f"po{i}") for i in range(2)]
                rec_in, fetched, written = ph.dmas("rec_in", 4), ph.dmas("fetched", K), ph.dmas("written", K)
                go = ph.sem("go")
                dve_w = ph.steps("dve_w", "top", "drop", "part", "total", "inverse", "weight", "agg")
                dve_o = ph.steps("dve_o", "z", "stats", "moments", "rstd", "zn", "zg", "zb", "o")
                act_e, act_a = ph.steps("act_e", "shrink"), ph.steps("act_a", "aT")
                pe_a, pe_o = ph.steps("pe_a", "aT"), ph.steps("pe_o", "o")

                with nc.Block() as block:
                    @block.sync
                    def _(sp):
                        def body(t):
                            s = t.slot
                            if t.follows(2):
                                sp.wait_ge(dve_o.sem, dve_o.at("o", t - 2))
                            if t.follows(2):
                                sp.wait_ge(written.sems[(t - 2).slot], written.full(t - 2))
                            sp.dma_start(index[s][:, :], block_of(index_rec, t)).then_inc(rec_in.sems[t.slot], 16)
                            for tile, table in ((v, v_e), (h, h_e), (x, xl_e)):
                                sp.dma_start(flat(tile[s][:, :, :]), group(table, t)).then_inc(rec_in.sems[t.slot], 16)

                        run(sp, EG, 0, body)

                    @block.gpsimd
                    def _(pool):
                        def body(t):
                            if inside(t, EG):
                                s = t.slot
                                pool.wait_ge(rec_in.sems[t.slot], rec_in.full(t))
                                if t.follows(2):
                                    pool.wait_ge(dve_w.sem, dve_w.at("part", t - 2))
                                for k in range(K):
                                    indirect(
                                        pool, go, out=lanes[s][:, k, :, :, :].rearrange("p l t h -> p (l t h)"),
                                        out_offset=None,
                                        in_=soft[0:EP * K, :].rearrange("(e l) c -> e (l c)", l=K),
                                        in_offset=rows_at(index[s][:, REP + k:REP + k + 1])).then_inc(fetched.sems[t.slot], 16)
                            b = t - 1
                            if inside(b, EG):
                                pool.wait_ge(dve_o.sem, dve_o.at("o", b))
                                if b.follows(1):
                                    pool.wait_ge(written.sems[(b - 1).slot], written.full(b - 1))
                                for k in range(K):
                                    indirect(
                                        pool, go, out=out,
                                        out_offset=rows_at(index[b.slot][:, WRITE_AT + k:WRITE_AT + k + 1]),
                                        in_=o[b.slot][:, k, :], in_offset=None).then_inc(written.sems[b.slot], 16)

                        run(pool, EG, 1, body)
                        for t in (EG - 2, EG - 1):
                            pool.wait_ge(written.sems[(Turn(None, t)).slot], written.full(Turn(None, t)))

                    @block.vector
                    def _(dve):
                        def weigh(t):
                            s = t.slot
                            dve.wait_ge(rec_in.sems[t.slot], rec_in.full(t))
                            dve.wait_ge(fetched.sems[t.slot], fetched.full(t))
                            tops = lanes[s][:, :, :, 0, :]
                            dve.tensor_reduce(top[:, :, :], tops.rearrange("p k l h -> p k h l"), AX_X,
                                                         ALU.max).then_inc(dve_w.step("top"), 1)
                            dve.wait_ge(dve_w.sem, dve_w.at("top", t))
                            if t.follows(1):
                                dve.wait_ge(act_e.sem, act_e.at("shrink", t - 1))
                            for k in range(K):
                                ins = dve.tensor_tensor(
                                    drop[:, k, :, :], lanes[s][:, k, :, 0, :],
                                    top[:, k, :].unsqueeze(1).to_broadcast([P, K, HEADS]), ALU.subtract)
                            ins.then_inc(dve_w.step("drop"), 1)
                            dve.wait_ge(act_e.sem, act_e.at("shrink", t))
                            dve.tensor_tensor(part[:, :, :, :], lanes[s][:, :, :, 1, :],
                                                         shrink[:, :, :, :], ALU.mult).then_inc(dve_w.step("part"), 1)
                            dve.wait_ge(dve_w.sem, dve_w.at("part", t))
                            dve.tensor_reduce(total[:, :, :], part[:, :, :, :].rearrange("p k l h -> p k h l"),
                                                         AX_X, ALU.add).then_inc(dve_w.step("total"), 1)
                            dve.wait_ge(dve_w.sem, dve_w.at("total", t))
                            dve.reciprocal(inverse[:, :, :], total[:, :, :]).then_inc(dve_w.step("inverse"), 1)
                            dve.wait_ge(dve_w.sem, dve_w.at("inverse", t))
                            dve.tensor_tensor(weight[:, :, :], total[:, :, :], inverse[:, :, :],
                                                         ALU.mult).then_inc(dve_w.step("weight"), 1)
                            dve.wait_ge(dve_w.sem, dve_w.at("weight", t))
                            if t.follows(2):
                                dve.wait_ge(pe_a.sem, pe_a.at("aT", t - 2))
                            dve.tensor_tensor(
                                agg[s].rearrange("p k (h e) -> p (k h) e", h=HEADS),
                                v[s].rearrange("p k (h e) -> p (k h) e", h=HEADS),
                                over(weight.rearrange("p k h -> p (k h)"), HEAD_DIM), ALU.mult).then_inc(dve_w.step("agg"), 1)

                        def finish(t):
                            s = t.slot
                            dve.wait_ge(pe_o.sem, pe_o.at("o", t))
                            dve.tensor_tensor(z[:, :, :], by_k(po[s][:, :]), h[s][:, :, :], ALU.add).then_inc(dve_o.step("z"), 1)
                            dve.wait_ge(dve_o.sem, dve_o.at("z", t))
                            moments_of(dve, dve_o, t, z, z_norm, ("stats", "moments"))
                            dve.wait_ge(act_z.sem, act_z.at("dev", t))
                            inverted(dve, z_norm).then_inc(dve_o.step("rstd"), 1)
                            dve.wait_ge(dve_o.sem, dve_o.at("rstd", t))
                            normalize(dve, zn, z, z_norm).then_inc(dve_o.step("zn"), 1)
                            dve.wait_ge(dve_o.sem, dve_o.at("zn", t))
                            dve.tensor_tensor(zg[:, :, :], zn[:, :, :], R["gamma"], ALU.mult).then_inc(dve_o.step("zg"), 1)
                            dve.wait_ge(dve_o.sem, dve_o.at("zg", t))
                            dve.tensor_tensor(zb[:, :, :], zg[:, :, :], R["beta"], ALU.add).then_inc(dve_o.step("zb"), 1)
                            dve.wait_ge(dve_o.sem, dve_o.at("zb", t))
                            if t.follows(2):
                                dve.wait_ge(written.sems[(t - 2).slot], written.full(t - 2))
                            dve.tensor_tensor(o[s][:, :, :], zb[:, :, :], x[s][:, :, :], ALU.add).then_inc(dve_o.step("o"), 1)

                        def body(t):
                            if inside(t, EG):
                                weigh(t)
                            if inside(t - 1, EG):
                                finish(t - 1)

                        run(dve, EG, 1, body)

                    @block.scalar
                    def _(act):
                        def body(t):
                            if inside(t, EG):
                                act.wait_ge(dve_w.sem, dve_w.at("drop", t))
                                if t.follows(1):
                                    act.wait_ge(dve_w.sem, dve_w.at("part", t - 1))
                                act.activation(shrink[:, :, :, :], drop[:, :, :, :], ACT.Exp).then_inc(act_e.step("shrink"), 1)
                                act.wait_ge(pe_a.sem, pe_a.at("aT", t))
                                if t.follows(2):
                                    act.wait_ge(pe_o.sem, pe_o.at("o", t - 2))
                                act.copy(aT[t.slot][:, :], pa[t.slot][:, :]).then_inc(act_a.step("aT"), 1)
                            b = t - 1
                            if inside(b, EG):
                                act.wait_ge(dve_o.sem, dve_o.at("moments", b))
                                deviation(act, z_norm).then_inc(act_z.step("dev"), 1)

                        run(act, EG, 1, body)

                    @block.tensor
                    def _(pe):
                        def body(t):
                            s = t.slot
                            pe.wait_ge(dve_w.sem, dve_w.at("agg", t))
                            if t.follows(2):
                                pe.wait_ge(act_a.sem, act_a.at("aT", t - 2))
                            transposed(pe, pa[s], agg[s]).then_inc(pe_a.step("aT"), 1)
                            if t.follows(2):
                                pe.wait_ge(dve_o.sem, dve_o.at("z", t - 2))
                            pe.wait_ge(act_a.sem, act_a.at("aT", t))
                            pe.matmul(po[s][:, :], ones[0:1, :], flat(R["bo"])[0:1, :], start=True, stop=False,
                                      skip_group_check=True)
                            for k in range(K):
                                ins = pe.matmul(po[s][:, k * D:(k + 1) * D], aT[s][:, k * P:(k + 1) * P], W["l1_o"],
                                                start=False, stop=True, skip_group_check=True)
                            ins.then_inc(pe_o.step("o"), 1)

                        run(pe, EG, 0, body)

        index_edges()
        dense_first()
        first_rows()
        for layer in range(LAYERS):
            gather_messages(layer)
            update_nodes(layer)
        dense_second()
        dense_third()
        edge_scores()
        edge_output()


def kernel(**inputs):
    import numpy as np
    import concourse.bacc as bacc
    from concourse.bass_utils import run_bass_kernel_spmd

    def arr(name):
        return np.ascontiguousarray(inputs[name])

    n_nodes, n_edges = inputs["x"].shape[0], inputs["src"].shape[0]
    NG = -(-n_nodes // (2 * ROWS)) * 2
    EG = -(-n_edges // (2 * ROWS)) * 2
    NP, EP, SPARE = NG * ROWS, EG * ROWS, ROWS
    assert n_nodes < NP

    def padded(rows, n, fill=0):
        out = np.full((n, *rows.shape[1:]), fill, rows.dtype)
        out[:rows.shape[0]] = rows
        return out

    def groups_T(rows):
        c = rows.shape[1]
        out = np.ones((EG, c + 1, ROWS), np.float32)
        out[:, :c] = padded(rows, EP).reshape(EG, ROWS, c).transpose(0, 2, 1)
        return out.reshape(EG * (c + 1), ROWS)

    def with_one(w, b):
        c = w.shape[1]
        out = np.zeros((2, c + 1), np.float32)
        out[0, :c], out[1, :c], out[1, c] = w[0], b, 1
        return out

    def stacked(w, b):
        return np.concatenate([w, b[None]], 0)

    conv, qkv = arr("L0_gnn_conv_w"), arr("L0_gnn_qkv_w")
    bng, bnb, lng, lnb = (arr("L0_gnn_" + n) for n in ("bn_g", "bn_b", "t_ln_g", "t_ln_b"))
    conv_b = arr("L0_gnn_conv_b")
    columns = [arr("L0_gnn_g_fc_b"), conv_b[0], conv_b[1], conv_b[2], *bng, *bnb, *lng, *lnb]
    k = np.arange(K, dtype=np.float32)[None]
    p = np.arange(P, dtype=np.float32)[:, None]
    spare = k * P + p
    data = {
        "x": padded(arr("x"), NP),
        "node_vec": padded(arr("node_vec1"), NP + SPARE),
        "src": padded(arr("src").reshape(-1, 1), EP, n_nodes),
        "dst": padded(arr("dst").reshape(-1, 1), EP, n_nodes),
        "attr": groups_T(arr("edge_attr_64")),
        "dist": groups_T(arr("edge_weight1")),
        "edge_no": np.arange(1, EP + 1, dtype=np.float32)[:, None],
        "t_w": arr("L0_gnn_t_fc_w"), "g_w": arr("L0_gnn_g_fc_w"), "fc_w": arr("L0_gnn_fc_w"),
        "wq0": qkv[0, 0], "wk0": qkv[0, 1], "wv0": qkv[0, 2],
        "wq1": qkv[1, 0], "wk1": qkv[1, 1], "wv1": qkv[1, 2],
        "c0": conv[0], "c1": conv[1], "c2": conv[2],
        "l1_q": arr("L1_gnn_Wq"), "l1_k": arr("L1_gnn_Wk"), "l1_v": arr("L1_gnn_Wv"), "l1_o": arr("L1_gnn_Wo"),
        "t_b": arr("L0_gnn_t_fc_b"), "fc_b": arr("L0_gnn_fc_b"), "bq": arr("L1_gnn_bq"), "bk": arr("L1_gnn_bk"),
        "bv": arr("L1_gnn_bv"), "bo": arr("L1_gnn_bo"), "gamma": arr("L1_gnn_gamma"), "beta": arr("L1_gnn_beta"),
        "cols": np.stack(columns, 1),
        "c1w": with_one(arr("L1_gnn_Wc1"), arr("L1_gnn_bc1")), "c2w": stacked(arr("L1_gnn_Wc2"), arr("L1_gnn_bc2")),
        "d1w": with_one(arr("L1_gnn_Wd1"), arr("L1_gnn_bd1")), "d2w": stacked(arr("L1_gnn_Wd2"), arr("L1_gnn_bd2")),
        "ew": stacked(arr("L1_gnn_We"), arr("L1_gnn_be")),
        "ident": np.eye(P, dtype=np.float32),
        "before": np.tril(np.ones((P, P), np.float32), -1),
        "spare_node": NP + spare,
        "lane": np.concatenate([k + 0 * p, k % 2 - spare - 2 * EP, k - spare - K * EP, spare], 1),
    }
    nc = bacc.Bacc("TRN2", target_bir_lowering=False, num_devices=1)
    arrays, args = {}, {"n_nodes": n_nodes}
    for name, value in data.items():
        value = np.ascontiguousarray(value)
        arrays[f"in_{name}"] = value
        args[name] = nc.dram_tensor(f"in_{name}", value.shape, mybir.dt.from_np(value.dtype),
                                    kind="ExternalInput").ap()
    out = nc.dram_tensor("out_0", (NP + SPARE, D), F32, kind="ExternalOutput").ap()
    graph_kernel(nc, args, out)
    r = run_bass_kernel_spmd(nc, [arrays], core_ids=[0])
    return r.results[0]["out_0"][:n_nodes]
```

```python
from contextlib import ExitStack

import concourse.bass as bass
from concourse import mybir

ALU = mybir.AluOpType
ACT = mybir.ActivationFunctionType
F32 = mybir.dt.float32
I32 = mybir.dt.int32
AX_X = mybir.AxisListType.X

P = 128
K = 4
ROWS = P * K
D = 128
HEADS = 8
HEAD_DIM = D // HEADS
LAYERS = 3
EPS_LN = 1e-5
EPS_BN = 1e-5
EPS_Q = 1e-6
EXP_MAX = 87.0
TINY = 1e-30
LOWEST = -1e30
REC = 16
SRC, DST, REP, ADD_AT, SOFT_AT, WRITE_AT = range(0, 6 * K, K)


class Turn:

    def __init__(self, reg, offset):
        self.reg, self.offset = reg, offset
        self.slot = offset % 2

    def __sub__(self, n):
        return Turn(self.reg, self.offset - n)

    @property
    def known(self):
        return self.reg is None

    def follows(self, n):
        return not self.known or self.number >= n

    def __add__(self, n):
        return self - -n

    @property
    def count(self):
        return self.number + 1

    @property
    def number(self):
        return self.offset if self.reg is None else 2 * self.reg + self.offset

    @property
    def half(self):
        return self.offset // 2 if self.reg is None else self.reg + self.offset // 2


class Steps:

    def __init__(self, sem, *names):
        self.sem, self.names = sem, names

    def sem_of(self, name):
        return self.sem

    def step(self, name):
        assert name in self.names
        return self.sem

    def at(self, name, turn):
        return turn.number * len(self.names) + self.names.index(name) + 1


class Marks:

    def __init__(self, sems):
        self.sems = sems

    def __getitem__(self, name):
        return self.sems[name]

    sem_of = step = __getitem__

    def at(self, name, turn):
        return turn.count


class Landed:

    def __init__(self, sems, each=1):
        self.sems, self.each = sems, each

    def full(self, turn):
        return 16 * self.each * turn.half + 16 * self.each


def run(engine, groups, lag, body):
    head = (2 + lag + 1) // 2 * 2
    for t in range(min(head, groups + lag)):
        body(Turn(None, t))
    if groups > head:
        with engine.Fori(head // 2, groups // 2) as i:
            for odd in range(2):
                body(Turn(i, odd))
    for t in range(max(groups, head), groups + lag):
        body(Turn(None, t))


def inside(turn, groups):
    return not turn.known or 0 <= turn.number < groups


def graph_kernel(nc, a, out):
    n_nodes = a["n_nodes"]
    NG = a["x"].shape[0] // ROWS
    EG = a["src"].shape[0] // ROWS
    NP, EP = NG * ROWS, EG * ROWS
    SPARE = ROWS
    last_nodes = n_nodes - (NG - 1) * ROWS
    assert NG % 2 == 0 and EG % 2 == 0 and 0 < last_nodes <= ROWS and last_nodes % K == 0
    last_parts = last_nodes // K

    def dram(name, shape, dtype=F32):
        return nc.dram_tensor(name, shape, dtype, kind="Internal").ap()

    node_rec = dram("node_rec", [NP + SPARE, REC])
    g_rows = [dram(f"g{i}_rows", [NP + SPARE, D]) for i in range(LAYERS + 1)]
    t0_T = dram("t0_T", [NG * P, ROWS])
    t1_T = dram("t1_T", [NG * P, ROWS])
    xl_rows = dram("xl_rows", [NP, D])
    first_e = dram("first_e", [EG * P, K])
    index_rec = dram("index_rec", [EG * P, 6 * K], I32)
    scale_rec = dram("scale_rec", [EG * P, 2 * K])
    nodevec_e = dram("nodevec_e", [EP, 1])
    g0_e = dram("g0_e", [EP, D])
    acc = [dram(f"acc{i}", [EP + SPARE // 2, 2 * D]) for i in range(LAYERS)]
    soft = dram("soft", [EP * K + SPARE, 2 * HEADS])
    v_e = dram("v_e", [EP, D])
    h_e = dram("h_e", [EP, D])
    xl_e = dram("xl_e", [EP, D])

    def group(table, turn):
        return table[bass.ds(turn.number * ROWS, ROWS), :].rearrange("(p k) d -> p (k d)", p=P)

    def block_of(table, turn, rows=P):
        return table[bass.ds(turn.number * rows, rows), :]

    def indirect(pool, go, **args):
        pool.sem_inc(go)
        return pool.indirect_dma_start(**args)

    def rows_at(column):
        return bass.IndirectOffsetOnAxis(ap=column, axis=0)

    with ExitStack() as whole:
        def keep(name, shape, dtype=F32):
            return whole.enter_context(nc.sbuf_tensor(name, shape, dtype))

        names = ("t_w", "wq0", "wk0", "wv0", "wq1", "wk1", "wv1", "g_w", "c0", "c1", "c2", "fc_w",
                 "l1_q", "l1_k", "l1_v", "l1_o")
        weights = keep("weights", [P, len(names), D])
        W = {n: weights[:, i, :] for i, n in enumerate(names)}
        rows_names = ("t_b", "fc_b", "bq", "bk", "bv", "bo", "gamma", "beta")
        wide = keep("wide", [P, len(rows_names), K, D])
        R = {n: wide[:, i, :, :] for i, n in enumerate(rows_names)}
        col_names = ("g_b", "cb0", "cb1", "cb2", "bg0", "bg1", "bg2", "bg3", "bb0", "bb1", "bb2", "bb3",
                     "lg0", "lg1", "lg2", "lb0", "lb1", "lb2")
        cols = keep("cols", [P, len(col_names)])
        C = {n: cols[:, i:i + 1] for i, n in enumerate(col_names)}
        bn_bias = keep("bn_bias", [P, LAYERS + 1])
        bn_scale = keep("bn_scale", [P, LAYERS + 1])
        ident = keep("ident", [P, P])
        before = keep("before", [P, K, P])
        spare_node = keep("spare_node", [P, K])
        lane = keep("lane", [P, 4 * K])
        ones = keep("ones", [P, P])
        ATTR, HIDDEN = a["attr"].shape[0] // EG, a["small_w1"].shape[1]
        small_w1 = keep("small_w1", [3, HIDDEN])
        small_w2 = keep("small_w2", [HIDDEN, 3 * HEADS])
        zeros = keep("zeros", [P, K, D])
        eps = keep("eps", [P, 2])
        kv = [keep(f"kv{i}", [P, D + 1]) for i in range(2)]
        passed = whole.enter_context(nc.semaphore("passed"))

        with ExitStack() as ctx:
            def sem(name):
                return ctx.enter_context(nc.semaphore(name))

            fill = ctx.enter_context(nc.sbuf_tensor("fill", [P, (NP + SPARE) // P, REC], F32))
            nodevec = ctx.enter_context(nc.sbuf_tensor("nodevec", [P, (NP + SPARE) // P], F32))
            nosoft = ctx.enter_context(nc.sbuf_tensor("nosoft", [P, (EP * K + SPARE) // P, 2, HEADS], F32))
            landed, filled, stored, scaled = sem("landed"), sem("filled"), sem("stored"), sem("scaled")
            cleared = sem("cleared")
            n_loads = len(names) + K * len(rows_names) + 7 + K
            with nc.Block() as block:
                @block.sync
                def _(sp):
                    n = 0
                    for name in names:
                        sp.dma_start(W[name], a[name]).then_inc(landed, 16)
                        n += 1
                    for name in rows_names:
                        for k in range(K):
                            sp.dma_start(R[name][:, k, :], a[name].partition_broadcast(P)).then_inc(landed, 16)
                            n += 1
                    sp.dma_start(cols[:, :], a["cols"]).then_inc(landed, 16)
                    for tile, name in ((ident, "ident"), (spare_node, "spare_node"), (lane, "lane"),
                                       (small_w1, "small_w1"), (small_w2, "small_w2")):
                        sp.dma_start(tile[:, :], a[name]).then_inc(landed, 16)
                    for k in range(K):
                        sp.dma_start(before[:, k, :], a["before"]).then_inc(landed, 16)
                    sp.dma_start(nodevec[:, :], a["node_vec"].rearrange("(p n) o -> p (n o)", p=P)).then_inc(landed, 16)
                    n += 7 + K
                    assert n == n_loads
                    sp.wait_ge(filled, 1)
                    sp.dma_start(node_rec.rearrange("(p n) r -> p (n r)", p=P),
                                 fill[:, :, :].rearrange("p n r -> p (n r)")).then_inc(stored, 16)
                    sp.wait_ge(cleared, 7)
                    sp.dma_start(soft.rearrange("(p n) r -> p (n r)", p=P),
                                 nosoft[:, :, :, :].rearrange("p n t h -> p (n t h)")).then_inc(stored, 16)
                    for table in acc:
                        sp.dma_start(table[EP:EP + SPARE // 2, :].rearrange("(p n) d -> p (n d)", p=P),
                                     zeros[:, :, :].rearrange("p k d -> p (k d)")).then_inc(stored, 16)
                    sp.wait_ge(stored, 16 * (2 + LAYERS))


                @block.vector
                def _(dve):
                    dve.memset(fill[:, :, :], 0.0).then_inc(cleared, 1)
                    dve.memset(nosoft[:, :, 0, :], LOWEST).then_inc(cleared, 1)
                    dve.memset(nosoft[:, :, 1, :], 0.0).then_inc(cleared, 1)
                    dve.memset(zeros[:, :, :], 0.0).then_inc(cleared, 1)
                    dve.memset(ones[:, :], 1.0).then_inc(cleared, 1)
                    dve.memset(eps[:, 0:1], EPS_LN).then_inc(cleared, 1)
                    dve.memset(eps[:, 1:2], 4 * EPS_LN).then_inc(cleared, 1)
                    dve.wait_ge(cleared, 7)
                    dve.wait_ge(landed, 16 * n_loads)
                    dve.tensor_copy(fill[:, :, 8], nodevec[:, :]).then_inc(filled, 1)
                    for w in ("wq0", "wk0", "wq1", "wk1"):
                        dve.tensor_scalar(W[w], W[w], 1.0 / EPS_Q, None, ALU.mult)
                    dve.tensor_scalar(W["fc_w"], W["fc_w"], 0.5, None, ALU.mult)
                    at = col_names.index("bg0")
                    dve.tensor_scalar(bn_scale[:, :], cols[:, at:at + 4], (1.0 + EPS_BN) ** -0.5, None,
                                      ALU.mult).then_inc(scaled, 1)
                    dve.wait_ge(scaled, 1)
                    dve.tensor_tensor(bn_bias[:, :], cols[:, 0:4], bn_scale[:, :], ALU.mult).then_inc(scaled, 1)
                    dve.wait_ge(scaled, 2)
                    at = col_names.index("bb0")
                    dve.tensor_tensor(bn_bias[:, :], bn_bias[:, :], cols[:, at:at + 4], ALU.add)


        class Phase:

            def __init__(self, name):
                self.name, self.ctx, self.sems = name, ExitStack(), []
                self.ctx.callback(self.clear)

            def clear(self):
                nc.clear_and_free_semaphores(self.sems)
                nc.all_engine_barrier()

            def sb(self, name, shape, dtype=F32):
                return [self.ctx.enter_context(nc.sbuf_tensor(f"{self.name}_{name}{i}", shape, dtype))
                        for i in range(2)]

            def one(self, name, shape, dtype=F32):
                return self.ctx.enter_context(nc.sbuf_tensor(f"{self.name}_{name}", shape, dtype))

            def bank(self, name, banks=1):
                return self.ctx.enter_context(nc.psum_tensor(f"{self.name}_{name}", [P, 512 * banks], F32))

            def sem(self, name):
                self.sems.append(nc.alloc_semaphore(name=f"{self.name}_{name}"))
                return self.sems[-1]

            def steps(self, name, *steps):
                return Steps(self.sem(name), *steps)

            def marks(self, *names):
                return Marks({name: self.sem(name) for name in names})

            def dmas(self, name, each=1):
                return Landed([self.sem(f"{name}{i}") for i in range(2)], each)

        def by_k(tile):
            return tile.rearrange("p (k d) -> p k d", k=K)

        def flat(tile):
            return tile.rearrange("p k d -> p (k d)")

        def over(column, n):
            return column.unsqueeze(2).to_broadcast([P, column.shape[1], n])

        def moments_of(dve, steps, turn, src, norm, names):
            for k in range(K):
                ins = dve.bn_stats(norm["stats"][:, k, :], src[:, k, :])
            ins.then_inc(steps.step(names[0]), 1)
            dve.wait_ge(steps.sem_of(names[0]), steps.at(names[0], turn))
            dve.sem_inc(passed)
            for k in range(K):
                ins = dve.bn_aggr(norm["moments"][:, k, :], norm["stats"][:, k, :])
            ins.then_inc(steps.step(names[1]), 1)

        def deviation(act, norm, column=0):
            return act.activation(norm["dev"][:, :], norm["moments"][:, :, 1], ACT.Sqrt,
                                  bias=eps[:, column:column + 1])

        def norm_tiles(ph, name):
            return {"stats": ph.one(f"{name}_stats", [P, K, 6]), "moments": ph.one(f"{name}_moments", [P, K, 2]),
                    "dev": ph.one(f"{name}_dev", [P, K]), "rstd": ph.one(f"{name}_rstd", [P, K]),
                    "bias": ph.one(f"{name}_bias", [P, K])}

        def normalize(dve, dst, src, norm):
            for k in range(K):
                ins = dve.tensor_scalar(dst[:, k, :], src[:, k, :], norm["moments"][:, k, 0:1],
                                        norm["rstd"][:, k:k + 1], ALU.subtract, ALU.mult)
            return ins

        def inverted(dve, norm):
            return dve.reciprocal(norm["rstd"][:, :], norm["dev"][:, :])

        def transposed(pe, dst, src):
            for k in range(K):
                ins = pe.transpose(dst[:, k * P:(k + 1) * P], src[:, k, :], ident[:, :])
            return ins

        def index_edges():
            ph = Phase("count")
            with ph.ctx:
                dst_col, dst_row = ph.sb("dst_col", [P, K], I32), ph.sb("dst_row", [P, ROWS], I32)
                edge_no = ph.sb("edge_no", [P, K])
                same, earlier = ph.one("same", [P, K, P]), ph.one("earlier", [P, K, P])
                n_earlier, first = ph.one("n_earlier", [P, K]), ph.sb("first", [P, K])
                count = ph.sb("count", [P, K])
                dst_f, node, at = ph.one("dst_f", [P, K]), ph.one("node", [P, K]), ph.one("at", [P, K])
                count_at, edge_at = ph.sb("count_at", [P, K], I32), ph.sb("edge_at", [P, K], I32)
                cols_in, first_out = ph.dmas("cols_in", 3), ph.dmas("first_out")
                found = ph.steps("found", "same", "earlier", "n_earlier", "count", "first", "dst_f", "less",
                                 "picked", "node", "scaled", "count_at", "edge_at")
                counted = [ph.sem(f"counted{k}") for k in range(K)]
                named = [ph.sem(f"named{k}") for k in range(K)]
                go = ph.sem("go")
                rec = node_rec.rearrange("n (r o) -> (n r) o", o=1)

                def done_with(engine, turn):
                    if turn.known and turn.number < 0:
                        return
                    for k in range(K):
                        engine.wait_ge(counted[k], turn.number * 16 + 16)
                        engine.wait_ge(named[k], turn.number * 16 + 16)

                with nc.Block() as block:
                    @block.sync
                    def _(sp):
                        def body(t):
                            s = t.slot
                            if t.follows(2):
                                sp.wait_ge(found.sem, found.at("edge_at", t - 2))
                            done_with(sp, t - 2)
                            sp.dma_start(dst_col[s][:, :], group(a["dst"], t)).then_inc(cols_in.sems[t.slot], 16)
                            sp.dma_start(edge_no[s][:, :], group(a["edge_no"], t)).then_inc(cols_in.sems[t.slot], 16)
                            sp.dma_start(
                                dst_row[s][:, :],
                                a["dst"][bass.ds(t.number * ROWS, ROWS), :].rearrange("e o -> (e o)")
                                .partition_broadcast(P)).then_inc(cols_in.sems[t.slot], 16)

                        run(sp, EG, 0, body)

                    @block.scalar
                    def _(act):
                        def body(t):
                            s = t.slot
                            act.wait_ge(found.sem, found.at("first", t))
                            act.dma_start(block_of(first_e, t), first[s][:, :]).then_inc(first_out.sems[t.slot], 16)

                        run(act, EG, 0, body)
                        act.wait_ge(first_out.sems[Turn(None, EG - 2).slot], first_out.full(Turn(None, EG - 2)))
                        act.wait_ge(first_out.sems[Turn(None, EG - 1).slot], first_out.full(Turn(None, EG - 1)))

                    @block.vector
                    def _(dve):
                        def body(t):
                            s = t.slot
                            dve.wait_ge(cols_in.sems[t.slot], cols_in.full(t))
                            done_with(dve, t - 2)
                            if t.follows(2):
                                dve.wait_ge(first_out.sems[(t - 2).slot], first_out.full(t - 2))
                            dve.tensor_tensor(
                                same[:, :, :], dst_row[s].rearrange("p (q k) -> p k q", k=K),
                                over(dst_col[s][:, :], P), ALU.is_equal).then_inc(found.step("same"), 1)
                            dve.wait_ge(found.sem, found.at("same", t))
                            dve.tensor_tensor(earlier[:, :, :], same[:, :, :], before[:, :, :],
                                                         ALU.mult).then_inc(found.step("earlier"), 1)
                            dve.wait_ge(found.sem, found.at("earlier", t))
                            dve.tensor_reduce(n_earlier[:, :], earlier[:, :, :], AX_X, ALU.add).then_inc(
                                found.step("n_earlier"), 1)
                            dve.tensor_reduce(count[s][:, :], same[:, :, :], AX_X, ALU.add).then_inc(
                                found.step("count"), 1)
                            dve.wait_ge(found.sem, found.at("n_earlier", t))
                            dve.tensor_scalar(first[s][:, :], n_earlier[:, :], 0.0, None,
                                                         ALU.is_equal).then_inc(found.step("first"), 1)
                            dve.tensor_copy(dst_f[:, :], dst_col[s][:, :]).then_inc(found.step("dst_f"), 1)
                            dve.wait_ge(found.sem, found.at("dst_f", t))
                            dve.tensor_tensor(node[:, :], dst_f[:, :], spare_node[:, :],
                                                         ALU.subtract).then_inc(found.step("less"), 1)
                            dve.wait_ge(found.sem, found.at("less", t))
                            dve.tensor_tensor(node[:, :], node[:, :], first[s][:, :], ALU.mult).then_inc(
                                found.step("picked"), 1)
                            dve.wait_ge(found.sem, found.at("picked", t))
                            dve.tensor_tensor(node[:, :], node[:, :], spare_node[:, :], ALU.add).then_inc(
                                found.step("node"), 1)
                            dve.wait_ge(found.sem, found.at("node", t))
                            dve.scalar_tensor_tensor(at[:, :], node[:, :], float(REC), lane[:, 0:K],
                                                                ALU.mult, ALU.add).then_inc(found.step("scaled"), 1)
                            dve.wait_ge(found.sem, found.at("scaled", t))
                            dve.tensor_copy(count_at[s][:, :], at[:, :]).then_inc(found.step("count_at"), 1)
                            dve.tensor_scalar(edge_at[s][:, :], at[:, :], float(K), None, ALU.add).then_inc(
                                found.step("edge_at"), 1)

                        run(dve, EG, 0, body)

                    @block.gpsimd
                    def _(pool):
                        def body(t):
                            s = t.slot
                            pool.wait_ge(found.sem, found.at("edge_at", t))
                            pool.wait_ge(cols_in.sems[t.slot], cols_in.full(t))
                            for k in range(K):
                                if not (t.known and t.number == 0):
                                    pool.wait_ge(counted[k], t.number * 16)
                                    pool.wait_ge(named[k], t.number * 16)
                                indirect(pool, go, out=rec, out_offset=rows_at(count_at[s][:, k:k + 1]),
                                         in_=count[s][:, k:k + 1], in_offset=None,
                                         compute_op=ALU.add).then_inc(counted[k], 16)
                                indirect(pool, go, out=rec, out_offset=rows_at(edge_at[s][:, k:k + 1]),
                                         in_=edge_no[s][:, k:k + 1], in_offset=None).then_inc(named[k], 16)

                        run(pool, EG, 0, body)
                        done_with(pool, Turn(None, EG - 1))

            ph = Phase("recs")
            with ph.ctx:
                src_col, dst_col = ph.sb("src_col", [P, K], I32), ph.sb("dst_col", [P, K], I32)
                edge_no, first = ph.sb("edge_no", [P, K]), ph.sb("first", [P, K])
                src_rec, dst_rec = ph.sb("src_rec", [P, K, REC]), ph.sb("dst_rec", [P, K, REC])
                degree, root = ph.one("degree", [P, 2 * K]), ph.one("root", [P, 2 * K])
                scale = ph.sb("scale", [P, 2 * K])
                rep, mine, dst_f = ph.one("rep", [P, K]), ph.one("mine", [P, K]), ph.one("dst_f", [P, K])
                to_add, to_soft, to_write = (ph.one(n, [P, K]) for n in ("to_add", "to_soft", "to_write"))
                index, nodevec = ph.sb("index", [P, 6 * K], I32), ph.sb("nodevec", [P, K])
                cols_in, out_dmas = ph.dmas("cols_in", 4), ph.dmas("out", 3)
                fetched = [[ph.sem(f"fetched{i}{k}") for k in range(2)] for i in range(2)]
                go = ph.sem("go")
                made = ph.steps("made", "sums", "scale", "rep1", "rep", "mine", "dst_f", "a0", "a1",
                                "a2", "b0", "b1", "b2", "all")
                rooted = ph.steps("rooted", "root")

                def fetched_wait(engine, t):
                    if t.known and t.number < 0:
                        return
                    for i in range(2):
                        engine.wait_ge(fetched[i][t.slot], 64 * t.half + 64)

                with nc.Block() as block:
                    @block.sync
                    def _(sp):
                        def body(t):
                            s = t.slot
                            if t.follows(2):
                                sp.wait_ge(made.sem, made.at("all", t - 2))
                            for tile, table in ((src_col, "src"), (dst_col, "dst"), (edge_no, "edge_no")):
                                sp.dma_start(tile[s][:, :], group(a[table], t)).then_inc(cols_in.sems[t.slot], 16)
                            sp.dma_start(first[s][:, :], block_of(first_e, t)).then_inc(cols_in.sems[t.slot], 16)

                        run(sp, EG, 0, body)

                    @block.gpsimd
                    def _(pool):
                        def body(t):
                            s = t.slot
                            pool.wait_ge(cols_in.sems[t.slot], cols_in.full(t))
                            if t.follows(2):
                                pool.wait_ge(made.sem, made.at("all", t - 2))
                            for i, (rec, col) in enumerate(((src_rec, src_col), (dst_rec, dst_col))):
                                for k in range(K):
                                    indirect(pool, go, out=rec[s][:, k, :], out_offset=None, in_=node_rec,
                                             in_offset=rows_at(col[s][:, k:k + 1])).then_inc(fetched[i][s], 16)

                        run(pool, EG, 0, body)

                    @block.vector
                    def _(dve):
                        def body(t):
                            s = t.slot
                            dve.wait_ge(cols_in.sems[t.slot], cols_in.full(t))
                            fetched_wait(dve, t)
                            if t.follows(2):
                                dve.wait_ge(out_dmas.sems[(t - 2).slot], out_dmas.full(t - 2))
                            dve.tensor_reduce(degree[:, 0:K], src_rec[s][:, :, 0:K], AX_X, ALU.add)
                            dve.tensor_reduce(degree[:, K:2 * K], dst_rec[s][:, :, 0:K], AX_X,
                                                        ALU.add).then_inc(made.step("sums"), 1)
                            dve.wait_ge(made.sem, made.at("sums", t))
                            dve.wait_ge(rooted.sem, rooted.at("root", t))
                            dve.reciprocal(scale[s][:, :], root[:, :]).then_inc(made.step("scale"), 1)
                            dve.tensor_reduce(rep[:, :], dst_rec[s][:, :, K:2 * K], AX_X, ALU.max).then_inc(
                                made.step("rep1"), 1)
                            dve.wait_ge(made.sem, made.at("rep1", t))
                            dve.tensor_scalar(rep[:, :], rep[:, :], -1.0, None, ALU.add).then_inc(made.step("rep"), 1)
                            dve.wait_ge(made.sem, made.at("rep", t))
                            dve.scalar_tensor_tensor(mine[:, :], rep[:, :], 1.0, edge_no[s][:, :],
                                                               ALU.add, ALU.is_equal).then_inc(made.step("mine"), 1)
                            dve.tensor_copy(dst_f[:, :], dst_col[s][:, :]).then_inc(made.step("dst_f"), 1)
                            dve.wait_ge(made.sem, made.at("dst_f", t))
                            dve.scalar_tensor_tensor(to_add[:, :], rep[:, :], 2.0, lane[:, K:2 * K],
                                                     ALU.mult, ALU.add)
                            dve.scalar_tensor_tensor(to_soft[:, :], rep[:, :], float(K), lane[:, 2 * K:3 * K],
                                                     ALU.mult, ALU.add)
                            dve.tensor_tensor(to_write[:, :], dst_f[:, :], spare_node[:, :],
                                                        ALU.subtract).then_inc(made.step("a0"), 1)
                            dve.wait_ge(made.sem, made.at("a0", t))
                            dve.tensor_tensor(to_add[:, :], to_add[:, :], first[s][:, :], ALU.mult)
                            dve.tensor_tensor(to_soft[:, :], to_soft[:, :], first[s][:, :], ALU.mult)
                            dve.tensor_tensor(to_write[:, :], to_write[:, :], mine[:, :], ALU.mult).then_inc(
                                made.step("a1"), 1)
                            dve.wait_ge(made.sem, made.at("a1", t))
                            dve.scalar_tensor_tensor(index[s][:, ADD_AT:ADD_AT + K], to_add[:, :],
                                                     float(2 * EP), lane[:, 3 * K:4 * K], ALU.add, ALU.add)
                            dve.scalar_tensor_tensor(index[s][:, SOFT_AT:SOFT_AT + K], to_soft[:, :],
                                                     float(K * EP), lane[:, 3 * K:4 * K], ALU.add, ALU.add)
                            dve.tensor_tensor(index[s][:, WRITE_AT:WRITE_AT + K], to_write[:, :],
                                                        spare_node[:, :], ALU.add).then_inc(made.step("a2"), 1)
                            dve.tensor_copy(index[s][:, REP:REP + K], rep[:, :]).then_inc(made.step("b0"), 1)
                            dve.tensor_copy(index[s][:, SRC:SRC + K], src_col[s][:, :]).then_inc(made.step("b1"), 1)
                            dve.tensor_copy(index[s][:, DST:DST + K], dst_col[s][:, :]).then_inc(made.step("b2"), 1)
                            dve.tensor_copy(nodevec[s][:, :], dst_rec[s][:, :, 8]).then_inc(made.step("all"), 1)

                        run(dve, EG, 0, body)

                    @block.scalar
                    def _(act):
                        def body(t):
                            s = t.slot
                            act.wait_ge(made.sem, made.at("sums", t))
                            act.activation(root[:, :], degree[:, :], ACT.Sqrt, bias=ones[:, 0:1]).then_inc(
                                rooted.step("root"), 1)
                            act.wait_ge(made.sem, made.at("all", t))
                            act.dma_start(block_of(index_rec, t), index[s][:, :]).then_inc(out_dmas.sems[t.slot], 16)
                            act.dma_start(block_of(scale_rec, t), scale[s][:, :]).then_inc(out_dmas.sems[t.slot], 16)
                            act.dma_start(group(nodevec_e, t), nodevec[s][:, :]).then_inc(out_dmas.sems[t.slot], 16)

                        run(act, EG, 0, body)
                        act.wait_ge(out_dmas.sems[Turn(None, EG - 2).slot], out_dmas.full(Turn(None, EG - 2)))
                        act.wait_ge(out_dmas.sems[Turn(None, EG - 1).slot], out_dmas.full(Turn(None, EG - 1)))

        KV_MARKS = ("k", "v", "k_raw", "k_full", "k_sq", "k_root", "k_norm", "v_scaled", "sum")

        def kv_tiles(ph):
            tiles = {name: ph.one(name, [P, K, D]) for name in ("k_raw", "k", "k_sq")}
            tiles.update({name: ph.one(name, [P, K]) for name in ("k_norm", "k_dev")})
            tiles.update({name: ph.bank(f"p_{name}") for name in ("key", "value", "sum")})
            return {**tiles, "v": ph.one("v", [P, K, D + 1]), "sum": tiles["sum"]}

        def k_project(pe, kvt, done, cur, wk, t):
            pe.wait_ge(done["tT"], t.count)
            if t.follows(1):
                pe.wait_ge(done["k_raw"], (t - 1).count)
            for k in range(K):
                ins = pe.matmul(kvt["key"][:, k * D:(k + 1) * D], cur[:, k * P:(k + 1) * P], W[wk],
                                start=True, stop=True)
            ins.then_inc(done["k"], 1)

        def v_project(pe, kvt, done, cur, wv, t):
            if t.follows(1):
                pe.wait_ge(done["v_scaled"], (t - 1).count)
            for k in range(K):
                ins = pe.matmul(kvt["value"][:, k * D:(k + 1) * D], cur[:, k * P:(k + 1) * P], W[wv],
                                start=True, stop=True)
            ins.then_inc(done["v"], 1)

        def kv_sum(pe, kvt, done, t):
            pe.wait_ge(done["v_scaled"], t.count)
            rows = last_parts if t.known and t.number == NG - 1 else P
            for k in range(K):
                ins = pe.matmul(kvt["sum"][:, 0:D + 1], kvt["k"][0:rows, k, :], kvt["v"][0:rows, k, :],
                                start=t.known and t.number == 0 and k == 0, stop=False, skip_group_check=True)
            ins.then_inc(done["sum"], 1)

        def k_copy(act, kvt, done, t):
            act.wait_ge(done["k"], t.count)
            if t.follows(1):
                act.wait_ge(done["k_full"], (t - 1).count)
            act.copy(flat(kvt["k_raw"][:, :, :]), kvt["key"][:, :]).then_inc(done["k_raw"], 1)

        def kv_guard(dve, kvt, done, t):
            raw = kvt["k_raw"][:, :, :]
            dve.wait_ge(done["k_raw"], t.count)
            if t.follows(1):
                dve.wait_ge(done["sum"], (t - 1).count)
            dve.scalar_tensor_tensor(kvt["k"][:, :, :], raw, 0.0, raw, ALU.is_equal,
                                     ALU.add).then_inc(done["k_full"], 1)
            dve.wait_ge(done["k_full"], t.count)
            for k in range(K):
                ins = dve.tensor_tensor_reduce(kvt["k_sq"][:, k, :], kvt["k"][:, k, :], kvt["k"][:, k, :], 1.0, 0.0,
                                               ALU.mult, ALU.add, kvt["k_norm"][:, k:k + 1])
            ins.then_inc(done["k_sq"], 1)

        def kv_root(act, kvt, done, t):
            act.wait_ge(done["k_sq"], t.count)
            act.activation(kvt["k_dev"][:, :], kvt["k_norm"][:, :], ACT.Sqrt).then_inc(done["k_root"], 1)

        def kv_scale(dve, kvt, done, t):
            dve.wait_ge(done["k_root"], t.count)
            dve.reciprocal(kvt["v"][:, :, D], kvt["k_dev"][:, :]).then_inc(done["k_norm"], 1)
            dve.wait_ge(done["k_norm"], t.count)
            dve.wait_ge(done["v"], t.count)
            dve.tensor_tensor(kvt["v"][:, :, 0:D], by_k(kvt["value"][:, :]), over(kvt["v"][:, :, D], D),
                              ALU.mult).then_inc(done["v_scaled"], 1)

        def dense_first():
            ph = Phase("first")
            with ph.ctx:
                x, x_norm, y_norm = ph.sb("x", [P, K, D]), norm_tiles(ph, "x"), norm_tiles(ph, "y")
                xn, hT = ph.sb("xn", [P, K, D]), ph.sb("hT", [P, ROWS])
                gT = [ph.sb(f"g{i}T", [P, K, P]) for i in range(LAYERS + 1)]
                u = [ph.one(f"u{i}", [P, K, P]) for i in range(LAYERS)]
                rows_out = [ph.sb(f"rows{i}", [P, ROWS]) for i in range(LAYERS + 1)]
                y, yn, tT = ph.one("y", [P, K, D]), ph.sb("yn", [P, K, D]), ph.sb("tT", [P, ROWS])
                p_cols, pt, pr = ph.bank("p_cols"), ph.bank("pt"), ph.bank("pr")
                pg, pc = ph.bank("pg"), ph.bank("pc")
                kvt = kv_tiles(ph)
                x_in, t_out = ph.dmas("x_in"), ph.dmas("t_out")
                g_out = [ph.dmas(f"g{i}_out") for i in range(LAYERS + 1)]
                done = ph.marks("x_stats", "x_moments", "x_dev", "x_rstd", "xn", "xT", "hT", "g", "g0T", "c0", "u0",
                                "g1T", "c1", "u1", "g2T", "c2", "u2", "g3T", "g0r", "g1r", "g2r", "g3r", "g0o",
                                "g1o", "g2o", "g3o", "t", "y", "y_stats", "y_moments", "y_dev", "y_rstd", "yn",
                                "yT", "tT", *KV_MARKS, "kept")

                with nc.Block() as block:
                    @block.sync
                    def _(sp):
                        def store_rows(b, i):
                            sp.wait_ge(done[f"g{i}o"], b.count)
                            sp.dma_start(group(g_rows[i], b), rows_out[i][b.slot][:, :]).then_inc(
                                g_out[i].sems[b.slot], 16)

                        def body(t):
                            if inside(t, NG):
                                if t.follows(2):
                                    sp.wait_ge(done["xn"], (t - 2).count)
                                sp.dma_start(flat(x[t.slot][:, :, :]), group(a["x"], t)).then_inc(
                                    x_in.sems[t.slot], 16)
                            if inside(t - 3, NG):
                                store_rows(t - 3, 0)
                                store_rows(t - 3, 1)
                                store_rows(t - 3, 2)
                                b = t - 3
                                sp.wait_ge(done["tT"], b.count)
                                sp.dma_start(block_of(t0_T, b), tT[b.slot][:, :]).then_inc(t_out.sems[b.slot], 16)
                            if inside(t - 4, NG):
                                store_rows(t - 4, 3)

                        run(sp, NG, 4, body)
                        for t in (Turn(None, NG - 2), Turn(None, NG - 1)):
                            for stream in (*g_out, t_out):
                                sp.wait_ge(stream.sems[t.slot], stream.full(t))

                    @block.vector
                    def _(dve):
                        def x_stats(t):
                            if t.follows(1):
                                dve.wait_ge(done["xn"], (t - 1).count)
                            dve.wait_ge(x_in.sems[t.slot], x_in.full(t))
                            moments_of(dve, done, t, x[t.slot], x_norm, ("x_stats", "x_moments"))

                        def x_scale(t):
                            dve.wait_ge(done["x_dev"], t.count)
                            inverted(dve, x_norm).then_inc(done["x_rstd"], 1)
                            dve.wait_ge(done["x_rstd"], t.count)
                            if t.follows(2):
                                dve.wait_ge(done["xT"], (t - 2).count)
                            normalize(dve, xn[t.slot], x[t.slot], x_norm).then_inc(done["xn"], 1)

                        def y_stats(b):
                            dve.wait_ge(done["t"], b.count)
                            if b.follows(1):
                                dve.wait_ge(done["yn"], (b - 1).count)
                            dve.tensor_tensor(y[:, :, :], by_k(pt[:, :]), R["t_b"], ALU.add).then_inc(done["y"], 1)
                            dve.wait_ge(done["y"], b.count)
                            moments_of(dve, done, b, y, y_norm, ("y_stats", "y_moments"))

                        def y_scale(b):
                            dve.wait_ge(done["y_dev"], b.count)
                            inverted(dve, y_norm).then_inc(done["y_rstd"], 1)
                            dve.wait_ge(done["y_rstd"], b.count)
                            if b.follows(2):
                                dve.wait_ge(done["yT"], (b - 2).count)
                            normalize(dve, yn[b.slot], y, y_norm).then_inc(done["yn"], 1)

                        def body(t):
                            if inside(t - 1, NG):
                                x_scale(t - 1)
                            if inside(t - 3, NG):
                                kv_guard(dve, kvt, done, t - 3)
                            if inside(t, NG):
                                x_stats(t)
                            if inside(t - 3, NG):
                                kv_scale(dve, kvt, done, t - 3)
                            if inside(t - 1, NG):
                                y_stats(t - 1)
                                y_scale(t - 1)

                        run(dve, NG, 3, body)
                        dve.wait_ge(done["sum"], NG)
                        dve.tensor_copy(kv[0][:, :], kvt["sum"][:, 0:D + 1]).then_inc(done["kept"], 1)
                        dve.wait_ge(done["kept"], 1)

                    @block.gpsimd
                    def _(pool):
                        def add(b, i):
                            pool.wait_ge(done[f"u{i - 1}"], b.count)
                            pool.wait_ge(done["g0T"], b.count)
                            if b.follows(2):
                                pool.wait_ge(done[f"g{i}r"], (b - 2).count)
                            if b.follows(2) and i < LAYERS:
                                pool.wait_ge(done[f"c{i}"], (b - 2).count)
                            pool.tensor_tensor(gT[i][b.slot][:, :, :], u[i - 1][:, :, :], gT[0][b.slot][:, :, :],
                                               ALU.add).then_inc(done[f"g{i}T"], 1)

                        def body(t):
                            if inside(t - 3, NG):
                                add(t - 3, 3)
                            if inside(t - 2, NG):
                                add(t - 2, 1)
                                add(t - 2, 2)

                        run(pool, NG, 3, body)

                    @block.scalar
                    def _(act):
                        def out_rows(b, i):
                            act.wait_ge(done[f"g{i}r"], b.count)
                            if b.follows(2):
                                act.wait_ge(g_out[i].sems[b.slot], g_out[i].full(b - 2))
                            act.copy(rows_out[i][b.slot][:, :], pr[:, :]).then_inc(done[f"g{i}o"], 1)

                        def convolved(b, i):
                            act.wait_ge(done[f"c{i}"], b.count)
                            if b.follows(1):
                                act.wait_ge(done[f"g{i + 1}T"], (b - 1).count)
                            act.activation(flat(u[i][:, :, :]), (pc if i else pg)[:, :], ACT.Relu,
                                           bias=bn_bias[:, i + 1:i + 2],
                                           scale=bn_scale[:, i + 1:i + 2]).then_inc(done[f"u{i}"], 1)

                        def g_first(b):
                            act.wait_ge(done["g"], b.count)
                            if b.follows(2):
                                act.wait_ge(done["g3T"], (b - 2).count)
                                act.wait_ge(done["g0r"], (b - 2).count)
                                act.wait_ge(done["c0"], (b - 2).count)
                            act.activation(flat(gT[0][b.slot][:, :, :]), pg[:, :], ACT.Relu,
                                           bias=bn_bias[:, 0:1], scale=bn_scale[:, 0:1]).then_inc(done["g0T"], 1)

                        def h_first(b):
                            act.wait_ge(done["xT"], b.count)
                            if b.follows(2):
                                act.wait_ge(done["t"], (b - 2).count)
                            act.activation(hT[b.slot][:, :], p_cols[:, :], ACT.Relu).then_inc(done["hT"], 1)

                        def t_first(b):
                            act.wait_ge(done["yT"], b.count)
                            if b.follows(2):
                                act.wait_ge(t_out.sems[b.slot], t_out.full(b - 2))
                                act.wait_ge(done["v"], (b - 2).count)
                            act.activation(tT[b.slot][:, :], p_cols[:, :], ACT.Relu,
                                           bias=C["lb0"], scale=C["lg0"]).then_inc(done["tT"], 1)

                        def body(t):
                            if inside(t - 1, NG):
                                act.wait_ge(done["x_moments"], (t - 1).count)
                                deviation(act, x_norm).then_inc(done["x_dev"], 1)
                            if inside(t - 2, NG):
                                out_rows(t - 2, 0)
                                convolved(t - 2, 1)
                            if inside(t - 3, NG):
                                out_rows(t - 3, 3)
                            if inside(t - 2, NG):
                                t_first(t - 2)
                            if inside(t - 1, NG):
                                h_first(t - 1)
                            if inside(t - 2, NG):
                                out_rows(t - 2, 1)
                            if inside(t - 3, NG):
                                kv_root(act, kvt, done, t - 3)
                            if inside(t - 2, NG):
                                convolved(t - 2, 2)
                            if inside(t - 1, NG):
                                g_first(t - 1)
                                convolved(t - 1, 0)
                            if inside(t - 2, NG):
                                out_rows(t - 2, 2)
                            if inside(t - 1, NG):
                                act.wait_ge(done["y_moments"], (t - 1).count)
                                deviation(act, y_norm).then_inc(done["y_dev"], 1)
                            if inside(t - 2, NG):
                                k_copy(act, kvt, done, t - 2)

                        run(act, NG, 3, body)

                    @block.tensor
                    def _(pe):
                        def product(bank, w, right):
                            return pe.matmul(bank[:, :], W[w], right, start=True, stop=True)

                        def to_rows(b, i):
                            pe.wait_ge(done[f"g{i}T"], b.count)
                            transposed(pe, pr, gT[i][b.slot]).then_inc(done[f"g{i}r"], 1)

                        def body(t):
                            d, c, b = t - 3, t - 2, t - 1
                            if inside(d, NG):
                                if inside(d + 1, NG):
                                    pe.wait_ge(done["g0o"], (d + 1).count)
                                else:
                                    pe.wait_ge(done["g2o"], d.count)
                                to_rows(d, 3)
                            if inside(c, NG):
                                pe.wait_ge(done["yn"], c.count)
                                pe.wait_ge(done["hT"], c.count)
                                transposed(pe, p_cols, yn[c.slot]).then_inc(done["yT"], 1)
                            if inside(t - 4, NG):
                                kv_sum(pe, kvt, done, t - 4)
                            if inside(c, NG):
                                if c.follows(1):
                                    pe.wait_ge(done["g3o"], (c - 1).count)
                                else:
                                    pe.wait_ge(done["g0o"], c.count)
                                to_rows(c, 1)
                            if inside(b, NG):
                                pe.wait_ge(done["xn"], b.count)
                                if b.follows(1):
                                    pe.wait_ge(done["tT"], (b - 1).count)
                                transposed(pe, p_cols, xn[b.slot]).then_inc(done["xT"], 1)
                            if inside(c, NG):
                                pe.wait_ge(done["g2T"], c.count)
                                pe.wait_ge(done["u1"], c.count)
                                product(pc, "c2", flat(gT[2][c.slot][:, :, :])).then_inc(done["c2"], 1)
                            if inside(b, NG):
                                pe.wait_ge(done["hT"], b.count)
                                if b.follows(1):
                                    pe.wait_ge(done["u0"], (b - 1).count)
                                product(pg, "g_w", hT[b.slot][:, :]).then_inc(done["g"], 1)
                                if b.follows(1):
                                    pe.wait_ge(done["y"], (b - 1).count)
                                for k in range(K):
                                    ins = pe.matmul(pt[:, k * D:(k + 1) * D], hT[b.slot][:, k * P:(k + 1) * P],
                                                    W["t_w"], start=True, stop=True)
                                ins.then_inc(done["t"], 1)
                                pe.wait_ge(done["g0T"], b.count)
                                product(pg, "c0", flat(gT[0][b.slot][:, :, :])).then_inc(done["c0"], 1)
                            if inside(c, NG):
                                pe.wait_ge(done["g1o"], c.count)
                                to_rows(c, 2)
                                k_project(pe, kvt, done, tT[c.slot], "wk0", c)
                                v_project(pe, kvt, done, tT[c.slot], "wv0", c)
                            if inside(b, NG):
                                if b.follows(1):
                                    pe.wait_ge(done["g2o"], (b - 1).count)
                                to_rows(b, 0)
                                pe.wait_ge(done["g1T"], b.count)
                                if b.follows(1):
                                    pe.wait_ge(done["u2"], (b - 1).count)
                                product(pc, "c1", flat(gT[1][b.slot][:, :, :])).then_inc(done["c1"], 1)

                        run(pe, NG, 4, body)
        ATTEND_MARKS = ("q", "rows", "u", "norms", "q_raw", "q_full", "q_sq", "q_dev", "rows_out", "den", "wkv", "weights", "t", "y", "y_stats", "y_moments", "y_dev", "y_rstd",
                        "y_bias", "yn", "yT", "tT")

        def attend_tiles(ph):
            tiles = {name: ph.sb(name, [P, K, D]) for name in ("qT", "rows", "yn")}
            tiles.update({name: ph.one(name, [P, K, D]) for name in ("q_raw", "q_sq", "t", "y")})
            tiles.update({name: ph.one(name, [P, K]) for name in ("den", "wkv", "wv", "q_dev")})
            tiles.update({name: ph.bank(name) for name in ("pq", "pn", "pv", "pu", "py")})
            return {**tiles, "cT": ph.sb("cT", [P, ROWS]), "norm": norm_tiles(ph, "y")}

        def biased_rstd(dve, done, t, norm, dev, rstd, bias, used):
            dve.wait_ge(done[dev], t.count)
            if t.follows(1):
                dve.wait_ge(done[used], (t - 1).count)
            inverted(dve, norm).then_inc(done[rstd], 1)
            dve.wait_ge(done[rstd], t.count)
            dve.scalar_tensor_tensor(norm["bias"][:, :], norm["moments"][:, :, 0], -1.0, norm["rstd"][:, :],
                                     ALU.mult, ALU.mult).then_inc(done[bias], 1)

        def scaled_rows(act, dst, src, norm, function):
            for k in range(K):
                ins = act.activation(dst[:, k, :], src[:, k, :], function, bias=norm["bias"][:, k:k + 1],
                                     scale=norm["rstd"][:, k:k + 1])
            return ins

        def pe_q(pe, at, layer, c_in, done, t):
            pe.wait_ge(c_in.sems[t.slot], c_in.full(t))
            if t.follows(1):
                pe.wait_ge(done["rows_out"], (t - 1).count)
            pe.matmul(at["pq"][:, :], W[f"wq{layer}"], at["cT"][t.slot][:, :], start=True,
                      stop=True).then_inc(done["q"], 1)

        def pe_rows(pe, at, done, t):
            pe.wait_ge(done["q_raw"], t.count)
            transposed(pe, at["pq"], by_k(at["cT"][t.slot][:, :])).then_inc(done["rows"], 1)

        def pe_yT(pe, at, done, b):
            if b.follows(1):
                pe.wait_ge(done["tT"], (b - 1).count)
            pe.wait_ge(done["yn"], b.count)
            transposed(pe, at["py"], at["yn"][b.slot]).then_inc(done["yT"], 1)

        def pe_v(pe, at, layer, done, t):
            if t.follows(1):
                pe.wait_ge(done["y"], (t - 1).count)
            for k in range(K):
                ins = pe.matmul(at["pv"][:, k * D:(k + 1) * D], at["cT"][t.slot][:, k * P:(k + 1) * P],
                                W[f"wv{layer}"], start=True, stop=True)
            ins.then_inc(done["av"], 1)

        def pe_u(pe, at, kvs, done, t):
            pe.wait_ge(done["q_full"], t.count)
            if t.follows(1):
                pe.wait_ge(done["t"], (t - 1).count)
            for k in range(K):
                ins = pe.matmul(at["pu"][:, k * D:(k + 1) * D], at["qT"][t.slot][:, k, :], kvs[:, 0:D],
                                start=True, stop=True)
            ins.then_inc(done["u"], 1)

        def pe_norms(pe, at, kvs, done, t):
            pe.wait_ge(done["q_full"], t.count)
            pe.wait_ge(done["q_sq"], t.count)
            if t.follows(1):
                pe.wait_ge(done["den"], (t - 1).count)
            for k in range(K):
                pe.matmul(at["pn"][:, K + k:K + k + 1], at["qT"][t.slot][:, k, :], kvs[:, D:D + 1],
                          start=True, stop=True)
                ins = pe.matmul(at["pn"][:, k:k + 1], at["q_sq"][:, k, :], ones[:, 0:1], start=True, stop=True)
            ins.then_inc(done["norms"], 1)

        def act_q_raw(act, at, done, t):
            act.wait_ge(done["q"], t.count)
            if t.follows(1):
                act.wait_ge(done["q_full"], (t - 1).count)
            act.copy(flat(at["q_raw"][:, :, :]), at["pq"][:, :]).then_inc(done["q_raw"], 1)

        def act_rows(act, at, done, t):
            act.wait_ge(done["rows"], t.count)
            if t.follows(2):
                act.wait_ge(done["t"], (t - 2).count)
            act.copy(flat(at["rows"][t.slot][:, :, :]), at["pq"][:, :]).then_inc(done["rows_out"], 1)

        def act_q_sq(act, at, done, t):
            act.wait_ge(done["q_full"], t.count)
            if t.follows(1):
                act.wait_ge(done["norms"], (t - 1).count)
            act.activation(at["q_sq"][:, :, :], at["qT"][t.slot][:, :, :], ACT.Square).then_inc(done["q_sq"], 1)

        def act_q_dev(act, at, done, t):
            act.wait_ge(done["norms"], t.count)
            if t.follows(1):
                act.wait_ge(done["weights"], (t - 1).count)
            act.activation(at["q_dev"][:, :], at["pn"][:, 0:K], ACT.Sqrt).then_inc(done["q_dev"], 1)

        def act_y_dev(act, at, done, b):
            act.wait_ge(done["y_moments"], b.count)
            deviation(act, at["norm"], 1).then_inc(done["y_dev"], 1)

        def act_yn(act, at, done, b):
            act.wait_ge(done["y_bias"], b.count)
            if b.follows(2):
                act.wait_ge(done["yT"], (b - 2).count)
            scaled_rows(act, at["yn"][b.slot], at["y"], at["norm"], ACT.Identity).then_inc(done["yn"], 1)

        def dve_q_full(dve, at, done, t):
            dve.wait_ge(done["q_raw"], t.count)
            if t.follows(2):
                dve.wait_ge(done["u"], (t - 2).count)
                dve.wait_ge(done["norms"], (t - 2).count)
            raw = at["q_raw"][:, :, :]
            dve.scalar_tensor_tensor(at["qT"][t.slot][:, :, :], raw, 0.0, raw, ALU.is_equal,
                                        ALU.add).then_inc(done["q_full"], 1)

        def dve_weights(dve, at, done, t):
            dve.wait_ge(done["q_dev"], t.count)
            dve.scalar_tensor_tensor(at["den"][:, :], at["q_dev"][:, :], float(n_nodes), at["pn"][:, K:2 * K],
                                     ALU.mult, ALU.add).then_inc(done["den"], 1)
            dve.wait_ge(done["den"], t.count)
            if t.follows(1):
                dve.wait_ge(done["y"], (t - 1).count)
            dve.reciprocal(at["wkv"][:, :], at["den"][:, :]).then_inc(done["wkv"], 1)
            dve.wait_ge(done["wkv"], t.count)
            dve.scalar_tensor_tensor(at["wv"][:, :], at["q_dev"][:, :], float(n_nodes), at["wkv"][:, :],
                                     ALU.mult, ALU.mult).then_inc(done["weights"], 1)

        def dve_t(dve, at, done, t):
            dve.wait_ge(done["weights"], t.count)
            dve.wait_ge(done["u"], t.count)
            dve.wait_ge(done["rows_out"], t.count)
            for k in range(K):
                ins = dve.scalar_tensor_tensor(at["t"][:, k, :], at["pu"][:, k * D:(k + 1) * D], at["wkv"][:, k:k + 1],
                                               at["rows"][t.slot][:, k, :], ALU.mult, ALU.add)
            ins.then_inc(done["t"], 1)

        def dve_y(dve, at, done, b):
            dve.wait_ge(done["t"], b.count)
            dve.wait_ge(done["av"], b.count)
            if b.follows(1):
                dve.wait_ge(done["yn"], (b - 1).count)
            for k in range(K):
                ins = dve.scalar_tensor_tensor(at["y"][:, k, :], at["pv"][:, k * D:(k + 1) * D], at["wv"][:, k:k + 1],
                                               at["t"][:, k, :], ALU.mult, ALU.add)
            ins.then_inc(done["y"], 1)
            dve.wait_ge(done["y"], b.count)
            moments_of(dve, done, b, at["y"], at["norm"], ("y_stats", "y_moments"))

        def dve_y_rstd(dve, at, done, b):
            biased_rstd(dve, done, b, at["norm"], "y_dev", "y_rstd", "y_bias", "yn")

        def dense_second():
            ph = Phase("second")
            with ph.ctx:
                at, kvt = attend_tiles(ph), kv_tiles(ph)
                tT = ph.sb("tT", [P, ROWS])
                c_in, t_out = ph.dmas("c_in"), ph.dmas("t_out")
                done = ph.marks(*dict.fromkeys(ATTEND_MARKS + KV_MARKS + ("av", "kept")))

                with nc.Block() as block:
                    @block.sync
                    def _(sp):
                        def body(t):
                            if inside(t, NG):
                                if t.follows(2):
                                    sp.wait_ge(done["av"], (t - 2).count)
                                    sp.wait_ge(done["rows"], (t - 2).count)
                                sp.dma_start(at["cT"][t.slot][:, :], block_of(t0_T, t)).then_inc(c_in.sems[t.slot], 16)
                            b = t - 3
                            if inside(b, NG):
                                sp.wait_ge(done["tT"], b.count)
                                sp.dma_start(block_of(t1_T, b), tT[b.slot][:, :]).then_inc(t_out.sems[b.slot], 16)

                        run(sp, NG, 3, body)
                        for t in (Turn(None, NG - 2), Turn(None, NG - 1)):
                            sp.wait_ge(t_out.sems[t.slot], t_out.full(t))

                    @block.tensor
                    def _(pe):
                        def body(t):
                            if inside(t - 2, NG):
                                k_project(pe, kvt, done, tT[t.slot], "wk1", t - 2)
                            if inside(t, NG):
                                pe_q(pe, at, 0, c_in, done, t)
                                pe_rows(pe, at, done, t)
                            if inside(t - 3, NG):
                                kv_sum(pe, kvt, done, t - 3)
                            if inside(t - 2, NG):
                                v_project(pe, kvt, done, tT[t.slot], "wv1", t - 2)
                            if inside(t, NG):
                                pe_u(pe, at, kv[0], done, t)
                                pe_norms(pe, at, kv[0], done, t)
                            if inside(t - 1, NG):
                                pe_yT(pe, at, done, t - 1)
                            if inside(t, NG):
                                pe_v(pe, at, 0, done, t)

                        run(pe, NG, 3, body)

                    @block.scalar
                    def _(act):
                        def body(t):
                            c = t - 2
                            if inside(c, NG):
                                act.wait_ge(done["yT"], c.count)
                                if c.follows(2):
                                    act.wait_ge(t_out.sems[c.slot], t_out.full(c - 2))
                                    act.wait_ge(done["v"], (c - 2).count)
                                act.activation(tT[c.slot][:, :], at["py"][:, :], ACT.Relu,
                                               bias=C["lb1"], scale=C["lg1"]).then_inc(done["tT"], 1)
                            if inside(t, NG):
                                act_q_raw(act, at, done, t)
                            if inside(c, NG):
                                k_copy(act, kvt, done, c)
                            if inside(t, NG):
                                act_rows(act, at, done, t)
                            if inside(t - 1, NG):
                                act_y_dev(act, at, done, t - 1)
                            if inside(t, NG):
                                act_q_sq(act, at, done, t)
                            if inside(t - 1, NG):
                                act_yn(act, at, done, t - 1)
                            if inside(c, NG):
                                kv_root(act, kvt, done, c)
                            if inside(t, NG):
                                act_q_dev(act, at, done, t)

                        run(act, NG, 2, body)

                    @block.vector
                    def _(dve):
                        def body(t):
                            b, c = t - 1, t - 2
                            if inside(b, NG):
                                dve_weights(dve, at, done, b)
                                dve_t(dve, at, done, b)
                                dve_y(dve, at, done, b)
                            if inside(t, NG):
                                dve_q_full(dve, at, done, t)
                            if inside(c, NG):
                                kv_guard(dve, kvt, done, c)
                            if inside(b, NG):
                                dve_y_rstd(dve, at, done, b)
                            if inside(c, NG):
                                kv_scale(dve, kvt, done, c)

                        run(dve, NG, 2, body)
                        dve.wait_ge(done["sum"], NG)
                        dve.tensor_copy(kv[1][:, :], kvt["sum"][:, 0:D + 1]).then_inc(done["kept"], 1)
                        dve.wait_ge(done["kept"], 1)

        def dense_third():
            ph = Phase("third")
            with ph.ctx:
                at = attend_tiles(ph)
                x, x2 = ph.sb("x", [P, K, D]), ph.sb("x2", [P, K, D])
                tT, sT = ph.one("tT", [P, ROWS]), ph.one("sT", [P, ROWS])
                xb, xl = ph.one("xb", [P, K, D]), ph.sb("xl", [P, K, D])
                h, z, zn, zg = (ph.one(n, [P, K, D]) for n in ("h", "z", "zn", "zg"))
                xlb, o = ph.sb("xlb", [P, K, D]), ph.sb("o", [P, K, D])
                x_norm, z_norm = norm_tiles(ph, "x"), norm_tiles(ph, "z")
                px, po = ph.bank("px"), ph.bank("po")
                c_in, x_in, x2_in = ph.dmas("c_in"), ph.dmas("x_in"), ph.dmas("x2_in")
                xl_out, o_out = ph.dmas("xl_out"), ph.dmas("o_out")
                done = ph.marks(*ATTEND_MARKS, "av", "x2T", "fc", "sT", "xb", "xl", "xl_stats", "xl_moments", "dev",
                                "rstd", "bias", "h", "z", "z_stats", "z_moments", "z_dev", "z_rstd", "z_bias", "zn",
                                "zg", "xlb", "o")

                with nc.Block() as block:
                    @block.sync
                    def _(sp):
                        def body(t):
                            if inside(t, NG):
                                if t.follows(2):
                                    sp.wait_ge(done["av"], (t - 2).count)
                                    sp.wait_ge(done["rows"], (t - 2).count)
                                sp.dma_start(at["cT"][t.slot][:, :], block_of(t1_T, t)).then_inc(c_in.sems[t.slot], 16)
                            b = t - 1
                            if inside(b, NG):
                                if b.follows(2):
                                    sp.wait_ge(done["x2T"], (b - 2).count)
                                sp.dma_start(flat(x2[b.slot][:, :, :]), group(g_rows[LAYERS], b)).then_inc(
                                    x2_in.sems[b.slot], 16)
                                if b.follows(2):
                                    sp.wait_ge(done["xb"], (b - 2).count)
                                sp.dma_start(flat(x[b.slot][:, :, :]), group(a["x"], b)).then_inc(
                                    x_in.sems[b.slot], 16)
                            d = t - 3
                            if inside(d, NG):
                                sp.wait_ge(done["xl"], d.count)
                                sp.dma_start(group(xl_rows, d), flat(xl[d.slot][:, :, :])).then_inc(
                                    xl_out.sems[d.slot], 16)
                            f = t - 5
                            if inside(f, NG):
                                sp.wait_ge(done["o"], f.count)
                                sp.dma_start(group(out, f), flat(o[f.slot][:, :, :])).then_inc(o_out.sems[f.slot], 16)

                        run(sp, NG, 5, body)
                        for t in (Turn(None, NG - 2), Turn(None, NG - 1)):
                            sp.wait_ge(xl_out.sems[t.slot], xl_out.full(t))
                            sp.wait_ge(o_out.sems[t.slot], o_out.full(t))

                    @block.tensor
                    def _(pe):
                        def body(t):
                            b, c = t - 1, t - 2
                            if inside(b, NG):
                                pe_v(pe, at, 1, done, b)
                            if inside(t, NG):
                                pe_q(pe, at, 1, c_in, done, t)
                            if inside(b, NG):
                                pe.wait_ge(x2_in.sems[b.slot], x2_in.full(b))
                                if b.follows(1):
                                    pe.wait_ge(done["sT"], (b - 1).count)
                                transposed(pe, px, x2[b.slot]).then_inc(done["x2T"], 1)
                            if inside(c, NG):
                                pe.wait_ge(done["sT"], c.count)
                                if c.follows(1):
                                    pe.wait_ge(done["xl"], (c - 1).count)
                                for k in range(K):
                                    ins = pe.matmul(po[:, k * D:(k + 1) * D], sT[:, k * P:(k + 1) * P], W["fc_w"],
                                                    start=True, stop=True)
                                ins.then_inc(done["fc"], 1)
                            if inside(t, NG):
                                pe_rows(pe, at, done, t)
                                pe_norms(pe, at, kv[1], done, t)
                                pe_u(pe, at, kv[1], done, t)
                            if inside(b, NG):
                                pe_yT(pe, at, done, b)

                        run(pe, NG, 2, body)

                    @block.scalar
                    def _(act):
                        def body(t):
                            b, c, d = t - 1, t - 2, t - 3
                            if inside(t, NG):
                                act_q_raw(act, at, done, t)
                                act_q_sq(act, at, done, t)
                            if inside(b, NG):
                                act_y_dev(act, at, done, b)
                            if inside(t, NG):
                                act_rows(act, at, done, t)
                                act_q_dev(act, at, done, t)
                            if inside(c, NG):
                                act.wait_ge(done["xl_moments"], c.count)
                                deviation(act, x_norm).then_inc(done["dev"], 1)
                            if inside(b, NG):
                                act_yn(act, at, done, b)
                            if inside(d, NG):
                                act.wait_ge(done["z_moments"], d.count)
                                deviation(act, z_norm).then_inc(done["z_dev"], 1)
                            if inside(b, NG):
                                act.wait_ge(done["yT"], b.count)
                                if b.follows(1):
                                    act.wait_ge(done["sT"], (b - 1).count)
                                act.activation(tT[:, :], at["py"][:, :], ACT.Relu,
                                               bias=C["lb2"], scale=C["lg2"]).then_inc(done["tT"], 1)
                            if inside(c, NG):
                                act.wait_ge(done["bias"], c.count)
                                if c.follows(1):
                                    act.wait_ge(done["z"], (c - 1).count)
                                scaled_rows(act, h, xl[c.slot], x_norm, ACT.Relu).then_inc(done["h"], 1)
                            if inside(d, NG):
                                act.wait_ge(done["z_bias"], d.count)
                                if d.follows(1):
                                    act.wait_ge(done["zg"], (d - 1).count)
                                scaled_rows(act, zn, z, z_norm, ACT.Identity).then_inc(done["zn"], 1)

                        run(act, NG, 3, body)

                    @block.gpsimd
                    def _(pool):
                        def body(t):
                            b, d, e, f = t - 1, t - 3, t - 4, t - 5
                            if inside(e, NG):
                                pool.wait_ge(done["xl"], e.count)
                                if e.follows(2):
                                    pool.wait_ge(done["o"], (e - 2).count)
                                pool.tensor_tensor(xlb[e.slot][:, :, :], xl[e.slot][:, :, :], R["beta"],
                                                   ALU.add).then_inc(done["xlb"], 1)
                            if inside(d, NG):
                                pool.wait_ge(done["h"], d.count)
                                if d.follows(1):
                                    pool.wait_ge(done["zn"], (d - 1).count)
                                pool.tensor_tensor(z[:, :, :], h[:, :, :], R["bo"], ALU.add).then_inc(done["z"], 1)
                            if inside(f, NG):
                                pool.wait_ge(done["zg"], f.count)
                                pool.wait_ge(done["xlb"], f.count)
                                if f.follows(2):
                                    pool.wait_ge(o_out.sems[f.slot], o_out.full(f - 2))
                                pool.tensor_tensor(o[f.slot][:, :, :], zg[:, :, :], xlb[f.slot][:, :, :],
                                                  ALU.add).then_inc(done["o"], 1)
                            if inside(e, NG):
                                pool.wait_ge(done["zn"], e.count)
                                if e.follows(1):
                                    pool.wait_ge(done["o"], (e - 1).count)
                                pool.tensor_tensor(zg[:, :, :], zn[:, :, :], R["gamma"],
                                                   ALU.mult).then_inc(done["zg"], 1)
                            if inside(b, NG):
                                pool.wait_ge(x_in.sems[b.slot], x_in.full(b))
                                if b.follows(1):
                                    pool.wait_ge(done["xl"], (b - 1).count)
                                pool.tensor_tensor(xb[:, :, :], x[b.slot][:, :, :], R["fc_b"],
                                                   ALU.add).then_inc(done["xb"], 1)

                        run(pool, NG, 5, body)

                    @block.vector
                    def _(dve):
                        def body(t):
                            b, c, d = t - 1, t - 2, t - 3
                            if inside(b, NG):
                                dve_y(dve, at, done, b)
                            if inside(t, NG):
                                dve_q_full(dve, at, done, t)
                            if inside(c, NG):
                                dve.wait_ge(done["fc"], c.count)
                                dve.wait_ge(done["xb"], c.count)
                                if c.follows(2):
                                    dve.wait_ge(xl_out.sems[c.slot], xl_out.full(c - 2))
                                    dve.wait_ge(done["xlb"], (c - 2).count)
                                dve.tensor_tensor(xl[c.slot][:, :, :], by_k(po[:, :]), xb[:, :, :],
                                                  ALU.add).then_inc(done["xl"], 1)
                                dve.wait_ge(done["xl"], c.count)
                                if c.follows(1):
                                    dve.wait_ge(done["h"], (c - 1).count)
                                moments_of(dve, done, c, xl[c.slot], x_norm, ("xl_stats", "xl_moments"))
                            if inside(b, NG):
                                dve_y_rstd(dve, at, done, b)
                            if inside(d, NG):
                                dve.wait_ge(done["z"], d.count)
                                moments_of(dve, done, d, z, z_norm, ("z_stats", "z_moments"))
                            if inside(t, NG):
                                dve_weights(dve, at, done, t)
                            if inside(c, NG):
                                biased_rstd(dve, done, c, x_norm, "dev", "rstd", "bias", "h")
                            if inside(t, NG):
                                dve_t(dve, at, done, t)
                            if inside(d, NG):
                                biased_rstd(dve, done, d, z_norm, "z_dev", "z_rstd", "z_bias", "zn")
                            if inside(b, NG):
                                dve.wait_ge(done["tT"], b.count)
                                dve.wait_ge(done["x2T"], b.count)
                                if b.follows(1):
                                    dve.wait_ge(done["fc"], (b - 1).count)
                                dve.tensor_tensor(sT[:, :], tT[:, :], px[:, :], ALU.add).then_inc(done["sT"], 1)

                        run(dve, NG, 3, body)

        def first_rows():
            ph = Phase("own")
            with ph.ctx:
                index, scale = ph.sb("index", [P, 6 * K], I32), ph.sb("scale", [P, 2 * K])
                g = ph.sb("g", [P, K, D])
                start = ph.sb("start", [P, K, 2, D])
                rec_in, stores = ph.dmas("rec_in", 2), ph.dmas("stores", 2)
                fetched = ph.dmas("fetched", K)
                go, blank = ph.sem("go"), ph.sem("blank")
                own = ph.steps("own", "own")

                with nc.Block() as block:
                    @block.sync
                    def _(sp):
                        def body(t):
                            s = t.slot
                            if inside(t, EG):
                                if t.follows(2):
                                    sp.wait_ge(own.sem, own.at("own", t - 2))
                                sp.dma_start(index[s][:, :], block_of(index_rec, t)).then_inc(rec_in.sems[t.slot], 16)
                                sp.dma_start(scale[s][:, :], block_of(scale_rec, t)).then_inc(rec_in.sems[t.slot], 16)
                            b = t - 1
                            if inside(b, EG):
                                sp.wait_ge(own.sem, own.at("own", b))
                                sp.dma_start(group(g0_e, b), flat(g[b.slot][:, :, :])).then_inc(stores.sems[b.slot], 16)
                                sp.dma_start(group(acc[0], b),
                                                          start[b.slot].rearrange("p k l d -> p (k l d)")).then_inc(
                                                              stores.sems[b.slot], 16)

                        run(sp, EG, 1, body)
                        for t in (EG - 2, EG - 1):
                            sp.wait_ge(stores.sems[Turn(None, t).slot], stores.full(Turn(None, t)))

                    @block.gpsimd
                    def _(pool):
                        def body(t):
                            s = t.slot
                            pool.wait_ge(rec_in.sems[t.slot], rec_in.full(t))
                            if t.follows(2):
                                pool.wait_ge(stores.sems[(t - 2).slot], stores.full(t - 2))
                            for k in range(K):
                                indirect(pool, go, out=g[s][:, k, :], out_offset=None,
                                                       in_=g_rows[0][0:NP, :],
                                                       in_offset=rows_at(index[s][:, DST + k:DST + k + 1])).then_inc(
                                                           fetched.sems[t.slot], 16)

                        run(pool, EG, 0, body)

                    @block.vector
                    def _(dve):
                        for s in range(2):
                            dve.memset(start[s][:, :, :, :], 0.0).then_inc(blank, 1)
                        dve.wait_ge(blank, 2)

                        def body(t):
                            s = t.slot
                            dve.wait_ge(rec_in.sems[t.slot], rec_in.full(t))
                            dve.wait_ge(fetched.sems[t.slot], fetched.full(t))
                            if t.follows(2):
                                dve.wait_ge(stores.sems[(t - 2).slot], stores.full(t - 2))
                            dve.tensor_tensor(start[s][:, :, 0, :], g[s][:, :, :],
                                                       over(scale[s][:, K:2 * K], D), ALU.mult).then_inc(
                                                           own.step("own"), 1)

                        run(dve, EG, 0, body)

        def gather_messages(layer):
            ph = Phase(f"send{layer}")
            with ph.ctx:
                index, scale = ph.sb("index", [P, 6 * K], I32), ph.sb("scale", [P, 2 * K])
                late = ph.sb("late", [P, 6 * K], I32)
                dst_row = ph.sb("dst_row", [P, ROWS], I32)
                same = ph.sb("same", [P, K, P])
                g, m, total = ph.sb("g", [P, K, D]), ph.sb("m", [P, K, D]), ph.sb("total", [P, K, D])
                pm = [ph.bank(f"pm{i}") for i in range(2)]
                rec_in, late_in = ph.dmas("rec_in", 3), ph.dmas("late_in")
                fetched = ph.dmas("fetched", K)
                added = [ph.sem(f"added{k}") for k in range(K)]
                go = ph.sem("go")
                made = ph.steps("made", "same", "m")
                summed, copied = ph.steps("summed", "sum"), ph.steps("copied", "total")
                sums = acc[layer].rearrange("e (l d) -> (e l) d", l=2)

                def added_wait(engine, t, ks=range(K)):
                    if t.known and t.number < 0:
                        return
                    for k in ks:
                        engine.wait_ge(added[k], 16 * t.number + 16)

                with nc.Block() as block:
                    @block.sync
                    def _(sp):
                        def body(t):
                            s = t.slot
                            if inside(t, EG):
                                if t.follows(2):
                                    sp.wait_ge(made.sem, made.at("m", t - 2))
                                    sp.wait_ge(fetched.sems[s], fetched.full(t - 2))
                                sp.dma_start(index[s][:, :], block_of(index_rec, t)).then_inc(rec_in.sems[s], 16)
                                sp.dma_start(scale[s][:, :], block_of(scale_rec, t)).then_inc(rec_in.sems[s], 16)
                                sp.dma_start(
                                    dst_row[s][:, :],
                                    a["dst"][bass.ds(t.number * ROWS, ROWS), :].rearrange("e o -> (e o)")
                                    .partition_broadcast(P)).then_inc(rec_in.sems[s], 16)
                            b = t - 1
                            if inside(b, EG):
                                added_wait(sp, b - 2)
                                sp.dma_start(late[b.slot][:, :], block_of(index_rec, b)).then_inc(
                                    late_in.sems[b.slot], 16)

                        run(sp, EG, 1, body)

                    @block.gpsimd
                    def _(pool):
                        def body(t):
                            b = t - 2
                            if inside(t, EG):
                                pool.wait_ge(rec_in.sems[t.slot], rec_in.full(t))
                                if t.follows(2):
                                    pool.wait_ge(made.sem, made.at("m", t - 2))
                            if inside(b, EG):
                                pool.wait_ge(late_in.sems[b.slot], late_in.full(b))
                                pool.wait_ge(copied.sem, copied.at("total", b))
                            for k in range(K):
                                if inside(t, EG):
                                    indirect(
                                        pool, go, out=g[t.slot][:, k, :], out_offset=None, in_=g_rows[layer][0:NP, :],
                                        in_offset=rows_at(index[t.slot][:, SRC + k:SRC + k + 1])).then_inc(
                                            fetched.sems[t.slot], 16)
                                if inside(b, EG):
                                    added_wait(pool, b if k >= 2 else b - 1, [(k + 2) % K])
                                    indirect(pool, go, out=sums,
                                             out_offset=rows_at(late[b.slot][:, ADD_AT + k:ADD_AT + k + 1]),
                                             in_=total[b.slot][:, k, :], in_offset=None,
                                             compute_op=ALU.add).then_inc(added[k], 16)

                        run(pool, EG, 2, body)
                        added_wait(pool, Turn(None, EG - 1))

                    @block.vector
                    def _(dve):
                        def body(t):
                            s = t.slot
                            dve.wait_ge(rec_in.sems[t.slot], rec_in.full(t))
                            if t.follows(2):
                                dve.wait_ge(summed.sem, summed.at("sum", t - 2))
                            dve.tensor_tensor(
                                same[s][:, :, :], dst_row[s].rearrange("p (q k) -> p k q", k=K),
                                over(index[s][:, DST:DST + K], P), ALU.is_equal).then_inc(made.step("same"), 1)
                            dve.wait_ge(fetched.sems[t.slot], fetched.full(t))
                            dve.tensor_tensor(m[s][:, :, :], g[s][:, :, :],
                                                        over(scale[s][:, 0:K], D), ALU.mult).then_inc(made.step("m"), 1)

                        run(dve, EG, 0, body)

                    @block.tensor
                    def _(pe):
                        def body(t):
                            s = t.slot
                            pe.wait_ge(made.sem, made.at("m", t))
                            if t.follows(2):
                                pe.wait_ge(copied.sem, copied.at("total", t - 2))
                            for k in range(K):
                                ins = pe.matmul(pm[s][:, k * D:(k + 1) * D], same[s][:, k, :], m[s][:, k, :],
                                                start=True, stop=True)
                            ins.then_inc(summed.step("sum"), 1)

                        run(pe, EG, 0, body)

                    @block.scalar
                    def _(act):
                        def body(t):
                            s = t.slot
                            act.wait_ge(summed.sem, summed.at("sum", t))
                            added_wait(act, t - 2)
                            act.copy(flat(total[s][:, :, :]), pm[s][:, :]).then_inc(copied.step("total"), 1)

                        run(act, EG, 0, body)

        def update_nodes(layer):
            last = layer == LAYERS - 1
            ph = Phase(f"update{layer}")
            with ph.ctx:
                index = ph.sb("index", [P, 6 * K], I32)
                scale, late = ph.sb("scale", [P, 2 * K]), ph.sb("late", [P, 2 * K])
                parts, g0 = ph.sb("parts", [P, K, 2, D]), ph.sb("g0", [P, K, D])
                s0, s1 = ph.sb("s0", [P, K, D]), ph.sb("s1", [P, K, D])
                sT, uT = ph.sb("sT", [P, ROWS]), ph.sb("uT", [P, K, P])
                g = ph.sb("g", [P, K, D])
                start = ph.sb("start", [P, K, 2, D])
                ps, pc, pu = ([ph.bank(f"{n}{i}") for i in range(2)] for n in ("ps", "pc", "pu"))
                rec_in, parts_in = ph.dmas("rec_in", 3), ph.dmas("parts_in", 2)
                written, stores = ph.dmas("written", K), ph.dmas("stores")
                go, blank = ph.sem("go"), ph.sem("blank")
                summed = ph.steps("summed", "s0", "s1")
                finished = ph.steps("finished", "g", "start")
                pe_s, pe_c, pe_u = ph.steps("pe_s", "sT"), ph.steps("pe_c", "c"), ph.steps("pe_u", "u")
                act_s, act_u = ph.steps("act_s", "sT"), ph.steps("act_u", "uT")

                with nc.Block() as block:
                    @block.sync
                    def _(sp):
                        def body(t):
                            if inside(t, EG):
                                if t.follows(2):
                                    sp.wait_ge(summed.sem, summed.at("s1", t - 2))
                                sp.dma_start(parts[t.slot].rearrange("p k l d -> p (k l d)"),
                                             group(acc[layer], t)).then_inc(parts_in.sems[t.slot], 16)
                                sp.dma_start(scale[t.slot][:, :], block_of(scale_rec, t)).then_inc(
                                    parts_in.sems[t.slot], 16)
                            c = t - 3
                            if not last and inside(c, EG):
                                sp.wait_ge(finished.sem, finished.at("start", c))
                                sp.dma_start(group(acc[layer + 1], c),
                                             start[c.slot].rearrange("p k l d -> p (k l d)")).then_inc(
                                                 stores.sems[c.slot], 16)
                            b = t - 2
                            if inside(b, EG):
                                s = b.slot
                                if b.follows(2):
                                    sp.wait_ge(finished.sem, finished.at("start", b - 2))
                                    sp.wait_ge(written.sems[s], written.full(b - 2))
                                sp.dma_start(index[s][:, :], block_of(index_rec, b)).then_inc(rec_in.sems[s], 16)
                                sp.dma_start(late[s][:, :], block_of(scale_rec, b)).then_inc(rec_in.sems[s], 16)
                                sp.dma_start(flat(g0[s][:, :, :]), group(g0_e, b)).then_inc(rec_in.sems[s], 16)

                        run(sp, EG, 3, body)
                        if not last:
                            for t in (EG - 2, EG - 1):
                                sp.wait_ge(stores.sems[Turn(None, t).slot], stores.full(Turn(None, t)))

                    @block.gpsimd
                    def _(pool):
                        def body(t):
                            b = t - 3
                            if inside(b, EG):
                                pool.wait_ge(rec_in.sems[b.slot], rec_in.full(b))
                                pool.wait_ge(finished.sem, finished.at("g", b))
                                if b.follows(1):
                                    pool.wait_ge(written.sems[(b - 1).slot], written.full(b - 1))
                                for k in range(K):
                                    indirect(
                                        pool, go, out=g_rows[layer + 1],
                                        out_offset=rows_at(index[b.slot][:, WRITE_AT + k:WRITE_AT + k + 1]),
                                        in_=g[b.slot][:, k, :], in_offset=None).then_inc(written.sems[b.slot], 16)

                        run(pool, EG, 3, body)
                        for t in (EG - 2, EG - 1):
                            pool.wait_ge(written.sems[Turn(None, t).slot], written.full(Turn(None, t)))

                    @block.vector
                    def _(dve):
                        for s in range(2):
                            dve.memset(start[s][:, :, :, :], 0.0).then_inc(blank, 1)
                        dve.wait_ge(blank, 2)

                        def body(t):
                            b, n = t - 3, t - 1
                            if inside(n, EG):
                                s = n.slot
                                dve.wait_ge(parts_in.sems[n.slot], parts_in.full(n))
                                dve.tensor_tensor(s0[s][:, :, :], parts[s][:, :, 0, :],
                                                              parts[s][:, :, 1, :], ALU.add).then_inc(
                                                                  summed.step("s0"), 1)
                                dve.wait_ge(summed.sem, summed.at("s0", n))
                                if n.follows(2):
                                    dve.wait_ge(pe_s.sem, pe_s.at("sT", n - 2))
                                dve.tensor_tensor(s1[s][:, :, :], s0[s][:, :, :],
                                                              over(scale[s][:, K:2 * K], D), ALU.mult).then_inc(
                                                                  summed.step("s1"), 1)
                            if inside(b, EG):
                                s = b.slot
                                dve.wait_ge(rec_in.sems[s], rec_in.full(b))
                                dve.wait_ge(pe_u.sem, pe_u.at("u", b))
                                if b.follows(2):
                                    dve.wait_ge(written.sems[(b - 2).slot], written.full(b - 2))
                                dve.tensor_tensor(g[s][:, :, :], by_k(pu[s][:, :]), g0[s][:, :, :],
                                                                ALU.add).then_inc(finished.step("g"), 1)
                                dve.wait_ge(finished.sem, finished.at("g", b))
                                if not last:
                                    if b.follows(2):
                                        dve.wait_ge(stores.sems[(b - 2).slot], stores.full(b - 2))
                                dve.tensor_tensor(start[s][:, :, 0, :], g[s][:, :, :],
                                                                over(late[s][:, K:2 * K], D), ALU.mult).then_inc(
                                                                    finished.step("start"), 1)

                        run(dve, EG, 3, body)

                    @block.tensor
                    def _(pe):
                        def body(t):
                            c, b = t - 2, t - 1
                            if inside(c, EG):
                                pe.wait_ge(act_u.sem, act_u.at("uT", c))
                                if c.follows(2):
                                    pe.wait_ge(finished.sem, finished.at("g", c - 2))
                                transposed(pe, pu[c.slot], uT[c.slot]).then_inc(pe_u.step("u"), 1)
                            if inside(b, EG):
                                pe.wait_ge(act_s.sem, act_s.at("sT", b))
                                if b.follows(2):
                                    pe.wait_ge(act_u.sem, act_u.at("uT", b - 2))
                                pe.matmul(pc[b.slot][:, :], W[f"c{layer}"], sT[b.slot][:, :], start=True,
                                          stop=True).then_inc(pe_c.step("c"), 1)
                            if inside(t, EG):
                                pe.wait_ge(summed.sem, summed.at("s1", t))
                                if t.follows(2):
                                    pe.wait_ge(act_s.sem, act_s.at("sT", t - 2))
                                transposed(pe, ps[t.slot], s1[t.slot]).then_inc(pe_s.step("sT"), 1)

                        run(pe, EG, 2, body)

                    @block.scalar
                    def _(act):
                        def body(t):
                            b = t - 1
                            if inside(b, EG):
                                act.wait_ge(pe_c.sem, pe_c.at("c", b))
                                if b.follows(2):
                                    act.wait_ge(pe_u.sem, pe_u.at("u", b - 2))
                                i = layer + 1
                                act.activation(flat(uT[b.slot][:, :, :]), pc[b.slot][:, :], ACT.Relu,
                                               bias=bn_bias[:, i:i + 1],
                                               scale=bn_scale[:, i:i + 1]).then_inc(act_u.step("uT"), 1)
                            if inside(t, EG):
                                act.wait_ge(pe_s.sem, pe_s.at("sT", t))
                                if t.follows(2):
                                    act.wait_ge(pe_c.sem, pe_c.at("c", t - 2))
                                act.copy(sT[t.slot][:, :], ps[t.slot][:, :]).then_inc(act_s.step("sT"), 1)

                        run(act, EG, 1, body)

        def edge_scores():
            ph = Phase("score")
            with ph.ctx:
                index, late = ph.sb("index", [P, 6 * K], I32), ph.sb("late", [P, 6 * K], I32)
                dst_row = ph.sb("dst_row", [P, ROWS], I32)
                terms = ph.sb("terms", [HIDDEN, ROWS])
                hidden = slice(ATTR, HIDDEN)
                scalars = ph.sb("scalars", [3, ROWS])
                xs, xd = ph.sb("xs", [P, K, D]), ph.sb("xd", [P, K, D])
                s_norm, d_norm = norm_tiles(ph, "s"), norm_tiles(ph, "d")
                hs, hd, h = ph.one("hs", [P, K, D]), ph.one("hd", [P, K, D]), ph.sb("h", [P, K, D])
                hsT, hdT = ph.one("hsT", [P, ROWS]), ph.one("hdT", [P, ROWS])
                q, key, v = ph.one("q", [P, K, D]), ph.one("key", [P, K, D]), ph.sb("v", [P, K, D])
                qk, dot = ph.one("qk", [P, K * HEADS, HEAD_DIM]), ph.one("dot", [P, K * HEADS])
                neg, e0, e1, cons = (ph.one(n, [P, K * HEADS]) for n in ("neg", "e0", "e1", "cons"))
                sc0, sc1, score = (ph.one(n, [P, K * HEADS]) for n in ("sc0", "sc1", "score"))
                same, off = ph.sb("same", [P, K, P]), ph.one("off", [P, K, P])
                H4 = HEADS // 2
                masked = ph.sb("masked", [P, H4, P])
                top, less, w = (ph.one(n, [P, K * HEADS]) for n in ("top", "less", "w"))
                old, new = ph.one("old", [P, K, 2, HEADS]), ph.one("new", [P, K, 2, HEADS])
                drop, shrink = ph.one("drop", [P, 2, K, HEADS]), ph.one("shrink", [P, 2, K, HEADS])
                part = ph.one("part", [P, 2, K, HEADS])
                ph_t, pq, pk, pv = ph.bank("ph"), ph.bank("pq"), ph.bank("pk"), ph.bank("pv")
                psm, pw = ph.bank("psm"), ph.bank("pw")
                small = psm[:, 0:3 * K * HEADS].rearrange("p (k g h) -> p g k h", k=K, g=3)
                pb = [ph.bank(f"pb{i}") for i in range(2)]
                rec_in, late_in, small_in = ph.dmas("rec_in"), ph.dmas("late_in", 2), ph.dmas("small_in", 3)
                fetched, stores = ph.dmas("fetched", 2 * K), ph.dmas("stores", 3)
                old_in = [ph.sem(f"old_in{k}") for k in range(K)]
                new_out = [ph.sem(f"new_out{k}") for k in range(K)]
                go = ph.sem("go")
                done = ph.marks("s_stats", "s_moments", "d_stats", "d_moments", "s_dev", "d_dev", "s_rstd", "hs",
                                "d_rstd", "hd", "h", "hsT", "hsT_out", "q", "q_out", "hdT", "hdT_out", "k", "v",
                                "v_out", "k_out", "hidden", "hidden_out", "small", "same", "off", "neg", "e0", "e1", "qk", "dot",
                                "cons", "sc0", "sc1", "score", "less", "w", "wsum", "newtop", "drop", "shrink",
                                "part", "new")
                halves = 2 * K
                spread, masks, tops_in = (ph.steps(n, *(f"{n}{j}" for j in range(halves)))
                                          for n in ("spread", "masked", "top"))

                def by_head(tile):
                    return tile[:, :].rearrange("p (k h) -> p k h", k=K)

                def lane_wait(engine, sems, t, k):
                    if not (t.known and t.number < 0):
                        engine.wait_ge(sems[k], 16 * t.number + 16)

                with nc.Block() as block:
                    @block.sync
                    def _(sp):
                        def body(t):
                            s = t.slot
                            if inside(t, EG):
                                if t.follows(2):
                                    sp.wait_ge(fetched.sems[s], fetched.full(t - 2))
                                sp.dma_start(index[s][:, :], block_of(index_rec, t)).then_inc(rec_in.sems[s], 16)
                                if t.follows(2):
                                    sp.wait_ge(done["small"], (t - 2).count)
                                sp.dma_start(terms[s][0:ATTR, :], block_of(a["attr"], t, ATTR)).then_inc(
                                    small_in.sems[s], 16)
                                sp.dma_start(scalars[s][1:3, :], block_of(a["dist"], t, 2)).then_inc(
                                    small_in.sems[s], 16)
                                sp.dma_start(
                                    scalars[s][0:1, :],
                                    nodevec_e[bass.ds(t.number * ROWS, ROWS), :]
                                    .rearrange("(o e) u -> o (e u)", o=1)).then_inc(small_in.sems[s], 16)
                            c = t - 2
                            if inside(c, EG):
                                s = c.slot
                                sp.wait_ge(done["h"], c.count)
                                sp.dma_start(group(xl_e, c), flat(xd[s][:, :, :])).then_inc(stores.sems[s], 16)
                                sp.dma_start(group(h_e, c), flat(h[s][:, :, :])).then_inc(stores.sems[s], 16)
                                sp.wait_ge(done["v_out"], c.count)
                                sp.dma_start(group(v_e, c), flat(v[s][:, :, :])).then_inc(stores.sems[s], 16)
                            b = t - 1
                            if inside(b, EG):
                                s = b.slot
                                if b.follows(2):
                                    sp.wait_ge(done["same"], (b - 2).count)
                                for k in range(K):
                                    lane_wait(sp, new_out, b - 2, k)
                                sp.dma_start(late[s][:, :], block_of(index_rec, b)).then_inc(late_in.sems[s], 16)
                                sp.dma_start(
                                    dst_row[s][:, :],
                                    a["dst"][bass.ds(b.number * ROWS, ROWS), :].rearrange("e o -> (e o)")
                                    .partition_broadcast(P)).then_inc(late_in.sems[s], 16)

                        run(sp, EG, 2, body)
                        for t in (Turn(None, EG - 2), Turn(None, EG - 1)):
                            sp.wait_ge(stores.sems[t.slot], stores.full(t))

                    @block.gpsimd
                    def _(pool):
                        def body(t):
                            d = t - 3
                            if inside(d, EG):
                                pool.wait_ge(done["new"], d.count)
                                for k in range(K):
                                    indirect(pool, go, out=soft,
                                             out_offset=rows_at(late[d.slot][:, SOFT_AT + k:SOFT_AT + k + 1]),
                                             in_=new[:, k, :, :].rearrange("p t h -> p (t h)"),
                                             in_offset=None).then_inc(new_out[k], 16)
                            if inside(t, EG):
                                pool.wait_ge(rec_in.sems[t.slot], rec_in.full(t))
                                if t.follows(2):
                                    pool.wait_ge(done["hs"], (t - 2).count)
                                    pool.wait_ge(stores.sems[t.slot], stores.full(t - 2))
                                for k in range(K):
                                    for tile, col in ((xs, SRC), (xd, DST)):
                                        indirect(
                                            pool, go, out=tile[t.slot][:, k, :], out_offset=None, in_=xl_rows,
                                            in_offset=rows_at(index[t.slot][:, col + k:col + k + 1])).then_inc(
                                                fetched.sems[t.slot], 16)
                            c = t - 2
                            if inside(c, EG):
                                pool.wait_ge(late_in.sems[c.slot], late_in.full(c))
                                if c.follows(1):
                                    pool.wait_ge(done["part"], (c - 1).count)
                                for k in range(K):
                                    lane_wait(pool, new_out, c - 1, k)
                                    indirect(pool, go, out=old[:, k, :, :].rearrange("p t h -> p (t h)"),
                                             out_offset=None, in_=soft,
                                             in_offset=rows_at(late[c.slot][:, SOFT_AT + k:SOFT_AT + k + 1])).then_inc(
                                                 old_in[k], 16)

                        run(pool, EG, 3, body)
                        for k in range(K):
                            lane_wait(pool, new_out, Turn(None, EG - 1), k)

                    @block.vector
                    def _(dve):
                        def norms(t):
                            s = t.slot
                            dve.wait_ge(fetched.sems[s], fetched.full(t))
                            moments_of(dve, done, t, xs[s], s_norm, ("s_stats", "s_moments"))
                            moments_of(dve, done, t, xd[s], d_norm, ("d_stats", "d_moments"))
                            dve.wait_ge(done["s_dev"], t.count)
                            inverted(dve, s_norm).then_inc(done["s_rstd"], 1)
                            dve.wait_ge(done["s_rstd"], t.count)
                            if t.follows(1):
                                dve.wait_ge(done["hsT"], (t - 1).count)
                            normalize(dve, hs, xs[s], s_norm).then_inc(done["hs"], 1)
                            dve.wait_ge(done["d_dev"], t.count)
                            inverted(dve, d_norm).then_inc(done["d_rstd"], 1)
                            dve.wait_ge(done["d_rstd"], t.count)
                            if t.follows(1):
                                dve.wait_ge(done["hdT"], (t - 1).count)
                            normalize(dve, hd, xd[s], d_norm).then_inc(done["hd"], 1)
                            dve.wait_ge(done["hd"], t.count)
                            if t.follows(2):
                                dve.wait_ge(stores.sems[s], stores.full(t - 2))
                            dve.tensor_scalar(h[s][:, :, :], hd[:, :, :], 0.0, None, ALU.max).then_inc(done["h"], 1)

                        def scores(t):
                            s = t.slot
                            dve.wait_ge(done["small"], t.count)
                            if t.follows(1):
                                dve.wait_ge(done["e0"], (t - 1).count)
                            dve.tensor_scalar(by_head(neg), small[:, 1, :, :], -1.0, EXP_MAX, ALU.mult,
                                              ALU.min).then_inc(done["neg"], 1)
                            dve.wait_ge(late_in.sems[s], late_in.full(t))
                            if t.follows(2):
                                dve.wait_ge(done["wsum"], (t - 2).count)
                            dve.tensor_tensor(
                                same[s][:, :, :], dst_row[s].rearrange("p (q k) -> p k q", k=K),
                                over(late[s][:, DST:DST + K], P), ALU.is_equal).then_inc(done["same"], 1)
                            dve.wait_ge(done["k"], t.count)
                            dve.tensor_tensor(key[:, :, :], by_k(pk[:, :]), R["bk"], ALU.add).then_inc(done["k_out"], 1)
                            dve.wait_ge(done["v"], t.count)
                            if t.follows(2):
                                dve.wait_ge(stores.sems[s], stores.full(t - 2))
                            dve.tensor_tensor(v[s][:, :, :], by_k(pv[:, :]), R["bv"], ALU.add).then_inc(
                                done["v_out"], 1)
                            dve.wait_ge(done["k_out"], t.count)
                            dve.wait_ge(done["q_out"], t.count)
                            dve.tensor_tensor(qk.rearrange("p m d -> p (m d)"), flat(q[:, :, :]),
                                              flat(key[:, :, :]), ALU.mult).then_inc(done["qk"], 1)
                            dve.wait_ge(done["qk"], t.count)
                            dve.tensor_reduce(dot[:, :], qk[:, :, :], AX_X, ALU.add).then_inc(done["dot"], 1)
                            dve.wait_ge(done["e0"], t.count)
                            dve.tensor_scalar(e1[:, :], e0[:, :], 1.0, None, ALU.add).then_inc(done["e1"], 1)
                            dve.wait_ge(done["dot"], t.count)
                            dve.scalar_tensor_tensor(by_head(sc0), by_head(dot), HEAD_DIM ** -0.5,
                                                     small[:, 0, :, :], ALU.mult, ALU.add).then_inc(done["sc0"], 1)
                            dve.wait_ge(done["e1"], t.count)
                            dve.reciprocal(cons[:, :], e1[:, :]).then_inc(done["cons"], 1)
                            dve.wait_ge(done["cons"], t.count)
                            dve.tensor_tensor(sc1[:, :], sc0[:, :], cons[:, :], ALU.mult).then_inc(done["sc1"], 1)
                            dve.wait_ge(done["sc1"], t.count)
                            if t.follows(1):
                                dve.wait_ge(spread.sem, spread.at(f"spread{halves - 1}", t - 1))
                            dve.tensor_tensor(by_head(score), by_head(sc1), small[:, 2, :, :], ALU.add).then_inc(
                                done["score"], 1)
                            dve.wait_ge(done["same"], t.count)
                            dve.tensor_scalar(off[:, :, :], same[s][:, :, :], -1.0, -LOWEST, ALU.add,
                                              ALU.mult).then_inc(done["off"], 1)
                            dve.wait_ge(done["off"], t.count)
                            for j in range(halves):
                                if j >= 2:
                                    dve.wait_ge(tops_in.sem, tops_in.at(f"top{j - 2}", t))
                                dve.wait_ge(spread.sem, spread.at(f"spread{j}", t))
                                dve.tensor_tensor(
                                    masked[j % 2][:, :, :], pb[j % 2][:, :].rearrange("p (h q) -> p h q", h=H4),
                                    off[:, j // 2, :].unsqueeze(1).to_broadcast([P, H4, P]),
                                    ALU.add).then_inc(masks.step(f"masked{j}"), 1)
                                dve.wait_ge(masks.sem, masks.at(f"masked{j}", t))
                                dve.tensor_reduce(top[:, j * H4:(j + 1) * H4], masked[j % 2][:, :, :],
                                                  AX_X, ALU.max).then_inc(tops_in.step(f"top{j}"), 1)
                            dve.wait_ge(tops_in.sem, tops_in.at(f"top{halves - 1}", t))
                            if t.follows(1):
                                dve.wait_ge(done["w"], (t - 1).count)
                            dve.tensor_tensor(less[:, :], score[:, :], top[:, :], ALU.subtract).then_inc(
                                done["less"], 1)

                        def merge(t):
                            for k in range(K):
                                lane_wait(dve, old_in, t, k)
                                lane_wait(dve, new_out, t - 1, k)
                            tops = top[:, :].rearrange("p (k h) -> p k h", k=K)
                            dve.tensor_tensor(new[:, :, 0, :], old[:, :, 0, :], tops, ALU.max).then_inc(
                                done["newtop"], 1)
                            dve.wait_ge(done["newtop"], t.count)
                            dve.tensor_tensor(drop[:, 0, :, :], old[:, :, 0, :], new[:, :, 0, :], ALU.subtract)
                            dve.tensor_tensor(drop[:, 1, :, :], tops, new[:, :, 0, :], ALU.subtract).then_inc(
                                done["drop"], 1)
                            dve.wait_ge(done["shrink"], t.count)
                            dve.wait_ge(done["wsum"], t.count)
                            dve.tensor_tensor(part[:, 0, :, :], old[:, :, 1, :], shrink[:, 0, :, :], ALU.mult)
                            dve.tensor_tensor(
                                part[:, 1, :, :], pw[:, 0:32].rearrange("p (k h) -> p k h", k=K),
                                shrink[:, 1, :, :], ALU.mult).then_inc(done["part"], 1)
                            dve.wait_ge(done["part"], t.count)
                            dve.tensor_tensor(new[:, :, 1, :], part[:, 0, :, :], part[:, 1, :, :],
                                              ALU.add).then_inc(done["new"], 1)

                        def body(t):
                            if inside(t - 2, EG):
                                scores(t - 2)
                            if inside(t - 1, EG):
                                norms(t - 1)
                            if inside(t - 2, EG):
                                merge(t - 2)
                            b = t - 1
                            if inside(b, EG):
                                dve.wait_ge(done["q"], b.count)
                                if b.follows(1):
                                    dve.wait_ge(done["qk"], (b - 1).count)
                                dve.tensor_tensor(q[:, :, :], by_k(pq[:, :]), R["bq"], ALU.add).then_inc(
                                    done["q_out"], 1)

                        run(dve, EG, 2, body)

                    @block.scalar
                    def _(act):
                        def body(t):
                            b, c = t - 1, t - 2
                            if inside(c, EG):
                                act.wait_ge(done["neg"], c.count)
                                if c.follows(1):
                                    act.wait_ge(done["e1"], (c - 1).count)
                                act.activation(e0[:, :], neg[:, :], ACT.Exp).then_inc(done["e0"], 1)
                            if inside(b, EG):
                                act.wait_ge(done["hidden"], b.count)
                                if b.follows(2):
                                    act.wait_ge(done["small"], (b - 2).count)
                                act.activation(terms[b.slot][hidden, :], ph_t[hidden, :], ACT.Relu).then_inc(
                                    done["hidden_out"], 1)
                            if inside(c, EG):
                                act.wait_ge(done["less"], c.count)
                                if c.follows(1):
                                    act.wait_ge(done["wsum"], (c - 1).count)
                                act.activation(w[:, :], less[:, :], ACT.Exp).then_inc(done["w"], 1)
                            if inside(b, EG):
                                act.wait_ge(done["s_moments"], b.count)
                                deviation(act, s_norm).then_inc(done["s_dev"], 1)
                                act.wait_ge(done["d_moments"], b.count)
                                deviation(act, d_norm).then_inc(done["d_dev"], 1)
                                act.wait_ge(done["hsT"], b.count)
                                if b.follows(1):
                                    act.wait_ge(done["q"], (b - 1).count)
                                act.activation(hsT[:, :], ph_t[:, :], ACT.Relu).then_inc(done["hsT_out"], 1)
                            if inside(c, EG):
                                act.wait_ge(done["drop"], c.count)
                                if c.follows(1):
                                    act.wait_ge(done["part"], (c - 1).count)
                                act.activation(shrink[:, :, :, :], drop[:, :, :, :], ACT.Exp).then_inc(
                                    done["shrink"], 1)
                            if inside(b, EG):
                                act.wait_ge(done["hdT"], b.count)
                                if b.follows(1):
                                    act.wait_ge(done["v"], (b - 1).count)
                                act.activation(hdT[:, :], ph_t[:, :], ACT.Relu).then_inc(done["hdT_out"], 1)

                        run(act, EG, 2, body)

                    @block.tensor
                    def _(pe):
                        def rows_by(bank, left, w):
                            for k in range(K):
                                ins = pe.matmul(bank[:, k * D:(k + 1) * D], left[:, k * P:(k + 1) * P], W[w],
                                                start=True, stop=True)
                            return ins

                        def body(t):
                            b, c = t - 1, t - 2
                            if inside(c, EG):
                                pe.wait_ge(done["score"], c.count)
                                for j in range(halves):
                                    if j >= 2:
                                        pe.wait_ge(masks.sem, masks.at(f"masked{j - 2}", c))
                                    elif c.follows(1):
                                        pe.wait_ge(masks.sem, masks.at(f"masked{halves - 2 + j}", c - 1))
                                    for h in range(H4):
                                        at = j * H4 + h
                                        ins = pe.transpose(pb[j % 2][:, h * P:(h + 1) * P],
                                                           score[:, at:at + 1].to_broadcast([P, P]), ident[:, :])
                                    ins.then_inc(spread.step(f"spread{j}"), 1)
                            if inside(b, EG):
                                s = b.slot
                                pe.wait_ge(small_in.sems[s], small_in.full(b))
                                if b.follows(1):
                                    pe.wait_ge(done["hdT_out"], (b - 1).count)
                                pe.matmul(ph_t[0:HIDDEN, :], small_w1[:, :], scalars[s][:, :], start=True,
                                          stop=True).then_inc(done["hidden"], 1)
                            if inside(c, EG):
                                pe.wait_ge(done["w"], c.count)
                                if c.follows(1):
                                    pe.wait_ge(done["part"], (c - 1).count)
                                for k in range(K):
                                    ins = pe.matmul(pw[:, k * HEADS:(k + 1) * HEADS], same[c.slot][:, k, :],
                                                    w[:, k * HEADS:(k + 1) * HEADS], start=True, stop=True)
                                ins.then_inc(done["wsum"], 1)
                            if inside(b, EG):
                                pe.wait_ge(done["hs"], b.count)
                                pe.wait_ge(done["hidden_out"], b.count)
                                transposed(pe, ph_t, hs).then_inc(done["hsT"], 1)
                                if b.follows(1):
                                    pe.wait_ge(done["score"], (b - 1).count)
                                for k in range(K):
                                    ins = pe.matmul(psm[:, k * 3 * HEADS:(k + 1) * 3 * HEADS],
                                                    terms[s].rearrange("c (q k) -> c k q", k=K)[:, k, :],
                                                    small_w2[:, :], start=True, stop=True)
                                ins.then_inc(done["small"], 1)
                                pe.wait_ge(done["hsT_out"], b.count)
                                if b.follows(1):
                                    pe.wait_ge(done["q_out"], (b - 1).count)
                                rows_by(pq, hsT, "l1_q").then_inc(done["q"], 1)
                                pe.wait_ge(done["hd"], b.count)
                                transposed(pe, ph_t, hd).then_inc(done["hdT"], 1)
                                pe.wait_ge(done["hdT_out"], b.count)
                                if b.follows(1):
                                    pe.wait_ge(done["k_out"], (b - 1).count)
                                rows_by(pk, hdT, "l1_k").then_inc(done["k"], 1)
                                if b.follows(1):
                                    pe.wait_ge(done["v_out"], (b - 1).count)
                                rows_by(pv, hdT, "l1_v").then_inc(done["v"], 1)

                        run(pe, EG, 2, body)

        def edge_output():
            ph = Phase("final")
            with ph.ctx:
                index = ph.sb("index", [P, 6 * K], I32)
                lanes = ph.sb("lanes", [P, K, K, 2, HEADS])
                v, h, x = ph.sb("v", [P, K, D]), ph.sb("h", [P, K, D]), ph.sb("x", [P, K, D])
                top, drop, shrink = (ph.one("top", [P, K, HEADS]), ph.one("drop", [P, K, K, HEADS]),
                                     ph.one("shrink", [P, K, K, HEADS]))
                part, total, inverse = (ph.one("part", [P, K, K, HEADS]), ph.one("total", [P, K, HEADS]),
                                        ph.one("inverse", [P, K, HEADS]))
                floor = ph.one("floor", [P, K, HEADS])
                weight, agg, aT = (ph.one("weight", [P, K, HEADS]), ph.sb("agg", [P, K, D]),
                                   ph.sb("aT", [P, ROWS]))
                z, zn, zg, zb = (ph.one(n, [P, K, D]) for n in ("z", "zn", "zg", "zb"))
                o = ph.sb("o", [P, K, D])
                z_norm, act_z = norm_tiles(ph, "z"), ph.steps("act_z", "dev")
                pa, po = [ph.bank(f"pa{i}") for i in range(2)], [ph.bank(f"po{i}") for i in range(2)]
                rec_in, lanes_in, written = ph.dmas("rec_in", 4), ph.dmas("lanes_in"), ph.dmas("written", K)
                go = ph.sem("go")
                dve_w = ph.steps("dve_w", "top", "drop", "part", "total", "floor", "inverse", "weight", "agg")
                dve_o = ph.steps("dve_o", "z", "stats", "moments", "rstd", "zn", "zg", "zb", "o")
                act_e, act_a = ph.steps("act_e", "shrink"), ph.steps("act_a", "aT")
                pe_a, pe_o = ph.steps("pe_a", "aT"), ph.steps("pe_o", "o")

                with nc.Block() as block:
                    @block.sync
                    def _(sp):
                        def body(t):
                            if inside(t, EG):
                                if t.follows(2):
                                    sp.wait_ge(dve_w.sem, dve_w.at("part", t - 2))
                                sp.dma_start(
                                    lanes[t.slot].rearrange("p k l t h -> p (k l t h)"),
                                    soft[bass.ds(t.number * ROWS * K, ROWS * K), :]
                                    .rearrange("(p k) c -> p (k c)", p=P)).then_inc(lanes_in.sems[t.slot], 16)
                            b = t - 1
                            if inside(b, EG):
                                s = b.slot
                                if b.follows(2):
                                    sp.wait_ge(dve_o.sem, dve_o.at("o", b - 2))
                                    sp.wait_ge(written.sems[s], written.full(b - 2))
                                sp.dma_start(index[s][:, :], block_of(index_rec, b)).then_inc(rec_in.sems[s], 16)
                                for tile, table in ((v, v_e), (h, h_e), (x, xl_e)):
                                    sp.dma_start(flat(tile[s][:, :, :]), group(table, b)).then_inc(rec_in.sems[s], 16)

                        run(sp, EG, 1, body)

                    @block.gpsimd
                    def _(pool):
                        def body(t):
                            b = t - 2
                            if inside(b, EG):
                                pool.wait_ge(rec_in.sems[b.slot], rec_in.full(b))
                                pool.wait_ge(dve_o.sem, dve_o.at("o", b))
                                if b.follows(1):
                                    pool.wait_ge(written.sems[(b - 1).slot], written.full(b - 1))
                                for k in range(K):
                                    indirect(
                                        pool, go, out=out,
                                        out_offset=rows_at(index[b.slot][:, WRITE_AT + k:WRITE_AT + k + 1]),
                                        in_=o[b.slot][:, k, :], in_offset=None).then_inc(written.sems[b.slot], 16)

                        run(pool, EG, 2, body)
                        for t in (EG - 2, EG - 1):
                            pool.wait_ge(written.sems[Turn(None, t).slot], written.full(Turn(None, t)))

                    @block.vector
                    def _(dve):
                        def weigh(t):
                            s = t.slot
                            dve.wait_ge(lanes_in.sems[t.slot], lanes_in.full(t))
                            tops = lanes[s][:, :, :, 0, :]
                            dve.tensor_reduce(top[:, :, :], tops.rearrange("p k l h -> p k h l"), AX_X,
                                                         ALU.max).then_inc(dve_w.step("top"), 1)
                            dve.wait_ge(dve_w.sem, dve_w.at("top", t))
                            if t.follows(1):
                                dve.wait_ge(act_e.sem, act_e.at("shrink", t - 1))
                            for k in range(K):
                                ins = dve.tensor_tensor(
                                    drop[:, k, :, :], lanes[s][:, k, :, 0, :],
                                    top[:, k, :].unsqueeze(1).to_broadcast([P, K, HEADS]), ALU.subtract)
                            ins.then_inc(dve_w.step("drop"), 1)

                        def attended(t):
                            s = t.slot
                            dve.wait_ge(rec_in.sems[s], rec_in.full(t))
                            dve.wait_ge(act_e.sem, act_e.at("shrink", t))
                            dve.tensor_tensor(part[:, :, :, :], lanes[s][:, :, :, 1, :],
                                                         shrink[:, :, :, :], ALU.mult).then_inc(dve_w.step("part"), 1)
                            dve.wait_ge(dve_w.sem, dve_w.at("part", t))
                            dve.tensor_reduce(total[:, :, :], part[:, :, :, :].rearrange("p k l h -> p k h l"),
                                                         AX_X, ALU.add).then_inc(dve_w.step("total"), 1)
                            dve.wait_ge(dve_w.sem, dve_w.at("total", t))
                            dve.tensor_scalar(floor[:, :, :], total[:, :, :], TINY, None, ALU.max).then_inc(
                                dve_w.step("floor"), 1)
                            dve.wait_ge(dve_w.sem, dve_w.at("floor", t))
                            dve.reciprocal(inverse[:, :, :], floor[:, :, :]).then_inc(dve_w.step("inverse"), 1)
                            dve.wait_ge(dve_w.sem, dve_w.at("inverse", t))
                            dve.tensor_tensor(weight[:, :, :], total[:, :, :], inverse[:, :, :],
                                                         ALU.mult).then_inc(dve_w.step("weight"), 1)
                            dve.wait_ge(dve_w.sem, dve_w.at("weight", t))
                            if t.follows(2):
                                dve.wait_ge(pe_a.sem, pe_a.at("aT", t - 2))
                            dve.tensor_tensor(
                                agg[s].rearrange("p k (h e) -> p (k h) e", h=HEADS),
                                v[s].rearrange("p k (h e) -> p (k h) e", h=HEADS),
                                over(weight.rearrange("p k h -> p (k h)"), HEAD_DIM), ALU.mult).then_inc(
                                    dve_w.step("agg"), 1)

                        def finish(t):
                            s = t.slot
                            dve.wait_ge(pe_o.sem, pe_o.at("o", t))
                            dve.tensor_tensor(z[:, :, :], by_k(po[s][:, :]), h[s][:, :, :], ALU.add).then_inc(
                                dve_o.step("z"), 1)
                            dve.wait_ge(dve_o.sem, dve_o.at("z", t))
                            moments_of(dve, dve_o, t, z, z_norm, ("stats", "moments"))
                            dve.wait_ge(act_z.sem, act_z.at("dev", t))
                            inverted(dve, z_norm).then_inc(dve_o.step("rstd"), 1)
                            dve.wait_ge(dve_o.sem, dve_o.at("rstd", t))
                            normalize(dve, zn, z, z_norm).then_inc(dve_o.step("zn"), 1)
                            dve.wait_ge(dve_o.sem, dve_o.at("zn", t))
                            dve.tensor_tensor(zg[:, :, :], zn[:, :, :], R["gamma"], ALU.mult).then_inc(
                                dve_o.step("zg"), 1)
                            dve.wait_ge(dve_o.sem, dve_o.at("zg", t))
                            dve.tensor_tensor(zb[:, :, :], zg[:, :, :], R["beta"], ALU.add).then_inc(
                                dve_o.step("zb"), 1)
                            dve.wait_ge(dve_o.sem, dve_o.at("zb", t))
                            if t.follows(2):
                                dve.wait_ge(written.sems[(t - 2).slot], written.full(t - 2))
                            dve.tensor_tensor(o[s][:, :, :], zb[:, :, :], x[s][:, :, :], ALU.add).then_inc(
                                dve_o.step("o"), 1)

                        def body(t):
                            if inside(t - 1, EG):
                                weigh(t - 1)
                            if inside(t - 2, EG):
                                finish(t - 2)
                            if inside(t - 1, EG):
                                attended(t - 1)

                        run(dve, EG, 2, body)

                    @block.scalar
                    def _(act):
                        def body(t):
                            if inside(t, EG):
                                act.wait_ge(dve_w.sem, dve_w.at("drop", t))
                                if t.follows(1):
                                    act.wait_ge(dve_w.sem, dve_w.at("part", t - 1))
                                act.activation(shrink[:, :, :, :], drop[:, :, :, :], ACT.Exp).then_inc(
                                    act_e.step("shrink"), 1)
                            b = t - 1
                            if inside(b, EG):
                                act.wait_ge(dve_o.sem, dve_o.at("moments", b))
                                deviation(act, z_norm).then_inc(act_z.step("dev"), 1)
                            if inside(t, EG):
                                act.wait_ge(pe_a.sem, pe_a.at("aT", t))
                                if t.follows(2):
                                    act.wait_ge(pe_o.sem, pe_o.at("o", t - 2))
                                act.copy(aT[t.slot][:, :], pa[t.slot][:, :]).then_inc(act_a.step("aT"), 1)

                        run(act, EG, 1, body)

                    @block.tensor
                    def _(pe):
                        def body(t):
                            s = t.slot
                            pe.wait_ge(dve_w.sem, dve_w.at("agg", t))
                            if t.follows(2):
                                pe.wait_ge(act_a.sem, act_a.at("aT", t - 2))
                            transposed(pe, pa[s], agg[s]).then_inc(pe_a.step("aT"), 1)
                            if t.follows(2):
                                pe.wait_ge(dve_o.sem, dve_o.at("z", t - 2))
                            pe.wait_ge(act_a.sem, act_a.at("aT", t))
                            pe.matmul(po[s][:, :], ones[0:1, :], flat(R["bo"])[0:1, :], start=True, stop=False,
                                      skip_group_check=True)
                            for k in range(K):
                                ins = pe.matmul(po[s][:, k * D:(k + 1) * D], aT[s][:, k * P:(k + 1) * P], W["l1_o"],
                                                start=False, stop=True, skip_group_check=True)
                            ins.then_inc(pe_o.step("o"), 1)

                        run(pe, EG, 0, body)

        index_edges()
        dense_first()
        first_rows()
        for layer in range(LAYERS):
            gather_messages(layer)
            update_nodes(layer)
        dense_second()
        dense_third()
        edge_scores()
        edge_output()


def kernel(**inputs):
    import numpy as np
    import concourse.bacc as bacc
    from concourse.bass_utils import run_bass_kernel_spmd

    def arr(name):
        return np.ascontiguousarray(inputs[name])

    n_nodes, n_edges = inputs["x"].shape[0], inputs["src"].shape[0]
    NG = -(-n_nodes // (2 * ROWS)) * 2
    EG = -(-n_edges // (2 * ROWS)) * 2
    NP, EP, SPARE = NG * ROWS, EG * ROWS, ROWS
    assert n_nodes < NP

    def padded(rows, n, fill=0):
        out = np.full((n, *rows.shape[1:]), fill, rows.dtype)
        out[:rows.shape[0]] = rows
        return out

    def groups_T(rows, one=0):
        c = rows.shape[1]
        out = np.ones((EG, c + one, ROWS), np.float32)
        out[:, :c] = padded(rows, EP).reshape(EG, ROWS, c).transpose(0, 2, 1)
        return out.reshape(EG * (c + one), ROWS)

    we, wc1, wc2, wd1, wd2 = (arr("L1_gnn_" + n) for n in ("We", "Wc1", "Wc2", "Wd1", "Wd2"))
    n_attr, n_c, n_d = we.shape[0], wc1.shape[1], wd1.shape[1]
    c_at, d_at, one_at = n_attr, n_attr + n_c, n_attr + n_c + n_d
    small_w1 = np.zeros((3, one_at + 1), np.float32)
    small_w1[0, c_at:d_at], small_w1[2, c_at:d_at] = wc1[0], arr("L1_gnn_bc1")
    small_w1[1, d_at:one_at], small_w1[2, d_at:one_at] = wd1[0], arr("L1_gnn_bd1")
    small_w1[2, one_at] = 1
    small_w2 = np.zeros((one_at + 1, 3 * HEADS), np.float32)
    small_w2[:n_attr, :HEADS], small_w2[one_at, :HEADS] = we, arr("L1_gnn_be")
    small_w2[c_at:d_at, HEADS:2 * HEADS], small_w2[one_at, HEADS:2 * HEADS] = wc2, arr("L1_gnn_bc2")
    small_w2[d_at:one_at, 2 * HEADS:], small_w2[one_at, 2 * HEADS:] = wd2, arr("L1_gnn_bd2")

    conv, qkv = arr("L0_gnn_conv_w"), arr("L0_gnn_qkv_w")
    bng, bnb, lng, lnb = (arr("L0_gnn_" + n) for n in ("bn_g", "bn_b", "t_ln_g", "t_ln_b"))
    conv_b = arr("L0_gnn_conv_b")
    columns = [arr("L0_gnn_g_fc_b"), conv_b[0], conv_b[1], conv_b[2], *bng, *bnb, *lng, *lnb]
    k = np.arange(K, dtype=np.float32)[None]
    p = np.arange(P, dtype=np.float32)[:, None]
    spare = k * P + p
    data = {
        "x": padded(arr("x"), NP),
        "node_vec": padded(arr("node_vec1"), NP + SPARE),
        "src": padded(arr("src").reshape(-1, 1), EP, n_nodes),
        "dst": padded(arr("dst").reshape(-1, 1), EP, n_nodes),
        "attr": groups_T(arr("edge_attr_64")),
        "dist": groups_T(arr("edge_weight1"), 1),
        "edge_no": np.arange(1, EP + 1, dtype=np.float32)[:, None],
        "t_w": arr("L0_gnn_t_fc_w"), "g_w": arr("L0_gnn_g_fc_w"), "fc_w": arr("L0_gnn_fc_w"),
        "wq0": qkv[0, 0], "wk0": qkv[0, 1], "wv0": qkv[0, 2],
        "wq1": qkv[1, 0], "wk1": qkv[1, 1], "wv1": qkv[1, 2],
        "c0": conv[0], "c1": conv[1], "c2": conv[2],
        "l1_q": arr("L1_gnn_Wq"), "l1_k": arr("L1_gnn_Wk"), "l1_v": arr("L1_gnn_Wv"), "l1_o": arr("L1_gnn_Wo"),
        "t_b": arr("L0_gnn_t_fc_b"), "fc_b": arr("L0_gnn_fc_b"), "bq": arr("L1_gnn_bq"), "bk": arr("L1_gnn_bk"),
        "bv": arr("L1_gnn_bv"), "bo": arr("L1_gnn_bo"), "gamma": arr("L1_gnn_gamma"), "beta": arr("L1_gnn_beta"),
        "cols": np.stack(columns, 1),
        "small_w1": small_w1, "small_w2": small_w2,
        "ident": np.eye(P, dtype=np.float32),
        "before": np.tril(np.ones((P, P), np.float32), -1),
        "spare_node": NP + spare,
        "lane": np.concatenate([k + 0 * p, k % 2 - spare - 2 * EP, k - spare - K * EP, spare], 1),
    }
    nc = bacc.Bacc("TRN2", target_bir_lowering=False, num_devices=1)
    arrays, args = {}, {"n_nodes": n_nodes}
    for name, value in data.items():
        value = np.ascontiguousarray(value)
        arrays[f"in_{name}"] = value
        args[name] = nc.dram_tensor(f"in_{name}", value.shape, mybir.dt.from_np(value.dtype),
                                    kind="ExternalInput").ap()
    out = nc.dram_tensor("out_0", (NP + SPARE, D), F32, kind="ExternalOutput").ap()
    graph_kernel(nc, args, out)
    r = run_bass_kernel_spmd(nc, [arrays], core_ids=[0])
    return r.results[0]["out_0"][:n_nodes]
```
